# Optimizing a Trainium2 kernel written in Bass

```python
import numpy as np
import jax
import jax.numpy as jnp

def _softmax(x, axis=-1):
    return jax.nn.softmax(x, axis=axis)

def _gelu(x):
    return jax.nn.gelu(x, approximate=True)

def _silu(x):
    return jax.nn.silu(x)

def _sigmoid(x):
    return jax.nn.sigmoid(x)

def _layernorm(x, axis=-1, eps=1e-05):
    m = jnp.mean(x, axis=axis, keepdims=True)
    v = jnp.var(x, axis=axis, keepdims=True)
    return (x - m) / jnp.sqrt(v + eps)

def _scatter_add(tgt, idx, src, axis=0):
    return tgt.at[idx].add(src)

def _segment_sum(src, seg, n):
    return jax.ops.segment_sum(src, seg, n)
kernel_name = 'mk_gnn_resnorm_d4_gnn_r16_3f6014'

def setup_inputs(seed: int=0):
    np.random.seed(seed)
    _w = jnp.asarray

    def _rec_inputs():
        import jax
        import jax.numpy as jnp
        _gk = jax.random.key(seed)
        x = -0.0001126 + 1 * jax.random.normal(jax.random.fold_in(_gk, 1), (1875, 256), jnp.float32)
        src = jax.random.randint(jax.random.fold_in(_gk, 2), (60000,), 0, 1875, jnp.int32)
        dst = jnp.minimum((1875 * jax.random.uniform(jax.random.fold_in(_gk, 3), (60000,)) ** 2.0).astype(jnp.int32), 29999)
        _o = jnp.argsort(dst, stable=True)
        src = src[_o]
        dst = dst[_o]
        edge_type_2 = jax.random.randint(jax.random.fold_in(_gk, 13), (60000,), 0, 2, jnp.int32)
        edge_type_8 = jax.random.randint(jax.random.fold_in(_gk, 14), (60000,), 0, 8, jnp.int32)
        return (x, src, dst, edge_type_2, edge_type_8)
    x, src, dst, edge_type_2, edge_type_8 = _rec_inputs()

    def _L0_gnn_setup():
        import jax, jax.numpy as jnp
        import numpy as np
        N_NODES = 1875
        N_EDGES = 30000
        IN_FEAT = 256
        OUT_FEAT = 256
        N_RELS = 8
        N_HEADS = 4
        HEAD_DIM = OUT_FEAT // N_HEADS
        LEAKY_SLOPE = 0.2
        key = jax.random.key(seed)
        ks = jax.random.split(key, 8)
        inputs = jax.random.normal(ks[0], (N_NODES, IN_FEAT), dtype=jnp.float32)
        conv_weights = jax.random.normal(ks[1], (N_RELS, N_HEADS, IN_FEAT, HEAD_DIM), dtype=jnp.float32) * (1.0 / np.sqrt(IN_FEAT))
        attn_l = jax.random.normal(ks[2], (N_RELS, N_HEADS, HEAD_DIM), dtype=jnp.float32) * 0.1
        attn_r = jax.random.normal(ks[3], (N_RELS, N_HEADS, HEAD_DIM), dtype=jnp.float32) * 0.1
        h_bias = jax.random.normal(ks[4], (OUT_FEAT,), dtype=jnp.float32) * 0.02
        edge_src = jax.random.randint(ks[5], (N_EDGES,), 0, N_NODES, dtype=jnp.int32)
        edge_dst = jax.random.randint(ks[6], (N_EDGES,), 0, N_NODES, dtype=jnp.int32)
        edge_type = jax.random.randint(ks[7], (N_EDGES,), 0, N_RELS, dtype=jnp.int32)
        return {'inputs': inputs, 'conv_weights': conv_weights, 'attn_l': attn_l, 'attn_r': attn_r, 'h_bias': h_bias, 'edge_src': edge_src, 'edge_dst': edge_dst, 'edge_type': edge_type}
    _L0_gnn_all = _L0_gnn_setup()
    _L0_gnn_in = {k: v for k, v in _L0_gnn_all.items() if k in ('conv_weights', 'attn_l', 'attn_r', 'h_bias')}
    del _L0_gnn_all

    def _L1_gnn_setup():
        import jax, jax.numpy as jnp
        import numpy as np
        N_NODES = 625
        N_EDGES = 20000
        D = 256
        D_OUT = 256
        NUM_REL = 2
        key = jax.random.key(seed)
        ks = jax.random.split(key, 16)
        s = 1.0 / np.sqrt(D)
        inp = {}
        inp['feat'] = jax.random.normal(ks[0], (N_NODES, D), dtype=jnp.float32)
        inp['src'] = jax.random.randint(ks[1], (N_EDGES,), 0, N_NODES, dtype=jnp.int32)
        inp['dst'] = jax.random.randint(ks[2], (N_EDGES,), 0, N_NODES, dtype=jnp.int32)
        inp['rel'] = jax.random.randint(ks[3], (N_EDGES,), 0, NUM_REL, dtype=jnp.int32)
        inp['W_rel'] = jax.random.normal(ks[4], (NUM_REL, D, D), dtype=jnp.float32) * s
        inp['b_rel'] = jax.random.normal(ks[5], (NUM_REL, D), dtype=jnp.float32) * s
        inp['W_ih'] = jax.random.normal(ks[6], (4 * D, D), dtype=jnp.float32) * s
        inp['b_ih'] = jax.random.normal(ks[7], (4 * D,), dtype=jnp.float32) * s
        inp['b_hh'] = jax.random.normal(ks[8], (4 * D,), dtype=jnp.float32) * s
        h = D // 2
        inp['W1'] = jax.random.normal(ks[9], (h, D), dtype=jnp.float32) * s
        inp['b1'] = jax.random.normal(ks[10], (h,), dtype=jnp.float32) * s
        inp['W2'] = jax.random.normal(ks[11], (h, h), dtype=jnp.float32) * (1.0 / np.sqrt(h))
        inp['b2'] = jax.random.normal(ks[12], (h,), dtype=jnp.float32) * (1.0 / np.sqrt(h))
        inp['W3'] = jax.random.normal(ks[13], (D_OUT, h), dtype=jnp.float32) * (1.0 / np.sqrt(h))
        inp['b3'] = jax.random.normal(ks[14], (D_OUT,), dtype=jnp.float32) * (1.0 / np.sqrt(h))
        return inp
    _L1_gnn_all = _L1_gnn_setup()
    _L1_gnn_in = {k: v for k, v in _L1_gnn_all.items() if k in ('W_rel', 'b_rel', 'W_ih', 'b_ih', 'b_hh', 'W1', 'b1', 'W2', 'b2', 'W3', 'b3')}
    del _L1_gnn_all

    def _L2_gnn_setup():
        import jax, jax.numpy as jnp
        import numpy as np
        N_NODES = 3125
        N_EDGES = 50000
        D_IN = 256
        D_HID = 256
        D_OUT = 256
        EPS = 1e-12

        def _sage_conv(x, src, dst, W_proj, b_proj, W_l, b_l, W_r):
            n = x.shape[0]
            xp = jax.nn.relu(x @ W_proj + b_proj)
            msg_sum = jax.ops.segment_sum(xp[src], dst, num_segments=n)
            cnt = jax.ops.segment_sum(jnp.ones_like(dst, dtype=x.dtype), dst, num_segments=n)
            aggr = msg_sum / jnp.maximum(cnt, 1.0)[:, None]
            out = aggr @ W_l + b_l + x @ W_r
            norm = jnp.linalg.norm(out, axis=-1, keepdims=True)
            return out / jnp.maximum(norm, EPS)
        key = jax.random.key(seed)
        ks = jax.random.split(key, 12)
        s = 1.0 / np.sqrt(D_IN)
        sh = 1.0 / np.sqrt(D_HID)
        inp = {'node_emb': jax.random.normal(ks[0], (N_NODES, D_IN), dtype=jnp.float32), 'edge_index': jax.random.randint(ks[1], (2, N_EDGES), 0, N_NODES, dtype=jnp.int64), 'W_proj1': jax.random.uniform(ks[2], (D_IN, D_IN), jnp.float32, -s, s), 'b_proj1': jax.random.uniform(ks[3], (D_IN,), jnp.float32, -s, s), 'W_l1': jax.random.uniform(ks[4], (D_IN, D_HID), jnp.float32, -s, s), 'b_l1': jax.random.uniform(ks[5], (D_HID,), jnp.float32, -s, s), 'W_r1': jax.random.uniform(ks[6], (D_IN, D_HID), jnp.float32, -s, s), 'W_proj2': jax.random.uniform(ks[7], (D_HID, D_HID), jnp.float32, -sh, sh), 'b_proj2': jax.random.uniform(ks[8], (D_HID,), jnp.float32, -sh, sh), 'W_l2': jax.random.uniform(ks[9], (D_HID, D_OUT), jnp.float32, -sh, sh), 'b_l2': jax.random.uniform(ks[10], (D_OUT,), jnp.float32, -sh, sh), 'W_r2': jax.random.uniform(ks[11], (D_HID, D_OUT), jnp.float32, -sh, sh)}
        return inp
    _L2_gnn_all = _L2_gnn_setup()
    _L2_gnn_in = {k: v for k, v in _L2_gnn_all.items() if k in ('W_proj1', 'b_proj1', 'W_l1', 'b_l1', 'W_r1', 'W_proj2', 'b_proj2', 'W_l2', 'b_l2', 'W_r2')}
    del _L2_gnn_all

    def _L3_gnn_setup():
        import jax, jax.numpy as jnp
        import numpy as np
        N, IN_CH, HEADS, OUT_CH, E = (3125, 256, 4, 64, 50000)
        key = jax.random.key(seed)
        k1, k2, k3, k4, k5 = jax.random.split(key, 5)
        x = jax.random.normal(k1, (N, IN_CH), dtype=jnp.float32)
        edge_index = jax.random.randint(k2, (2, E), 0, N, dtype=jnp.int64)
        bw = float(np.sqrt(6.0 / (IN_CH + HEADS * OUT_CH)))
        ba = float(np.sqrt(6.0 / (HEADS + OUT_CH)))
        weight = jax.random.uniform(k3, (IN_CH, HEADS * OUT_CH), jnp.float32, -bw, bw)
        attn_l = jax.random.uniform(k4, (HEADS, OUT_CH), jnp.float32, -ba, ba)
        attn_r = jax.random.uniform(k5, (HEADS, OUT_CH), jnp.float32, -ba, ba)
        return {'x': x, 'edge_index': edge_index, 'weight': weight, 'attn_l': attn_l, 'attn_r': attn_r}
    _L3_gnn_all = _L3_gnn_setup()
    _L3_gnn_in = {k: v for k, v in _L3_gnn_all.items() if k in ('weight', 'attn_l', 'attn_r')}
    del _L3_gnn_all
    return {'x': x, 'src': src, 'dst': dst, 'edge_type_2': edge_type_2, 'edge_type_8': edge_type_8, 'L0_gnn_conv_weights': _L0_gnn_in['conv_weights'], 'L0_gnn_attn_l': _L0_gnn_in['attn_l'], 'L0_gnn_attn_r': _L0_gnn_in['attn_r'], 'L0_gnn_h_bias': _L0_gnn_in['h_bias'], 'L1_gnn_W_rel': _L1_gnn_in['W_rel'], 'L1_gnn_b_rel': _L1_gnn_in['b_rel'], 'L1_gnn_W_ih': _L1_gnn_in['W_ih'], 'L1_gnn_b_ih': _L1_gnn_in['b_ih'], 'L1_gnn_b_hh': _L1_gnn_in['b_hh'], 'L1_gnn_W1': _L1_gnn_in['W1'], 'L1_gnn_b1': _L1_gnn_in['b1'], 'L1_gnn_W2': _L1_gnn_in['W2'], 'L1_gnn_b2': _L1_gnn_in['b2'], 'L1_gnn_W3': _L1_gnn_in['W3'], 'L1_gnn_b3': _L1_gnn_in['b3'], 'L2_gnn_W_proj1': _L2_gnn_in['W_proj1'], 'L2_gnn_b_proj1': _L2_gnn_in['b_proj1'], 'L2_gnn_W_l1': _L2_gnn_in['W_l1'], 'L2_gnn_b_l1': _L2_gnn_in['b_l1'], 'L2_gnn_W_r1': _L2_gnn_in['W_r1'], 'L2_gnn_W_proj2': _L2_gnn_in['W_proj2'], 'L2_gnn_b_proj2': _L2_gnn_in['b_proj2'], 'L2_gnn_W_l2': _L2_gnn_in['W_l2'], 'L2_gnn_b_l2': _L2_gnn_in['b_l2'], 'L2_gnn_W_r2': _L2_gnn_in['W_r2'], 'L3_gnn_weight': _L3_gnn_in['weight'], 'L3_gnn_attn_l': _L3_gnn_in['attn_l'], 'L3_gnn_attn_r': _L3_gnn_in['attn_r']}

def reference(x, src, dst, edge_type_2, edge_type_8, L0_gnn_conv_weights, L0_gnn_attn_l, L0_gnn_attn_r, L0_gnn_h_bias, L1_gnn_W_rel, L1_gnn_b_rel, L1_gnn_W_ih, L1_gnn_b_ih, L1_gnn_b_hh, L1_gnn_W1, L1_gnn_b1, L1_gnn_W2, L1_gnn_b2, L1_gnn_W3, L1_gnn_b3, L2_gnn_W_proj1, L2_gnn_b_proj1, L2_gnn_W_l1, L2_gnn_b_l1, L2_gnn_W_r1, L2_gnn_W_proj2, L2_gnn_b_proj2, L2_gnn_W_l2, L2_gnn_b_l2, L2_gnn_W_r2, L3_gnn_weight, L3_gnn_attn_l, L3_gnn_attn_r):
    import jax
    import jax.numpy as jnp

    def _L0_gnn_ref(inputs, conv_weights, attn_l, attn_r, h_bias, edge_src, edge_dst, edge_type):
        import jax, jax.numpy as jnp
        import numpy as np
        N_NODES = 1875
        N_EDGES = 30000
        IN_FEAT = 256
        OUT_FEAT = 256
        N_RELS = 8
        N_HEADS = 4
        HEAD_DIM = OUT_FEAT // N_HEADS
        LEAKY_SLOPE = 0.2
        feat_all = jnp.einsum('ni,rhid->rnhd', inputs, conv_weights)
        feat_src_e = feat_all[edge_type, edge_src]
        feat_dst_e = feat_all[edge_type, edge_dst]
        el = jnp.sum(feat_src_e * attn_l[edge_type], axis=-1)
        er = jnp.sum(feat_dst_e * attn_r[edge_type], axis=-1)
        e = jax.nn.leaky_relu(el + er, negative_slope=LEAKY_SLOPE)
        m = jax.ops.segment_max(e, edge_dst, num_segments=N_NODES)
        ex = jnp.exp(e - m[edge_dst])
        denom = jax.ops.segment_sum(ex, edge_dst, num_segments=N_NODES)
        alpha = ex / denom[edge_dst]
        h = jax.ops.segment_sum(alpha[..., None] * feat_src_e, edge_dst, num_segments=N_NODES)
        h = h.reshape(N_NODES, OUT_FEAT) + h_bias
        return h

    def _L1_gnn_ref(feat, src, dst, rel, W_rel, b_rel, W_ih, b_ih, b_hh, W1, b1, W2, b2, W3, b3):
        import jax, jax.numpy as jnp
        import numpy as np
        N_NODES = 625
        N_EDGES = 20000
        D = 256
        D_OUT = 256
        NUM_REL = 2
        n_nodes = feat.shape[0]
        S = feat[src]

        def edge_nn(x, W, b):
            h = jax.nn.relu(x @ W.T + b)
            return jax.nn.relu(h @ W.T + b)
        msgs = jnp.zeros_like(S)
        for r in range(W_rel.shape[0]):
            msgs = jnp.where((rel == r)[:, None], edge_nn(S, W_rel[r], b_rel[r]), msgs)
        agg = jax.ops.segment_sum(msgs, dst, num_segments=n_nodes)
        gates = agg @ W_ih.T + b_ih + b_hh
        i, f, g, o = jnp.split(gates, 4, axis=-1)
        c = jax.nn.sigmoid(i) * jnp.tanh(g)
        hn = jax.nn.sigmoid(o) * jnp.tanh(c)
        x = jax.nn.relu(hn @ W1.T + b1)
        x = jax.nn.relu(x @ W2.T + b2)
        return x @ W3.T + b3

    def _L2_gnn_ref(node_emb, edge_index, W_proj1, b_proj1, W_l1, b_l1, W_r1, W_proj2, b_proj2, W_l2, b_l2, W_r2):
        import jax, jax.numpy as jnp
        import numpy as np
        N_NODES = 3125
        N_EDGES = 50000
        D_IN = 256
        D_HID = 256
        D_OUT = 256
        EPS = 1e-12

        def _sage_conv(x, src, dst, W_proj, b_proj, W_l, b_l, W_r):
            n = x.shape[0]
            xp = jax.nn.relu(x @ W_proj + b_proj)
            msg_sum = jax.ops.segment_sum(xp[src], dst, num_segments=n)
            cnt = jax.ops.segment_sum(jnp.ones_like(dst, dtype=x.dtype), dst, num_segments=n)
            aggr = msg_sum / jnp.maximum(cnt, 1.0)[:, None]
            out = aggr @ W_l + b_l + x @ W_r
            norm = jnp.linalg.norm(out, axis=-1, keepdims=True)
            return out / jnp.maximum(norm, EPS)
        src, dst = (edge_index[0], edge_index[1])
        h = _sage_conv(node_emb, src, dst, W_proj1, b_proj1, W_l1, b_l1, W_r1)
        h = jax.nn.relu(h)
        out = _sage_conv(h, src, dst, W_proj2, b_proj2, W_l2, b_l2, W_r2)
        return out

    def _L3_gnn_ref(x, edge_index, weight, attn_l, attn_r):
        import jax, jax.numpy as jnp
        import numpy as np
        N, IN_CH, HEADS, OUT_CH, E = (3125, 256, 4, 64, 50000)
        heads, out_ch = attn_l.shape
        n = x.shape[0]
        xt = jnp.matmul(x, weight).reshape(-1, heads, out_ch)
        row, col = (edge_index[0], edge_index[1])
        alpha_l = jnp.einsum('ehd,hd->eh', xt[row], attn_l)
        alpha_r = jnp.einsum('ehd,hd->eh', xt[col], attn_r)
        alpha = jax.nn.softmax(jax.nn.leaky_relu(alpha_l + alpha_r, 0.01), axis=1)
        tmp = jnp.einsum('nh,nhd->nd', alpha[:n], xt[col[:n]])
        out = jnp.broadcast_to(tmp[:, None, :], (n, heads, out_ch))
        return out.reshape(n, heads * out_ch)
    edge_index = jnp.stack([src, dst])
    x = _layernorm(x + _L0_gnn_ref(x, L0_gnn_conv_weights, L0_gnn_attn_l, L0_gnn_attn_r, L0_gnn_h_bias, src, dst, edge_type_8), axis=-1)
    x = _layernorm(x + _L1_gnn_ref(x, src, dst, edge_type_2, L1_gnn_W_rel, L1_gnn_b_rel, L1_gnn_W_ih, L1_gnn_b_ih, L1_gnn_b_hh, L1_gnn_W1, L1_gnn_b1, L1_gnn_W2, L1_gnn_b2, L1_gnn_W3, L1_gnn_b3), axis=-1)
    x = _layernorm(x + _L2_gnn_ref(x, edge_index, L2_gnn_W_proj1, L2_gnn_b_proj1, L2_gnn_W_l1, L2_gnn_b_l1, L2_gnn_W_r1, L2_gnn_W_proj2, L2_gnn_b_proj2, L2_gnn_W_l2, L2_gnn_b_l2, L2_gnn_W_r2), axis=-1)
    x = _layernorm(x + _L3_gnn_ref(x, edge_index, L3_gnn_weight, L3_gnn_attn_l, L3_gnn_attn_r), axis=-1)
    return x

_drawn_inputs = setup_inputs


def setup_inputs(seed=0):
    import zlib

    import numpy as np

    out = dict(_drawn_inputs(seed))
    spreads = {}
    factors = {'L1_gnn_b_ih': 8.0,
     'L1_gnn_b_hh': 8.0,
     'L2_gnn_W_proj1': 145.606,
     'L2_gnn_b_proj1': 200.0,
     'L2_gnn_W_l1': 6.525,
     'L2_gnn_b_l1': 200.0,
     'L2_gnn_W_proj2': 6.423,
     'L2_gnn_b_proj2': 3.484,
     'L2_gnn_W_r1': 64.0,
     'L2_gnn_W_r2': 2.677,
     'L2_gnn_b_l2': 2.806}
    for name, (base, spread) in spreads.items():
        noise = np.random.default_rng([zlib.crc32(name.encode()), seed]).standard_normal(out[name].shape)
        drawn = base * np.exp(spread * noise) if base else spread * noise
        out[name] = jnp.asarray(drawn.astype(out[name].dtype))
    for name, factor in factors.items():
        out[name] = (out[name] * factor).astype(out[name].dtype)
    return out
```

```python
import concourse.bass as bass
from concourse import mybir
from contextlib import ExitStack

F32 = mybir.dt.float32
F16 = mybir.dt.float16
I32 = mybir.dt.int32
U16 = mybir.dt.uint16
ALU = mybir.AluOpType
ACT = mybir.ActivationFunctionType
AX = mybir.AxisListType

N = 1875
E = 60000
D = 256
P = 128
NT = -(-N // P)
NP = NT * P
NLAST = N - (NT - 1) * P
H = 4
HD = D // H
R8 = 8
R2 = 2
GR = 4
EP = GR * P * P
TILES = -(-E // P)
WIN = 16
WINS = -(-N // WIN)
NW = WINS * WIN
STEPS = E // P + WINS
SH = NT
KW = WIN * SH
PAD_DST = 2047
BIG = 1e30
EPS = 1e-5
Q = 4 * P

GB = 7
NGB = TILES // GB
assert NGB * GB == TILES and NGB % 2 == 1
N_IT = (NGB - 3) // 2
LINKS = 4 + 4 * N_IT + 4
FR = 8
HEAD = 2
GRPS = (STEPS - HEAD) // FR
assert HEAD + GRPS * FR == STEPS and GRPS % 2 == 1
CW = NW // 4
CN = 3 * P
NC = NP // CN

A_SLO, A_KEY, A_DJ, A_IDX, A_WS, A_WI, A_IOT = (STEPS * i for i in range(7))
A_SEL = 7 * STEPS
A_F = A_SEL + GR * STEPS
A_SUM = A_F + 4 * Q
A_DG = A_SUM + H * STEPS
A_OH = A_DG + Q
A_EV = A_OH + 2 * (P // 2 + KW)
A_BIG = A_EV + 2 * KW
A_W0 = A_BIG
A_XT0 = A_W0 + 2 * R8 * D
A_FS = A_XT0 + 2 * NP
A_IE = A_FS + 4 * 512
A_ID = A_IE + Q
A_S = A_BIG
A_FA = A_S + H * Q
A_BA = A_FA + H * Q
A_FL = A_BA + H * Q
A_ROW = A_FL + 4 * Q
A_FB = A_BIG
A_WOH = A_FB + FR * D
A_ACC = A_WOH + 4 * 64
A_X = 0
A_XT = A_X + 2 * NP
A_B1 = A_XT + 2 * NP
A_B2 = A_B1 + NT * (D + 2 * H)
A_CH = A_B2 + 2 * NP
A_WT = A_CH + 2 * NW
A_BI = A_WT + 3200
A_END = A_BI + 4 * D
assert A_ACC + WINS * 64 <= A_BI and A_ROW + 5 * Q <= A_END and A_ID + Q <= A_END


def build(nc, rec, x, xT, edge0, w0, a0l, a0r, cols, wrel, brow, wih, w1, w2, w3, b3, wp1, bp1, wl1, bl1, wr1, wp2, bp2, wl2, bl2, wr2,
          wt3, a3l, a3r, out):
    ctx = ExitStack()
    with ctx:
        sb = lambda n, s, d: ctx.enter_context(nc.sbuf_tensor(n, s, d))
        sem = lambda n: ctx.enter_context(nc.semaphore(n))

        feat_t = nc.dram_tensor("feat_table", (NP * R8, D), F32).ap()
        el_t = nc.dram_tensor("el_table", (NP * R8, H), F32).ap()
        er_t = nc.dram_tensor("er_table", (NP * R8, H), F32).ap()
        xt_t = nc.dram_tensor("xt_table", (NP, D + 2 * H), F32).ap()
        al_t = nc.dram_tensor("al_table", (NP, H), F32).ap()

        AR = sb("arena", [P, A_END], F32)
        ADJ = sb("adjacency", [P, R2, NW * SH], U16)
        ident = sb("ident", [P, P], F32)
        ones = sb("ones", [P, P], F32)
        ones16 = sb("ones16", [P, P], F16)
        iota128 = sb("iota128", [P, P], F16)
        iota480 = sb("iota480", [P, R2 * KW], F16)
        iota16 = sb("iota16", [P, WIN], F32)
        pcol = sb("pcol", [P, GR], F32)
        w16col = sb("w16col", [P, 1], F32)
        cnt = sb("cnt", [P, 2], F32)
        GI = sb("gather_idx", [P, 2, 2 * GB], I32)
        GO = sb("gather_out", [P, 2, 2 * GB * H], F32)
        FI = sb("feat_idx", [P, 2, FR], I32)
        FI0 = sb("feat_idx0", [P, HEAD], I32)
        BC = sb("bias_cols", [P, 32], F32)
        ST = sb("ln_stats", [P, NT, 6], F32)
        MV = sb("ln_mean_var", [P, NT, 2], F32)
        RS = sb("ln_rstd", [P, NT], F32)
        RC = sb("recip_count", [P, NT], F32)
        E3 = sb("edge_ends", [P, 2, NT], I32)
        S3 = sb("scores3", [P, 3, NT * H], F32)
        SC16 = sb("edge_cols", [P, 2, H * GR], F32)
        poolpad = sb("pool_pad", [P, 1], F32)
        RD = sb("lane_ends", [P, 2, GR * H], F32)
        PS = [ctx.enter_context(nc.psum_tensor(f"bank{i}", [P, 512], F32)) for i in range(8)]

        def ar(off, *dims, dt=None):
            n = 1
            for d in dims:
                n *= d
            v = AR[:, off:off + n]
            if len(dims) == 2:
                v = v.rearrange("p (a b) -> p a b", b=dims[1])
            elif len(dims) == 3:
                v = v.rearrange("p (a b c) -> p a b c", b=dims[1], c=dims[2])
            return v

        EARLY = ADJ[:, :, :].rearrange("p r k -> p (r k)").bitcast(F32)
        RL = EARLY[:, 0:4 * Q].bitcast(I32)
        RLv = RL.rearrange("p (n f) -> p n f", f=4)
        LI = EARLY[:, 4 * Q:5 * Q].bitcast(I32)
        LJ = EARLY[:, 5 * Q:6 * Q].bitcast(I32)
        IDd = EARLY[:, 6 * Q:7 * Q]
        IDm = EARLY[:, 7 * Q:8 * Q]
        AT = EARLY[:, 8 * Q:8 * Q + 4 * Q * 2].rearrange("p (a n) -> p a n", a=2)
        TMP = EARLY[:, 16 * Q:20 * Q]
        VL = EARLY[:, 20 * Q:20 * Q + 128].rearrange("p (k n) -> p k n", k=2)
        ELS = EARLY[:, 21 * Q:21 * Q + NT * 64].rearrange("p (t n) -> p t n", n=64)

        SLO, KEY, DJ, IDX, WS, IOT = (ar(o, STEPS) for o in (A_SLO, A_KEY, A_DJ, A_IDX, A_WS, A_IOT))
        WI = ar(A_WI, STEPS).bitcast(I32)
        SEL = ar(A_SEL, GR, STEPS)
        Fl = ar(A_F, 4, Q)
        DST = Fl[:, 2, :].rearrange("p (g e) -> p g e", g=GR)
        SUM = ar(A_SUM, Q, H)
        ALS = ar(A_SUM, STEPS, H)
        DG = ar(A_DG, Q)
        OHS = [AR[:, A_OH + k * (P // 2 + KW):A_OH + k * (P // 2 + KW) + P // 2].bitcast(F16) for k in range(2)]
        OHK = [AR[:, A_OH + k * (P // 2 + KW) + P // 2:A_OH + (k + 1) * (P // 2 + KW)].bitcast(F16) for k in range(2)]
        EV = [AR[:, A_EV + k * KW:A_EV + (k + 1) * KW].bitcast(U16).rearrange("p (r k) -> p r k", r=R2) for k in range(2)]
        W0 = ar(A_W0, 2, R8 * D)
        XT0 = ar(A_XT0, 2, NP)
        FS = ar(A_FS, 4, 512)
        IE, ID = ar(A_IE, Q), ar(A_ID, Q)
        S, FA, BA = ar(A_S, H, Q), ar(A_FA, H, Q), ar(A_BA, H, Q)
        FL = ar(A_FL, 4, Q)
        ROW = ar(A_ROW, 5, Q)
        FB = ar(A_FB, FR, D)
        WOH = ar(A_WOH, 4, 64)
        ACC = ar(A_ACC, WINS, 64)
        ACCf = ar(A_ACC, WINS * 64)
        ALSf = ar(A_SUM, STEPS * H)
        X, XT = ar(A_X, NT, D), ar(A_XT, 2, NP)
        B1, B2 = ar(A_B1, NT, D), ar(A_B2, NT, D)
        M1, M2 = B1, B2
        XT3 = ar(A_B1, NT, D + 2 * H)
        G3 = ar(A_B2, NT, D + 2 * H)
        AG3 = ar(A_B2 + NT * (D + 2 * H), NT, H)
        T64 = ar(A_XT, NT, HD)
        B2T = ar(A_B2, 2, NP)
        CH = ar(A_CH, 2, NW)
        HC = [ar(A_CH + k * 2 * CN, 2, CN) for k in range(2)]
        WREL = ar(A_WT, 2 * R2, D).rearrange("p (k r) n -> p k r n", k=2)
        WIH = ar(A_WT + 1024, 2, 3 * D)
        W1s, W2s, W3s = ar(A_WT + 2560, 2, P), ar(A_WT + 2816, P), ar(A_WT + 2944, D)
        W2L = [ar(A_WT + 512 * i, 2, D) for i in range(6)]
        WT3 = ar(A_WT, 2, D + 2 * H)
        A3 = ar(A_WT + 528, 2, D)
        TMP3 = ar(A_WT + 1040, D)
        BROW = ar(A_BI, 4, D)
        GT = ar(A_B1, 6, CN)
        CC, HN, X1, X2 = ar(A_B1 + 6 * CN, 2, CN), ar(A_B1 + 8 * CN, 2, CN), ar(A_B1 + 10 * CN, CN), ar(A_B1 + 11 * CN, CN)

        names = """ld_rec ld_w0 ld_xt ld_at ld_e3 consts fields idx_mm idx_ev vl_done tab_mm tab_ev tab_st
            feat_mm feat_ev diag_done bc_mm cmp_done ws_mm sel_ready fld_mm fld_ev steps_done
            a_oh a_mm a_ev a_add pool_link sum_done lane_in lane_mm lane_ev flags_in flags_mm
            tail_ready tail_mm cin_ready cin_mm exp_ready exp_done alpha_ready als_mm als_ev 
            l_idx l_woh l_mm l_acc ld_x ld_bc ld_wt1 ht_ready ht_mm ht_add var_ready std_ready ln_done xt_mm
            xt_eva xt_evd h_mm h_ev m_mm m_ev chunk_ready chunk_used agg_eva agg_evd gate_mm gate_ev
            c_ready tc_ready hn_ready x1_mm x1_ev x2_mm x2_ev x3_mm x3_add ld_wt2 ld_wt3 p_mm p_ev
            cnt_acc cnt_mm cnt_ev o_mm o_ev o_ready sq_done nrm_done h_ready pool_gate vl3_done t_mm t_ev t_st
            g3 s3_ready s3_exp out_st dve_link""".split()
        s = {n: sem(n) for n in names}
        fs_st = [sem(f"feat_stored{i}") for i in range(4)]
        g_done = [sem(f"scores_gathered{i}") for i in range(2)]
        f_done = [sem(f"feat_gathered{i}") for i in range(FR)]

        block = ctx.enter_context(nc.Block())

        @block.sync
        def _(sp):
            sp.dma_start(RL.rearrange("p (g n) -> p g n", g=GR),
                         rec.rearrange("(g t e) f -> t g (e f)", g=GR, t=P)).then_inc(s["ld_rec"], 16)
            sp.dma_start(W0, w0.rearrange("(k p) n -> p k n", k=2)).then_inc(s["ld_w0"], 16)
            sp.dma_start(AT[:, 0, :], a0l.broadcast_to([P, R8 * D])).then_inc(s["ld_at"], 16)
            sp.dma_start(AT[:, 1, :], a0r.broadcast_to([P, R8 * D])).then_inc(s["ld_at"], 16)
            sp.dma_start(XT0, xT.rearrange("(k p) n -> p k n", k=2)).then_inc(s["ld_xt"], 16)
            sp.dma_start(E3[:, :, :], edge0).then_inc(s["ld_e3"], 16)
            sp.dma_start(BC[:, 0:20], cols).then_inc(s["ld_bc"], 16)
            sp.wait_ge(s["tab_ev"], 2)
            sp.dma_start(el_t.rearrange("(t p r) h -> p t (r h)", p=P, r=R8), ELS[:, :, 0:32]).then_inc(s["tab_st"], 16)
            sp.dma_start(er_t.rearrange("(t p r) h -> p t (r h)", p=P, r=R8), ELS[:, :, 32:64]).then_inc(s["tab_st"], 16)
            ft = feat_t.rearrange("(t p c r) d -> t p c (r d)", p=P, c=4, r=2)
            for i in range(NT * 4):
                sp.wait_ge(s["feat_ev"], i + 1)
                sp.dma_start(ft[i // 4, :, i % 4, :], FS[:, i % 4, :]).then_inc(fs_st[i % 4], 16)
            sp.wait_ge(s["l_acc"], STEPS + 1)
            sp.wait_ge(s["ht_ready"], 1)
            sp.dma_start(X[:, 0:NT - 1, :], x[0:(NT - 1) * P, :].rearrange("(t p) d -> p t d", p=P)).then_inc(s["ld_x"], 16)
            sp.dma_start(X[0:NLAST, NT - 1, :], x[(NT - 1) * P:N, :]).then_inc(s["ld_x"], 16)
            for r in range(R2):
                sp.dma_start(WREL[:, :, r, :], wrel[r, :, :].rearrange("(k p) n -> p k n", k=2)).then_inc(s["ld_wt1"], 16)
            sp.dma_start(WIH, wih.rearrange("(k p) n -> p k n", k=2)).then_inc(s["ld_wt1"], 16)
            sp.dma_start(W1s, w1.rearrange("(k p) n -> p k n", k=2)).then_inc(s["ld_wt1"], 16)
            sp.dma_start(W2s, w2).then_inc(s["ld_wt1"], 16)
            sp.dma_start(W3s, w3).then_inc(s["ld_wt1"], 16)
            for i, b in enumerate((brow[0:1, :], brow[1:2, :], b3)):
                sp.dma_start(BROW[0:1, i, :], b).then_inc(s["ld_wt1"], 16)
            sp.wait_ge(s["x3_mm"], NC)
            for i, w in enumerate((wp1, wl1, wr1, wp2, wl2, wr2)):
                sp.dma_start(W2L[i], w.rearrange("(k p) n -> p k n", k=2)).then_inc(s["ld_wt2"], 16)
            for i, b in enumerate((bp1, bl1, bp2, bl2)):
                sp.dma_start(BROW[0:1, i, :], b).then_inc(s["ld_wt2"], 16)
            sp.wait_ge(s["o_mm"], 2 * NT)
            sp.dma_start(WT3[:, :, 0:D], wt3.rearrange("(k p) n -> p k n", k=2)).then_inc(s["ld_wt3"], 16)
            sp.dma_start(A3[:, 0, :], a3l.broadcast_to([P, D])).then_inc(s["ld_wt3"], 16)
            sp.dma_start(A3[:, 1, :], a3r.broadcast_to([P, D])).then_inc(s["ld_wt3"], 16)
            sp.wait_ge(s["t_ev"], NT)
            sp.dma_start(xt_t.rearrange("(t p) n -> p t n", p=P), XT3).then_inc(s["t_st"], 16)
            sp.dma_start(al_t.rearrange("(t p) n -> p t n", p=P), XT3[:, :, D:D + H]).then_inc(s["t_st"], 16)
            sp.wait_ge(s["ln_done"], 4)
            sp.dma_start(out[0:(NT - 1) * P, :].rearrange("(t p) d -> p t d", p=P), X[:, 0:NT - 1, :]).then_inc(s["out_st"], 16)
            sp.dma_start(out[(NT - 1) * P:N, :], X[0:NLAST, NT - 1, :]).then_inc(s["out_st"], 16)
            sp.wait_ge(s["out_st"], 32)

        @block.gpsimd
        def _(pool):
            g = nc.gpsimd
            g.memset(ident[:, :], 0.0).then_inc(s["pool_link"], 1)
            g.memset(ones[:, :], 1.0)
            g.memset(ones16[:, :], 1.0)
            pool.wait_ge(s["pool_link"], 1)
            g.affine_select(out=ident[:, :], in_=ident[:, :], compare_op=ALU.not_equal, fill=1.0, base=0,
                            pattern=[[-1, P]], channel_multiplier=1)
            g.iota(iota128[:, :], pattern=[[1, P]], base=0, channel_multiplier=0, allow_small_or_imprecise_dtypes=True)
            g.iota(iota480[:, :], pattern=[[1, R2 * KW]], base=0, channel_multiplier=0, allow_small_or_imprecise_dtypes=True)
            g.iota(iota16[:, :], pattern=[[1, WIN]], base=0, channel_multiplier=0, allow_small_or_imprecise_dtypes=True)
            g.iota(IOT, pattern=[[1, STEPS]], base=0, channel_multiplier=0, allow_small_or_imprecise_dtypes=True)
            g.iota(pcol[:, :], pattern=[[P, GR]], base=0, channel_multiplier=1, allow_small_or_imprecise_dtypes=True)
            g.iota(w16col[:, :], pattern=[[0, 1]], base=0, channel_multiplier=WIN, allow_small_or_imprecise_dtypes=True)\
             .then_inc(s["consts"], 1)

            def issue(k, cols):
                g.tensor_copy(GI[:, k, 0:GB], IE[:, cols])
                g.tensor_copy(GI[:, k, GB:2 * GB], ID[:, cols]).then_inc(s["pool_link"], 1)

            def gathers(k):
                for j in range(2 * GB):
                    g.indirect_dma_start(out=GO[:, k, H * j:H * (j + 1)], out_offset=None,
                                         in_=(el_t if j < GB else er_t),
                                         in_offset=bass.IndirectOffsetOnAxis(ap=GI[:, k, j:j + 1], axis=0))\
                     .then_inc(g_done[k], 16)

            def collect(k, cols):
                g.tensor_tensor(SUM[:, cols, :].rearrange("p t h -> p (t h)"), GO[:, k, 0:GB * H],
                                GO[:, k, GB * H:2 * GB * H], ALU.add).then_inc(s["pool_link"], 1)

            BATCH = 2 * GB * 16
            g.memset(SUM[:, TILES:Q, :], 0.0).then_inc(s["pool_link"], 1)
            pool.wait_ge(s["idx_ev"], 2)
            pool.wait_ge(s["tab_st"], 32)
            for b in range(2):
                issue(b, slice(GB * b, GB * (b + 1)))
                pool.wait_ge(s["pool_link"], 3 + b)
                gathers(b)
            with pool.Fori(0, N_IT) as i:
                for k in range(2):
                    if k == 0:
                        pool.wait_ge(g_done[0], i * BATCH + BATCH)
                    else:
                        pool.wait_ge(g_done[1], i * BATCH + BATCH)
                    collect(k, bass.ds(i * (2 * GB) + GB * k, GB))
                    issue(k, bass.ds(i * (2 * GB) + GB * (k + 2), GB))
                    pool.wait_ge(s["pool_link"], i * 4 + (6 + 2 * k))
                    pool.sem_inc(s["pool_gate"], 1)
                    gathers(k)
            last = NGB - 1
            pool.wait_ge(g_done[0], (N_IT + 1) * BATCH)
            collect(0, slice(GB * (last - 2), GB * (last - 1)))
            issue(0, slice(GB * last, GB * NGB))
            pool.wait_ge(s["pool_link"], LINKS - 2)
            gathers(0)
            pool.wait_ge(g_done[1], (N_IT + 1) * BATCH)
            collect(1, slice(GB * (last - 1), GB * last))
            pool.wait_ge(g_done[0], (N_IT + 2) * BATCH)
            collect(0, slice(GB * last, GB * NGB))

            def feat(step_slot, idx_ap):
                g.indirect_dma_start(out=FB[:, step_slot, :], out_offset=None, in_=feat_t,
                                     in_offset=bass.IndirectOffsetOnAxis(ap=idx_ap, axis=0))\
                 .then_inc(f_done[step_slot], 16)

            for i in range(4):
                pool.wait_ge(fs_st[i], NT * 16)
            pool.wait_ge(s["l_acc"], 1)
            pool.wait_ge(s["l_idx"], 1)
            for st in range(HEAD):
                feat(st, FI0[:, st:st + 1])
            pool.wait_ge(s["l_idx"], 2)
            for u in range(FR):
                st = HEAD + u
                if st == FR:
                    pool.wait_ge(s["l_mm"], FR // 2)
                feat(st % FR, FI[:, 0, u:u + 1])
            with pool.Fori(0, (GRPS - 1) // 2) as i:
                for m in range(2):
                    pool.wait_ge(s["l_idx"], i * 2 + (3 + m))
                    pool.sem_inc(s["pool_gate"], 1)
                    for u in range(FR):
                        st = HEAD + FR * (1 + m) + u
                        if st % (FR // 2) == 0:
                            pool.wait_ge(s["l_mm"], i * (2 * FR) + (st - FR // 2))
                            pool.sem_inc(s["pool_gate"], 1)
                        feat(st % FR, FI[:, (m + 1) % 2, u:u + 1])

            CNTS = B2T[:, 0, 0:NW]
            for c in range(SH):
                pool.wait_ge(s["chunk_ready"], R2 * SH + c + 1)
                if c:
                    pool.wait_ge(s["cnt_acc"], c)
                if c == 0:
                    g.tensor_copy(CNTS, CH[:, 0, :]).then_inc(s["cnt_acc"], 1)
                else:
                    g.tensor_tensor(CNTS, CNTS, CH[:, c % 2, :], ALU.add).then_inc(s["cnt_acc"], 1)

            pool.wait_ge(s["ld_e3"], 16)
            pool.wait_ge(s["t_st"], 32)
            for t in range(NT):
                g.indirect_dma_start(out=AG3[:, t, :], out_offset=None, in_=al_t,
                                     in_offset=bass.IndirectOffsetOnAxis(ap=E3[:, 0, t:t + 1], axis=0)).then_inc(s["g3"], 16)
                g.indirect_dma_start(out=G3[:, t, :], out_offset=None, in_=xt_t,
                                     in_offset=bass.IndirectOffsetOnAxis(ap=E3[:, 1, t:t + 1], axis=0)).then_inc(s["g3"], 16)

        @block.scalar
        def _(act):
            a = nc.scalar
            for i in range(NT * 4):
                act.wait_ge(s["feat_mm"], i + 1)
                if i >= 4:
                    act.wait_ge(fs_st[i % 4], 16 * (i // 4))
                a.activation(FS[:, i % 4, :], PS[i % 4][:, :], ACT.Copy).then_inc(s["feat_ev"], 1)
            def a_evac(k):
                a.activation(EV[k].rearrange("p r k -> p (r k)"), PS[6 + k][:, 0:R2 * KW], ACT.Copy).then_inc(s["a_ev"], 1)
            for k in range(2):
                act.wait_ge(s["a_mm"], k + 1)
                a_evac(k)
            with act.Fori(0, STEPS // 2 - 1) as i:
                for k in range(2):
                    act.wait_ge(s["a_mm"], i * 2 + (3 + k))
                    act.wait_ge(s["a_add"], i * 2 + (2 + k))
                    a_evac(k)
            for h in range(H):
                act.wait_ge(s["lane_mm"], h + 1)
                a.activation(S[:, h, :], PS[h][:, :], ACT.Copy).then_inc(s["lane_ev"], 1)
            act.wait_ge(s["exp_ready"], 1)
            a.activation(S.rearrange("p h n -> p (h n)"), S.rearrange("p h n -> p (h n)"), ACT.Exp).then_inc(s["exp_done"], 1)
            for h in range(H):
                act.wait_ge(s["als_mm"], h + 1)
                a.activation(ALS[:, 0:512, h], PS[2 * h][:, 0:512], ACT.Copy)
                a.activation(ALS[:, 512:STEPS, h], PS[2 * h + 1][:, 0:STEPS - 512], ACT.Copy).then_inc(s["als_ev"], 1)
            a.activation(FI0[:, :], IDX[:, 0:HEAD], ACT.Copy).then_inc(s["l_idx"], 1)
            a.activation(FI[:, 0, :], IDX[:, HEAD:HEAD + FR], ACT.Copy).then_inc(s["l_idx"], 1)
            with act.Fori(0, (GRPS - 1) // 2) as i:
                for m in range(2):
                    act.wait_ge(s["l_mm"], i * (2 * FR) + (HEAD + FR * m))
                    a.activation(FI[:, (m + 1) % 2, :], IDX[:, bass.ds(i * (2 * FR) + (HEAD + FR * (m + 1)), FR)],
                                 ACT.Copy).then_inc(s["l_idx"], 1)

            def ln_sqrt(n):
                act.wait_ge(s["var_ready"], n)
                a.activation(RS[:, :], MV[:, :, 1], ACT.Sqrt).then_inc(s["std_ready"], 1)

            def xt_evac(n):
                for q in range(4):
                    act.wait_ge(s["xt_mm"], 8 * n + 2 * q + 1)
                    w = min(512, NP - 512 * q)
                    a.activation(XT[:, 0, 512 * q:512 * q + w], PS[2 * q][:, 0:w], ACT.Copy).then_inc(s["xt_eva"], 1)

            ln_sqrt(1)
            xt_evac(0)
            act.wait_ge(s["ld_bc"], 16)
            for i in range(R2 * NC):
                r = i // NC
                if i >= 2:
                    act.wait_ge(s["m_mm"], 3 * (i - 1))
                for fo in range(2):
                    act.wait_ge(s["h_mm"], 2 * i + fo + 1)
                    a.activation(HC[i % 2][:, fo, :], PS[2 * (i % 2) + fo][:, 0:CN], ACT.Relu,
                                 bias=BC[:, 2 + 2 * r + fo:3 + 2 * r + fo]).then_inc(s["h_ev"], 1)
            act.wait_ge(s["m_mm"], 3 * R2 * NC)
            for c in range(R2 * SH):
                r, sh = c // SH, c % SH
                if c >= 2:
                    act.wait_ge(s["chunk_used"], c - 1)
                a.activation(CH[:, c % 2, :], ADJ[:, r, :].rearrange("p (n s) -> p n s", s=SH)[:, :, sh], ACT.Copy)\
                 .then_inc(s["chunk_ready"], 1)

            def agg_evac(dst, total):
                act.wait_ge(s["chunk_used"], total)
                for j in range(4):
                    a.activation(dst[:, 1, CW * j:CW * (j + 1)], PS[4 + j][:, 0:CW], ACT.Copy).then_inc(s["agg_eva"], 1)

            agg_evac(XT, R2 * SH)
            funcs = (ACT.Sigmoid, ACT.Sigmoid, ACT.Tanh, ACT.Tanh, ACT.Sigmoid, ACT.Sigmoid)
            for c in range(NC):
                for j in range(6):
                    act.wait_ge(s["gate_mm"], 6 * c + j + 1)
                    if j == 0 and c:
                        act.wait_ge(s["hn_ready"], c)
                    a.activation(GT[:, j, :], PS[j][:, 0:CN], funcs[j], bias=BC[:, 20 + j:21 + j]).then_inc(s["gate_ev"], 1)
                act.wait_ge(s["c_ready"], c + 1)
                a.activation(CC, CC, ACT.Tanh).then_inc(s["tc_ready"], 1)
                act.wait_ge(s["x1_mm"], c + 1)
                a.activation(X1, PS[6][:, 0:CN], ACT.Relu, bias=BC[:, 18:19]).then_inc(s["x1_ev"], 1)
                act.wait_ge(s["x2_mm"], c + 1)
                a.activation(X2, PS[7][:, 0:CN], ACT.Relu, bias=BC[:, 19:20]).then_inc(s["x2_ev"], 1)
            ln_sqrt(2)
            xt_evac(1)
            for v in range(2):
                for t in range(NT):
                    act.wait_ge(s["p_mm"], NT * v + t + 1)
                    a.activation(M1[:, t, :], PS[t % 4][:, 0:D], ACT.Relu).then_inc(s["p_ev"], 1)
                agg_evac(B2T, (R2 + 1 + v) * SH)
                act.wait_ge(s["o_ready"], NT * (v + 1))
                a.activation(RS[:, :], RS[:, :], ACT.Sqrt).then_inc(s["nrm_done"], 1)
                if v == 0:
                    xt_evac(2)
            ln_sqrt(3)
            xt_evac(3)
            for t in range(NT):
                act.wait_ge(s["t_mm"], t + 1)
                a.activation(XT3[:, t, :], PS[t % 4][:, 0:D + 2 * H], ACT.Copy).then_inc(s["t_ev"], 1)
            act.wait_ge(s["s3_ready"], 1)
            a.activation(S3[:, 0, :], S3[:, 0, :], ACT.Exp).then_inc(s["s3_exp"], 1)
            ln_sqrt(4)

        @block.vector
        def _(dve):
            v = nc.vector
            chain = [0]

            def link(ins):
                chain[0] += 1
                ins.then_inc(s["dve_link"], 1)
                dve.wait_ge(s["dve_link"], chain[0])

            dve.wait_ge(s["ld_rec"], 16)
            v.tensor_single_scalar(LI, RLv[:, :, 0], P - 1, ALU.bitwise_and)
            link(v.tensor_single_scalar(LJ, RLv[:, :, 0], 7, ALU.arith_shift_right))
            v.tensor_copy(Fl[:, 0, :], LI)
            v.scalar_tensor_tensor(Fl[:, 1, :], RLv[:, :, 2], float(KW), LJ, ALU.mult, ALU.add)
            v.tensor_copy(Fl[:, 2, :], RLv[:, :, 1])
            v.scalar_tensor_tensor(Fl[:, 3, :], RLv[:, :, 0], float(R8), RLv[:, :, 3], ALU.mult, ALU.add)
            link(v.tensor_scalar(IDm, RLv[:, :, 1], float(N - 1), float(R8), ALU.min, ALU.mult))
            v.tensor_tensor(IDd, IDm, RLv[:, :, 3], ALU.add).then_inc(s["fields"], 1)
            dve.wait_ge(s["idx_mm"], 1)
            v.tensor_copy(IE, PS[4][:, :]).then_inc(s["idx_ev"], 1)
            dve.wait_ge(s["idx_mm"], 2)
            v.tensor_copy(ID, PS[5][:, :]).then_inc(s["idx_ev"], 1)
            dve.wait_ge(s["ld_w0"], 16)
            dve.wait_ge(s["ld_at"], 32)
            for lr in range(2):
                for k in range(2):
                    link(v.tensor_tensor(TMP, W0[:, k, :], AT[:, lr, :], ALU.mult))
                    ins = v.tensor_reduce(VL[:, k, 32 * lr:32 * lr + 32], TMP.rearrange("p (r d) -> p r d", d=HD),
                                          AX.X, ALU.add)
                    ins.then_inc(s["vl_done"], 1)
                    dve.wait_ge(s["vl_done"], 2 * lr + k + 1)
            dve.wait_ge(s["consts"], 1)
            for g in range(GR):
                last = v.tensor_scalar(DG[:, P * g:P * (g + 1)], ident[:, :], DST[:, g, P - 1:P], None, ALU.mult)
            last.then_inc(s["diag_done"], 1)
            dve.wait_ge(s["tab_mm"], 1)
            v.tensor_copy(ELS[:, 0:8, :].rearrange("p t n -> p (t n)"), PS[0][:, :]).then_inc(s["tab_ev"], 1)
            v.tensor_copy(ELS[:, 8:NT, :].rearrange("p t n -> p (t n)"), PS[1][:, 0:(NT - 8) * 64]).then_inc(s["tab_ev"], 1)
            dve.wait_ge(s["bc_mm"], 1)
            link(v.tensor_scalar(TMP[:, 0:Q], PS[4][:, :], w16col[:, 0:1], 0.0, ALU.is_lt, ALU.add, accum_out=cnt[:, 0:1]))
            link(v.tensor_tensor(cnt[:, 1:2], cnt[:, 0:1], pcol[:, 0:1], ALU.add))
            CMP = TMP[:, 0:STEPS // 2 + 1].bitcast(F16)[:, 0:STEPS]
            v.tensor_scalar(CMP, IOT, cnt[:, 1:2], None, ALU.is_ge).then_inc(s["cmp_done"], 1)
            dve.wait_ge(s["ws_mm"], 1)
            v.tensor_scalar(WS[:, 0:512], PS[5][:, :], 1.0, None, ALU.subtract)
            link(v.tensor_scalar(WS[:, 512:STEPS], PS[6][:, 0:STEPS - 512], 1.0, None, ALU.subtract))
            v.tensor_copy(WI, WS)
            link(v.tensor_tensor(TMP[:, 1024:1024 + STEPS], IOT, WS, ALU.subtract))
            for g in range(GR):
                last = v.tensor_scalar(SEL[:, g, :], TMP[:, 1024:1024 + STEPS], pcol[:, g:g + 1], None, ALU.is_equal)
            last.then_inc(s["sel_ready"], 1)
            dve.wait_ge(s["fld_mm"], 1)
            v.tensor_copy(SLO[:, 0:512], PS[4][:, :])
            v.tensor_copy(SLO[:, 512:STEPS], PS[5][:, 0:STEPS - 512]).then_inc(s["fld_ev"], 1)
            dve.wait_ge(s["fld_mm"], 2)
            v.scalar_tensor_tensor(DJ[:, 0:512], WS[:, 0:512], -float(WIN), PS[6][:, :], ALU.mult, ALU.add)
            v.scalar_tensor_tensor(DJ[:, 512:STEPS], WS[:, 512:STEPS], -float(WIN), PS[7][:, 0:STEPS - 512], ALU.mult, ALU.add)\
             .then_inc(s["fld_ev"], 1)
            dve.wait_ge(s["fld_ev"], 2)
            link(v.tensor_scalar(TMP[:, 0:STEPS], DJ, 0.0, 1e6, ALU.is_lt, ALU.mult))
            link(v.tensor_scalar(TMP[:, 1024:1024 + STEPS], DJ, float(WIN - 1), 1e6, ALU.is_gt, ALU.mult))
            link(v.tensor_tensor(KEY, TMP[:, 0:STEPS], TMP[:, 1024:1024 + STEPS], ALU.add))
            link(v.scalar_tensor_tensor(KEY, DJ, float(SH), KEY, ALU.mult, ALU.add))
            dve.wait_ge(s["fld_mm"], 3)
            v.tensor_tensor(KEY[:, 0:512], KEY[:, 0:512], PS[4][:, :], ALU.add)
            v.tensor_tensor(KEY[:, 512:STEPS], KEY[:, 512:STEPS], PS[5][:, 0:STEPS - 512], ALU.add)
            dve.wait_ge(s["fld_mm"], 4)
            v.tensor_copy(IDX[:, 0:512], PS[6][:, :])
            v.tensor_copy(IDX[:, 512:STEPS], PS[7][:, 0:STEPS - 512]).then_inc(s["steps_done"], 1)
            dve.wait_ge(s["tab_st"], 32)
            v.memset(ADJ[:, :, :].rearrange("p r k -> p (r k)").bitcast(F32), 0.0).then_inc(s["a_add"], 1)

            def onehots(k, col):
                v.tensor_scalar(OHS[k], iota128[:, :], SLO[:, col], None, ALU.is_equal)
                v.tensor_scalar(OHK[k], iota480[:, :], KEY[:, col], None, ALU.is_equal).then_inc(s["a_oh"], 1)

            def add_step(k, step):
                w = dve.value_load(WI[0:1, bass.ds(step, 1)], min_val=0, max_val=WINS - 1)
                dst = ADJ[:, :, bass.ds(w * KW, KW)]
                v.tensor_tensor(dst, dst, EV[k], ALU.add).then_inc(s["a_add"], 1)

            dve.wait_ge(s["steps_done"], 1)
            for k in range(2):
                onehots(k, slice(k, k + 1))
            with dve.Fori(0, STEPS // 2 - 1) as i:
                for k in range(2):
                    dve.wait_ge(s["a_mm"], i * 2 + (k + 1))
                    onehots(k, bass.ds(i * 2 + (2 + k), 1))
                    dve.wait_ge(s["a_ev"], i * 2 + (k + 1))
                    dve.wait_ge(s["a_add"], i * 2 + (k + 1))
                    add_step(k, i * 2 + k)
            for k in range(2):
                dve.wait_ge(s["a_ev"], STEPS - 1 + k)
                dve.wait_ge(s["a_add"], STEPS - 1 + k)
                w = dve.value_load(WI[0:1, STEPS - 2 + k:STEPS - 1 + k], min_val=0, max_val=WINS - 1)
                dst = ADJ[:, :, bass.ds(w * KW, KW)]
                v.tensor_tensor(dst, dst, EV[k], ALU.add).then_inc(s["a_add"], 1)

            dve.wait_ge(s["pool_link"], LINKS)
            for i in range(4):
                dve.wait_ge(fs_st[i], NT * 16)
            SUMf = SUM.rearrange("p t h -> p (t h)")
            v.scalar_tensor_tensor(SUMf, SUMf, 0.2, SUMf, ALU.mult, ALU.max).then_inc(s["lane_in"], 1)
            same = FL[:, 0, :].rearrange("p (g e) -> p g e", g=GR)
            sameb = FL[:, 1, :].rearrange("p (g e) -> p g e", g=GR)
            for f in (FL[:, 0, :], FL[:, 1, :]):
                link(v.memset(f, 0.0))
            v.tensor_tensor(same[:, :, 1:P], DST[:, :, 1:P], DST[:, :, 0:P - 1], ALU.is_equal)
            link(v.tensor_tensor(sameb[:, :, 0:P - 1], DST[:, :, 0:P - 1], DST[:, :, 1:P], ALU.is_equal))
            for j in range(2):
                link(v.tensor_scalar(FL[:, 2 + j, :], FL[:, j, :], -1.0, BIG, ALU.add, ALU.mult))
            for j, e in enumerate((0, P - 1)):
                for h in range(H):
                    last = v.tensor_copy(RD[:, j, :].rearrange("p (g h) -> p g h", h=H)[:, :, h], DST[:, :, e])
            last.then_inc(s["flags_in"], 1)
            D0R, D1R, LKR, UNR, CR = (ROW[0:H, j, :] for j in range(5))
            dve.wait_ge(s["flags_mm"], 1)
            v.tensor_copy(D0R, PS[4][0:H, :])
            link(v.tensor_copy(D1R, PS[5][0:H, :]))
            link(v.tensor_tensor(UNR, D0R, D1R, ALU.is_equal))
            link(v.memset(LKR, 0.0))
            link(v.tensor_tensor(LKR[:, 1:Q], D0R[:, 1:Q], D1R[:, 0:Q - 1], ALU.is_equal))
            D0R_, D1R_ = D0R, D1R

            def seg_scan(dst, op, mx, back, n):
                ident_ = -BIG if mx else 0.0
                op0 = ALU.add if mx else ALU.mult
                flags = FL[:, (2 if mx else 0) + back, :]
                e0, e1 = (P - 1, 0) if back else (0, P - 1)
                rev = (lambda ap: ap[:, ::-1]) if back else (lambda ap: ap)

                def scans():
                    for h in range(H):
                        ins = v.tensor_tensor_scan(rev(dst[:, h, :]), rev(flags), rev(S[:, h, :]), ident_, op0, op)
                    return ins

                scans().then_inc(s["tail_ready"], 1)
                cont = D0R_
                lk = LKR[:, 1:Q] if back else LKR[:, 0:Q]
                link(v.memset(cont, 0.0))
                m = Q - 1 if back else Q
                link(v.tensor_tensor(cont[:, 0:m], UNR[:, 0:m], lk, ALU.mult))
                if mx:
                    link(v.tensor_scalar(cont, cont, -1.0, BIG, ALU.add, ALU.mult))
                dve.wait_ge(s["tail_mm"], n)
                link(v.tensor_copy(D1R_, PS[4][0:H, :]))
                link(v.tensor_tensor_scan(rev(CR), rev(cont), rev(D1R_), ident_, op0, op))
                link(v.memset(cont, ident_))
                lk1 = LKR[:, 1:Q]
                src = CR[:, 1:Q] if back else CR[:, 0:Q - 1]
                to = cont[:, 0:Q - 1] if back else cont[:, 1:Q]
                if mx:
                    link(v.tensor_scalar(D1R_[:, 1:Q], lk1, -1.0, BIG, ALU.add, ALU.mult))
                    v.tensor_tensor(to, src, D1R_[:, 1:Q], ALU.add).then_inc(s["cin_ready"], 1)
                else:
                    v.tensor_tensor(to, src, lk1, ALU.mult).then_inc(s["cin_ready"], 1)
                edge = S.rearrange("p h (g e) -> p h g e", g=GR)[:, :, :, e0]
                keep = SC16[:, 0, :].rearrange("p (h g) -> p h g", h=H)
                link(v.tensor_copy(keep, edge))
                dve.wait_ge(s["cin_mm"], n)
                carry = PS[5][:, 0:GR * H].rearrange("p (g h) -> p h g", h=H)
                link(v.tensor_tensor(edge, keep, carry, op))
                link(scans())
                link(v.tensor_copy(edge, keep))

            dve.wait_ge(s["lane_ev"], H)
            seg_scan(FA, ALU.max, True, 0, 1)
            seg_scan(BA, ALU.max, True, 1, 2)
            flat = lambda ap: ap.rearrange("p h n -> p (h n)")
            link(v.tensor_tensor(flat(FA), flat(FA), flat(BA), ALU.max))
            v.tensor_tensor(flat(S), flat(S), flat(FA), ALU.subtract).then_inc(s["exp_ready"], 1)
            dve.wait_ge(s["exp_done"], 1)
            seg_scan(FA, ALU.add, False, 0, 3)
            seg_scan(BA, ALU.add, False, 1, 4)
            link(v.tensor_tensor(flat(FA), flat(FA), flat(BA), ALU.add))
            link(v.tensor_tensor(flat(FA), flat(FA), flat(S), ALU.subtract))
            link(v.reciprocal(flat(FA), flat(FA)))
            v.tensor_tensor(flat(S), flat(S), flat(FA), ALU.mult).then_inc(s["alpha_ready"], 1)
            dve.wait_ge(s["als_mm"], H)
            v.memset(ACCf, 0.0).then_inc(s["l_acc"], 1)
            dve.wait_ge(s["als_ev"], H)

            def weigh(slot, st):
                wv = WOH[:, slot, :].rearrange("p (h j) -> p h j", h=H)
                al = ALSf[:, bass.ds(st * H, H)]
                col = bass.ds(st, 1)
                v.scalar_tensor_tensor(wv, iota16[:, :].rearrange("p (a j) -> p a j", a=1).to_broadcast([P, H, WIN]),
                                       DJ[:, col],
                                       al.rearrange("p (h a) -> p h a", a=1).to_broadcast([P, H, WIN]),
                                       ALU.is_equal, ALU.mult).then_inc(s["l_woh"], 1)

            def accumulate(bank, col):
                w = dve.value_load(WI[0:1, col], min_val=0, max_val=WINS - 1)
                dst = ACCf[:, bass.ds(w * 64, 64)]
                v.tensor_tensor(dst, dst, PS[bank][:, 0:64], ALU.add).then_inc(s["l_acc"], 1)

            for st in range(HEAD + FR):
                if st >= 4:
                    dve.wait_ge(s["l_mm"], st - 3)
                weigh(st % 4, st)
                if st >= 2:
                    dve.wait_ge(s["l_mm"], st - 1)
                    dve.wait_ge(s["l_acc"], st - 1)
                    accumulate(6 + st % 2, slice(st - 2, st - 1))
            with dve.Fori(0, (GRPS - 1) // 2) as i:
                for u in range(2 * FR):
                    st = HEAD + FR + u
                    dve.wait_ge(s["l_mm"], i * (2 * FR) + (st - 3))
                    weigh(st % 4, i * (2 * FR) + st)
                    dve.wait_ge(s["l_mm"], i * (2 * FR) + (st - 1))
                    dve.wait_ge(s["l_acc"], i * (2 * FR) + (st - 1))
                    accumulate(6 + st % 2, bass.ds(i * (2 * FR) + (st - 2), 1))
            for st in range(STEPS, STEPS + 2):
                dve.wait_ge(s["l_mm"], st - 1)
                dve.wait_ge(s["l_acc"], st - 1)
                accumulate(6 + st % 2, slice(st - 2, st - 1))

            dve.wait_ge(s["l_acc"], STEPS + 1)
            dve.wait_ge(s["ld_bc"], 16)
            v.memset(XT[:, :, NW:NP], 0.0)
            for f in range(2):
                for hh in range(2):
                    p0 = 64 * hh
                    c0 = 32 * f + 16 * hh
                    v.tensor_scalar(XT[p0:p0 + 64, f, 0:NW].rearrange("p (w j) -> p w j", j=WIN),
                                    ACC[p0:p0 + 64, :, c0:c0 + WIN], BC[p0:p0 + 64, f:f + 1], None, ALU.add)
            v.memset(X[:, NT - 1, :], 0.0).then_inc(s["ht_ready"], 1)
            v.tensor_tensor(BC[:, 20:26], BC[:, 6:12], BC[:, 12:18], ALU.add)
            dve.wait_ge(s["ld_x"], 32)
            for t in range(NT):
                dve.wait_ge(s["ht_mm"], t + 1)
                v.tensor_tensor(X[:, t, :], X[:, t, :], PS[t % 4][:, 0:D], ALU.add).then_inc(s["ht_add"], 1)

            lns = [0]

            def layer_norm():
                lns[0] += 1
                for t in range(NT):
                    ins = v.bn_stats(ST[:, t, :], X[:, t, :])
                link(ins)
                for t in range(NT):
                    ins = v.bn_aggr(MV[:, t, :], ST[:, t, :])
                link(ins)
                v.tensor_scalar(MV[:, :, 1], MV[:, :, 1], EPS, None, ALU.add).then_inc(s["var_ready"], 1)
                dve.wait_ge(s["std_ready"], lns[0])
                link(v.reciprocal(RS[:, :], RS[:, :]))
                for t in range(NT):
                    ins = v.tensor_scalar(X[:, t, :], X[:, t, :], MV[:, t, 0:1], RS[:, t:t + 1], ALU.subtract, ALU.mult)
                ins.then_inc(s["ln_done"], 1)

            def xt_evac(n):
                for q in range(4):
                    dve.wait_ge(s["xt_mm"], 8 * n + 2 * q + 2)
                    w = min(512, NP - 512 * q)
                    v.tensor_copy(XT[:, 1, 512 * q:512 * q + w], PS[2 * q + 1][:, 0:w]).then_inc(s["xt_evd"], 1)

            dve.wait_ge(s["ht_add"], NT)
            layer_norm()
            xt_evac(0)
            for i in range(R2 * NC):
                r, c = i // NC, i % NC
                for j in range(3):
                    dve.wait_ge(s["m_mm"], 3 * i + j + 1)
                    v.tensor_scalar((M1, M2)[r][:, 3 * c + j, :], PS[4 + j][:, 0:D], 0.0, None, ALU.max).then_inc(s["m_ev"], 1)

            def agg_evac(dst, total):
                dve.wait_ge(s["chunk_used"], total)
                for j in range(4):
                    v.tensor_copy(dst[:, 0, CW * j:CW * (j + 1)], PS[j][:, 0:CW])
                v.memset(dst[:, :, NW:NP], 0.0).then_inc(s["agg_evd"], 1)

            agg_evac(XT, R2 * SH)
            for c in range(NC):
                dve.wait_ge(s["gate_ev"], 6 * c + 4)
                v.tensor_tensor(CC, GT[:, 0:2, :], GT[:, 2:4, :], ALU.mult).then_inc(s["c_ready"], 1)
                dve.wait_ge(s["tc_ready"], c + 1)
                dve.wait_ge(s["gate_ev"], 6 * c + 6)
                if c:
                    dve.wait_ge(s["x1_mm"], c)
                v.tensor_tensor(HN, CC, GT[:, 4:6, :], ALU.mult).then_inc(s["hn_ready"], 1)
                dve.wait_ge(s["x3_mm"], c + 1)
                xv = X[:, 3 * c:3 * c + 2, :].rearrange("p t d -> p (t d)")
                v.tensor_tensor(xv, xv, PS[6][:, :], ALU.add)
                v.tensor_tensor(X[:, 3 * c + 2, :], X[:, 3 * c + 2, :], PS[7][:, 0:D], ALU.add).then_inc(s["x3_add"], 1)
            dve.wait_ge(s["x3_add"], NC)
            layer_norm()
            xt_evac(1)
            link(v.memset(RC[:, :], 1.0))
            base = R2 * SH
            for u in range(2):
                for c in range(SH):
                    if c >= 2:
                        dve.wait_ge(s["chunk_used"], base + u * SH + c - 1)
                        if u == 0:
                            dve.wait_ge(s["cnt_acc"], c - 1)
                    a0, a1 = (ADJ[:, r, :].rearrange("p (n s) -> p n s", s=SH)[:, :, c] for r in range(R2))
                    v.tensor_tensor(CH[:, c % 2, :], a0, a1, ALU.add).then_inc(s["chunk_ready"], 1)
                if u == 0:
                    dve.wait_ge(s["cnt_mm"], 1)
                    lastn = NW - (NT - 1) * P
                    v.tensor_scalar(RC[:, 0:NT - 1], PS[4][:, 0:NT - 1], 1.0, None, ALU.max)
                    link(v.tensor_scalar(RC[0:lastn, NT - 1:NT], PS[4][0:lastn, NT - 1:NT], 1.0, None, ALU.max))
                    link(v.reciprocal(RC[:, :], RC[:, :]))
                agg_evac(B2T, base + (u + 1) * SH)
                for t in range(NT):
                    b = 2 * (t % 4)
                    dve.wait_ge(s["o_mm"], NT * u + t + 1)
                    link(v.tensor_scalar(B1[:, t, :], PS[b][:, 0:D], RC[:, t:t + 1], None, ALU.mult))
                    link(v.tensor_tensor(B1[:, t, :], B1[:, t, :], PS[b + 1][:, 0:D], ALU.add))
                    v.tensor_tensor_reduce(out=CH[:, 0, 0:D], in0=B1[:, t, :], in1=B1[:, t, :], scale=1.0, scalar=0.0,
                                           op0=ALU.mult, op1=ALU.add, accum_out=RS[:, t:t + 1]).then_inc(s["o_ready"], 1)
                dve.wait_ge(s["nrm_done"], u + 1)
                link(v.tensor_scalar(RS[:, :], RS[:, :], 1e-12, None, ALU.max))
                link(v.reciprocal(RS[:, :], RS[:, :]))
                if u == 0:
                    for t in range(NT):
                        ins = v.tensor_scalar(B1[:, t, :], B1[:, t, :], RS[:, t:t + 1], 0.0, ALU.mult, ALU.max)
                    ins.then_inc(s["h_ready"], 1)
                    xt_evac(2)
                else:
                    for t in range(NT):
                        ins = v.scalar_tensor_tensor(X[:, t, :], B1[:, t, :], RS[:, t:t + 1], X[:, t, :], ALU.mult, ALU.add)
                    link(ins)
            layer_norm()
            dve.wait_ge(s["ld_wt3"], 48)
            for lr in range(2):
                for k in range(2):
                    link(v.tensor_tensor(TMP3, WT3[:, k, 0:D], A3[:, lr, :], ALU.mult))
                    ins = v.tensor_reduce(WT3[:, k, D + H * lr:D + H * (lr + 1)], TMP3.rearrange("p (h d) -> p h d", d=HD),
                                          AX.X, ALU.add)
                    if (lr, k) == (1, 1):
                        ins.then_inc(s["vl3_done"], 1)
                    else:
                        link(ins)
            xt_evac(3)
            dve.wait_ge(s["g3"], 16 * 2 * NT)
            a3 = lambda j: S3[:, j, :].rearrange("p (t h) -> p t h", h=H)
            link(v.tensor_tensor(a3(0), AG3, G3[:, :, D + H:D + 2 * H], ALU.add))
            link(v.scalar_tensor_tensor(S3[:, 0, :], S3[:, 0, :], 0.01, S3[:, 0, :], ALU.mult, ALU.max))
            m3 = S3[:, 1, 0:NT]
            link(v.tensor_reduce(m3, a3(0), AX.X, ALU.max))
            v.tensor_tensor(a3(0), a3(0), m3.rearrange("p (t a) -> p t a", a=1).to_broadcast([P, NT, H]),
                            ALU.subtract).then_inc(s["s3_ready"], 1)
            dve.wait_ge(s["s3_exp"], 1)
            link(v.tensor_reduce(m3, a3(0), AX.X, ALU.add))
            link(v.reciprocal(m3, m3))
            link(v.tensor_tensor(a3(0), a3(0), m3.rearrange("p (t a) -> p t a", a=1).to_broadcast([P, NT, H]), ALU.mult))
            for t in range(NT):
                gv = G3[:, t, 0:D].rearrange("p (h d) -> p h d", h=H)
                ins = v.tensor_tensor(gv, gv, S3[:, 0, H * t:H * t + H].rearrange("p (h a) -> p h a", a=1).to_broadcast([P, H, HD]), ALU.mult)
            link(ins)
            for t in range(NT):
                ins = v.tensor_reduce(T64[:, t, :], G3[:, t, 0:D].rearrange("p (h d) -> p d h", h=H), AX.X, ALU.add)
            link(ins)
            for t in range(NT):
                xv = X[:, t, :].rearrange("p (h d) -> p h d", h=H)
                ins = v.tensor_tensor(xv, xv, T64[:, t, :].rearrange("p (a d) -> p a d", a=1).to_broadcast([P, H, HD]), ALU.add)
            link(ins)
            layer_norm()

        @block.tensor
        def _(pe):
            mm = nc.tensor.matmul
            tr = nc.tensor.transpose
            pe.wait_ge(s["consts"], 1)
            pe.wait_ge(s["fields"], 1)
            for j, src in enumerate((Fl[:, 3, :], IDd)):
                for g in range(GR):
                    ins = tr(PS[4 + j][:, P * g:P * (g + 1)], src[:, P * g:P * (g + 1)], ident[:, :])
                ins.then_inc(s["idx_mm"], 1)
            pe.wait_ge(s["vl_done"], 4)
            pe.wait_ge(s["ld_xt"], 16)
            for t in range(NT):
                for k in range(2):
                    ins = mm(PS[t // 8][:, 64 * (t % 8):64 * (t % 8 + 1)], XT0[:, k, P * t:P * (t + 1)], VL[:, k, :],
                             start=(k == 0), stop=(k == 1))
            ins.then_inc(s["tab_mm"], 1)
            pe.wait_ge(s["diag_done"], 1)
            pe.wait_ge(s["idx_ev"], 2)
            mm(PS[4][:, :], ones[:, :], DG, start=True, stop=True).then_inc(s["bc_mm"], 1)
            pe.wait_ge(s["cmp_done"], 1)
            CMP = TMP[:, 0:STEPS // 2 + 1].bitcast(F16)[:, 0:STEPS]
            mm(PS[5][:, :], ones16[:, :], CMP[:, 0:512], start=True, stop=True)
            mm(PS[6][:, 0:STEPS - 512], ones16[:, :], CMP[:, 512:STEPS], start=True, stop=True).then_inc(s["ws_mm"], 1)

            def select(lhs, b0):
                for (bank, lo, hi) in ((b0, 0, 512), (b0 + 1, 512, STEPS)):
                    for g in range(GR):
                        ins = mm(PS[bank][:, 0:hi - lo], lhs(g), SEL[:, g, lo:hi], start=(g == 0), stop=(g == GR - 1))
                return ins

            pe.wait_ge(s["sel_ready"], 1)
            for n, f in enumerate((0, 2, 1, 3)):
                if n >= 2:
                    pe.wait_ge(s["fld_ev"], n - 1)
                select(lambda g: Fl[:, f, P * g:P * (g + 1)], 4 + 2 * (n % 2)).then_inc(s["fld_mm"], 1)
            pe.wait_ge(s["tab_ev"], 2)
            for i in range(4 * NT):
                t, c = i // 4, i % 4
                if i >= 4:
                    pe.wait_ge(s["feat_ev"], i - 3)
                for k in range(2):
                    ins = mm(PS[c][:, :], XT0[:, k, P * t:P * (t + 1)], W0[:, k, 512 * c:512 * (c + 1)],
                             start=(k == 0), stop=(k == 1))
                ins.then_inc(s["feat_mm"], 1)
            pe.wait_ge(s["steps_done"], 1)
            for k in range(2):
                pe.wait_ge(s["a_oh"], k + 1)
                mm(PS[6 + k][:, 0:R2 * KW], OHS[k], OHK[k], start=True, stop=True).then_inc(s["a_mm"], 1)
            with pe.Fori(0, STEPS // 2 - 1) as i:
                for k in range(2):
                    pe.wait_ge(s["a_oh"], i * 2 + (3 + k))
                    pe.wait_ge(s["a_ev"], i * 2 + (1 + k))
                    mm(PS[6 + k][:, 0:R2 * KW], OHS[k], OHK[k], start=True, stop=True).then_inc(s["a_mm"], 1)
            pe.wait_ge(s["lane_in"], 1)
            for h in range(H):
                for g in range(GR):
                    ins = tr(PS[h][:, P * g:P * (g + 1)], SUM[:, P * g:P * (g + 1), h], ident[:, :])
                ins.then_inc(s["lane_mm"], 1)
            pe.wait_ge(s["flags_in"], 1)
            for j in range(2):
                for g in range(GR):
                    ins = tr(PS[4 + j][0:H, P * g:P * (g + 1)], RD[:, j, H * g:H * (g + 1)], ident[:, :])
            ins.then_inc(s["flags_mm"], 1)
            for n in range(4):
                dst = (FA, BA)[n % 2].rearrange("p h (g e) -> p h g e", g=GR)
                e1 = (P - 1, 0)[n % 2]
                pe.wait_ge(s["tail_ready"], n + 1)
                for g in range(GR):
                    ins = tr(PS[4][0:H, P * g:P * (g + 1)], dst[:, :, g, e1], ident[:, :])
                ins.then_inc(s["tail_mm"], 1)
                pe.wait_ge(s["cin_ready"], n + 1)
                for g in range(GR):
                    ins = tr(PS[5][:, H * g:H * (g + 1)], ROW[0:H, 0, P * g:P * (g + 1)], ident[0:H, 0:H])
                ins.then_inc(s["cin_mm"], 1)
            pe.wait_ge(s["alpha_ready"], 1)
            pe.wait_ge(s["a_ev"], STEPS)
            for h in range(H):
                select(lambda g: S[:, h, P * g:P * (g + 1)], 2 * h).then_inc(s["als_mm"], 1)
            pe.wait_ge(s["als_ev"], H)

            def scatter(slot, woh, bank):
                for f in range(2):
                    ins = mm(PS[bank][:, 32 * f:32 * (f + 1)], FB[:, slot, P * f:P * (f + 1)],
                             WOH[:, woh, 32 * f:32 * (f + 1)], start=True, stop=True)
                ins.then_inc(s["l_mm"], 1)

            for st in range(HEAD + FR):
                pe.wait_ge(s["l_woh"], st + 1)
                pe.wait_ge(f_done[st % FR], 16 * (st // FR + 1))
                if st >= 2:
                    pe.wait_ge(s["l_acc"], st)
                scatter(st % FR, st % 4, 6 + st % 2)
            with pe.Fori(0, (GRPS - 1) // 2) as i:
                for u in range(2 * FR):
                    st = HEAD + FR + u
                    pe.wait_ge(s["l_woh"], i * (2 * FR) + (st + 1))
                    pe.wait_ge(f_done[st % FR], i * 32 + 16 * (st // FR + 1))
                    pe.wait_ge(s["l_acc"], i * (2 * FR) + st)
                    scatter(st % FR, st % 4, 6 + st % 2)
            pe.wait_ge(s["ht_ready"], 1)
            for t in range(NT):
                if t >= 4:
                    pe.wait_ge(s["ht_add"], t - 3)
                for f in range(2):
                    ins = tr(PS[t % 4][:, P * f:P * (f + 1)], XT[:, f, P * t:P * (t + 1)], ident[:, :])
                ins.then_inc(s["ht_mm"], 1)

            def transpose_x(n, src, ready):
                pe.wait_ge(ready[0], ready[1])
                for q in range(4):
                    for k in range(2):
                        for j in range(min(4, NT - 4 * q)):
                            ins = tr(PS[2 * q + k][:, P * j:P * (j + 1)], src[:, 4 * q + j, P * k:P * (k + 1)], ident[:, :])
                        ins.then_inc(s["xt_mm"], 1)
                pe.wait_ge(s["xt_eva"], 4 * (n + 1))
                pe.wait_ge(s["xt_evd"], 4 * (n + 1))

            transpose_x(0, X, (s["ln_done"], 1))
            pe.wait_ge(s["ld_wt1"], 16 * 9)

            def hidden(i):
                r, c = i // NC, i % NC
                if i >= 2:
                    pe.wait_ge(s["h_ev"], 2 * (i - 1))
                for fo in range(2):
                    for k in range(2):
                        ins = mm(PS[2 * (i % 2) + fo][:, 0:CN], WREL[:, k, r, P * fo:P * (fo + 1)],
                                 XT[:, k, CN * c:CN * (c + 1)], start=(k == 0), stop=(k == 1))
                    ins.then_inc(s["h_mm"], 1)

            hidden(0)
            for i in range(R2 * NC):
                if i + 1 < R2 * NC:
                    hidden(i + 1)
                r = i // NC
                pe.wait_ge(s["h_ev"], 2 * (i + 1))
                if i:
                    pe.wait_ge(s["m_ev"], 3 * i)
                for j in range(3):
                    mm(PS[4 + j][:, 0:D], ones[0:1, :], BROW[0:1, r, :], start=True, stop=False)
                    for k in range(2):
                        ins = mm(PS[4 + j][:, 0:D], HC[i % 2][:, k, P * j:P * (j + 1)], WREL[:, k, r, :],
                                 start=False, stop=(k == 1))
                    ins.then_inc(s["m_mm"], 1)
            pe.wait_ge(s["m_ev"], 3 * R2 * NC)

            def aggregate(mats, first):
                n = len(mats) * SH
                for c in range(n):
                    m, sh = mats[c // SH], c % SH
                    pe.wait_ge(s["chunk_ready"], first + c + 1)
                    for fo in range(2):
                        for j in range(4):
                            ins = mm(PS[4 * fo + j][:, 0:CW], m[:, sh, P * fo:P * (fo + 1)],
                                     CH[:, c % 2, CW * j:CW * (j + 1)], start=(c == 0), stop=(c == n - 1))
                    ins.then_inc(s["chunk_used"], 1)

            aggregate((M1, M2), 0)
            pe.wait_ge(s["agg_evd"], 1)
            pe.wait_ge(s["agg_eva"], 4)
            for c in range(NC):
                cs = slice(CN * c, CN * (c + 1))
                if c:
                    pe.wait_ge(s["gate_ev"], 6 * c)
                for j in range(6):
                    for k in range(2):
                        ins = mm(PS[j][:, 0:CN], WIH[:, k, P * j:P * (j + 1)], XT[:, k, cs], start=(k == 0), stop=(k == 1))
                    ins.then_inc(s["gate_mm"], 1)
                pe.wait_ge(s["hn_ready"], c + 1)
                if c:
                    pe.wait_ge(s["x3_add"], c)
                for k in range(2):
                    ins = mm(PS[6][:, 0:CN], W1s[:, k, :], HN[:, k, :], start=(k == 0), stop=(k == 1))
                ins.then_inc(s["x1_mm"], 1)
                pe.wait_ge(s["x1_ev"], c + 1)
                mm(PS[7][:, 0:CN], W2s, X1, start=True, stop=True).then_inc(s["x2_mm"], 1)
                pe.wait_ge(s["x2_ev"], c + 1)
                for j in range(3):
                    o = PS[6 + j // 2][:, D * (j % 2):D * (j % 2 + 1)]
                    mm(o, ones[0:1, :], BROW[0:1, 2, :], start=True, stop=False)
                    ins = mm(o, X2[:, P * j:P * (j + 1)], W3s, start=False, stop=True)
                ins.then_inc(s["x3_mm"], 1)
            transpose_x(1, X, (s["ln_done"], 2))
            pe.wait_ge(s["ld_wt2"], 160)
            for u in range(2):
                Wp, Wl, Wr = W2L[3 * u:3 * u + 3]
                for t in range(NT):
                    if t >= 4:
                        pe.wait_ge(s["p_ev"], NT * u + t - 3)
                    mm(PS[t % 4][:, 0:D], ones[0:1, :], BROW[0:1, 2 * u, :], start=True, stop=False)
                    for k in range(2):
                        ins = mm(PS[t % 4][:, 0:D], XT[:, k, P * t:P * (t + 1)], Wp[:, k, :], start=False, stop=(k == 1))
                    ins.then_inc(s["p_mm"], 1)
                pe.wait_ge(s["p_ev"], NT * (u + 1))
                aggregate((M1,), (R2 + u) * SH)
                if u == 0:
                    pe.wait_ge(s["cnt_acc"], SH)
                    pe.wait_ge(s["agg_eva"], 5)
                    for t in range(NT):
                        w = min(P, NW - P * t)
                        ins = mm(PS[4][0:w, t:t + 1], B2T[:, 0, P * t:P * t + w], ones[:, 0:1], start=True, stop=True)
                    ins.then_inc(s["cnt_mm"], 1)
                pe.wait_ge(s["agg_evd"], 2 + u)
                pe.wait_ge(s["agg_eva"], 4 * (2 + u))
                for t in range(NT):
                    if t >= 4:
                        pe.wait_ge(s["o_ready"], NT * u + t - 3)
                    b = 2 * (t % 4)
                    for k in range(2):
                        mm(PS[b][:, 0:D], B2T[:, k, P * t:P * (t + 1)], Wl[:, k, :], start=(k == 0), stop=(k == 1))
                    mm(PS[b + 1][:, 0:D], ones[0:1, :], BROW[0:1, 1 + 2 * u, :], start=True, stop=False)
                    for k in range(2):
                        ins = mm(PS[b + 1][:, 0:D], XT[:, k, P * t:P * (t + 1)], Wr[:, k, :], start=False, stop=(k == 1))
                    ins.then_inc(s["o_mm"], 1)
                if u == 0:
                    transpose_x(2, B1, (s["h_ready"], 1))
            transpose_x(3, X, (s["ln_done"], 3))
            pe.wait_ge(s["vl3_done"], 1)
            for t in range(NT):
                if t >= 4:
                    pe.wait_ge(s["t_ev"], t - 3)
                for k in range(2):
                    ins = mm(PS[t % 4][:, 0:D + 2 * H], XT[:, k, P * t:P * (t + 1)], WT3[:, k, :], start=(k == 0), stop=(k == 1))
                ins.then_inc(s["t_mm"], 1)


def layout(i):
    import numpy as np
    c = np.ascontiguousarray
    g = {k: np.asarray(v) for k, v in i.items()}
    rec = np.zeros((EP, 4), np.int32)
    rec[:, 1] = PAD_DST
    rec[:E, 0] = g["src"]
    rec[:E, 1] = g["dst"]
    rec[:E, 2] = g["edge_type_2"]
    rec[:E, 3] = g["edge_type_8"]
    xT = np.zeros((D, NP), np.float32)
    xT[:, :N] = g["x"].T
    w_ih = g["L1_gnn_W_ih"].T
    pick = lambda a: np.concatenate([a[..., 0:D], a[..., 2 * D:4 * D]], -1)
    row = lambda a: c(a.reshape(1, -1))
    cols = c(np.concatenate([g["L0_gnn_h_bias"], g["L1_gnn_b_rel"].reshape(-1), pick(g["L1_gnn_b_ih"]),
                             pick(g["L1_gnn_b_hh"]), g["L1_gnn_b1"], g["L1_gnn_b2"]]).reshape(20, P).T)
    return [
        ("rec", rec), ("x", c(g["x"])), ("xT", xT), ("edge0", c(np.stack([g["src"][:NP], g["dst"][:NP]]).reshape(2, NT, P).transpose(2, 0, 1))),
        ("w0", c(g["L0_gnn_conv_weights"].transpose(2, 0, 1, 3).reshape(D, R8 * D))),
        ("a0l", row(g["L0_gnn_attn_l"])), ("a0r", row(g["L0_gnn_attn_r"])), ("cols", cols),
        ("wrel", c(g["L1_gnn_W_rel"].transpose(0, 2, 1))), ("brow", c(g["L1_gnn_b_rel"])),
        ("wih", c(pick(w_ih))),
        ("w1", c(g["L1_gnn_W1"].T)), ("w2", c(g["L1_gnn_W2"].T)),
        ("w3", c(g["L1_gnn_W3"].T)), ("b3", row(g["L1_gnn_b3"])),
        ("wp1", c(g["L2_gnn_W_proj1"])), ("bp1", row(g["L2_gnn_b_proj1"])), ("wl1", c(g["L2_gnn_W_l1"])),
        ("bl1", row(g["L2_gnn_b_l1"])), ("wr1", c(g["L2_gnn_W_r1"])),
        ("wp2", c(g["L2_gnn_W_proj2"])), ("bp2", row(g["L2_gnn_b_proj2"])), ("wl2", c(g["L2_gnn_W_l2"])),
        ("bl2", row(g["L2_gnn_b_l2"])), ("wr2", c(g["L2_gnn_W_r2"])),
        ("wt3", c(g["L3_gnn_weight"])), ("a3l", row(g["L3_gnn_attn_l"])), ("a3r", row(g["L3_gnn_attn_r"])),
    ]


def kernel(**inputs):
    import concourse.bacc as bacc
    from concourse.bass_utils import run_bass_kernel_spmd as run

    nc = bacc.Bacc("TRN2", target_bir_lowering=False, num_devices=1)
    arrays, args = {}, []
    for name, a in layout(inputs):
        arrays["in_" + name] = a
        args.append(nc.dram_tensor("in_" + name, a.shape, mybir.dt.from_np(a.dtype), kind="ExternalInput").ap())
    args.append(nc.dram_tensor("out_0", (N, D), F32, kind="ExternalOutput").ap())
    build(nc, *args)
    r = run(nc, [arrays], core_ids=[0])
    return r.results[0]["out_0"]
```

```python
import concourse.bass as bass
from concourse import mybir
from contextlib import ExitStack

F32 = mybir.dt.float32
F16 = mybir.dt.float16
BF16 = mybir.dt.bfloat16
I32 = mybir.dt.int32
SP, DVE, PE = mybir.EngineType.SP, mybir.EngineType.DVE, mybir.EngineType.PE
U16 = mybir.dt.uint16
ALU = mybir.AluOpType
ACT = mybir.ActivationFunctionType
AX = mybir.AxisListType

N = 1875
E = 60000
D = 256
P = 128
NT = -(-N // P)
NP = NT * P
NLAST = N - (NT - 1) * P
H = 4
HD = D // H
R8 = 8
R2 = 2
GR = 4
EP = GR * P * P
TILES = -(-E // P)
WIN = 16
WINS = -(-N // WIN)
NW = WINS * WIN
STEPS = E // P + WINS
SH = NT
KW = WIN * SH
PAD_DST = 2047
BIG = 1e30
EPS = 1e-5
Q = 4 * P

FW = D + H
CK = 16
NCK = STEPS // CK
CTAIL = STEPS - NCK * CK
AU = 8
assert (STEPS - 2) % AU == 0
assert NCK % 2 == 0 and CTAIL > 0
TABS_AT = 14
SC = -(-STEPS // P)
GB = 7
NGB = TILES // GB
assert NGB * GB == TILES and NGB % 2 == 1
BATCH = 16 * GB
N_IT = (NGB - 3) // 2
LINKS = 4 + 4 * N_IT + 4
FR = 8
HEAD = 2
GRPS = (STEPS - HEAD) // FR
assert HEAD + GRPS * FR == STEPS and GRPS % 2 == 1
CW = NW // 4
CN = 3 * P
NC = NP // CN

A_SLO, A_KEY, A_DJ, A_IDX, A_WS, A_WI, A_IOT = (STEPS * i for i in range(7))
A_SEL = 7 * STEPS
A_F = A_SEL + GR * STEPS
A_SUM = A_F + 4 * Q
A_DG = A_SUM + H * STEPS
A_OH = A_DG + Q
A_EV = A_OH + 2 * (P // 2 + KW)
A_BIG = A_EV + 2 * KW
A_W0 = A_BIG
A_XT0 = A_W0 + 2 * R8 * D
A_FS = A_XT0 + 2 * NP
A_IE = A_DG
A_RING = A_BIG
A_KRB = A_RING + 2 * GB * FW
A_OHT = A_KRB + 2 * CK * P // 2
A_ERW = A_OHT + 2 * CK * P // 2
A_ERS = A_ERW + WINS * 3 * H // 2
A_ET = A_KRB
A_SELT = A_ET + 2 * 4 * P
A_S = A_BIG
A_FA = A_S + H * Q
A_BA = A_FA + H * Q
A_FL = A_BA + H * Q
A_ROW = A_FL + 4 * Q
A_FB = A_BIG
A_WOH = A_FB + FR * D
A_ACC = A_WOH + 4 * 64
A_X = 0
A_XT = A_X + 2 * NP
A_B1 = A_XT + 2 * NP
A_B2 = A_B1 + NT * (D + 2 * H)
A_CH = A_B2 + 2 * NP
A_WT = A_CH + 2 * NW
A_BI = A_WT + 3200
A_END = A_BI + 4 * D
assert A_ACC + WINS * 64 <= A_BI and A_ROW + 5 * Q <= A_END and A_ERS + STEPS * H <= A_END


def build(nc, rec, x, xT, edge0, w0, a0l, a0r, cols, wrel, brow, wih, w1, w2, w3, b3, wp1, bp1, wl1, bl1, wr1, wp2, bp2, wl2, bl2, wr2,
          wt3, a3l, a3r, out):
    ctx = ExitStack()
    with ctx:
        sb = lambda n, s, d: ctx.enter_context(nc.sbuf_tensor(n, s, d))
        sem = lambda n: ctx.enter_context(nc.semaphore(n))

        feat_t = nc.dram_tensor("feat_table", (NP * R8, FW), F32).ap()
        rows_t = nc.dram_tensor("edge_rows", (TILES * P, D), F32).ap()
        key_t = nc.dram_tensor("step_keys", (SC * P, P), F16).ap()
        er_t = nc.dram_tensor("er_table", (NP * R8, H), F32).ap()
        xt_t = nc.dram_tensor("xt_table", (NP, D + 2 * H), F32).ap()
        sorted_t = nc.dram_tensor("sorted_records", (EP, 4), I32).ap()
        al_t = nc.dram_tensor("al_table", (NP, H), F32).ap()

        AR = sb("arena", [P, A_END], F32)
        ADJ = sb("adjacency", [P, R2, NW * SH], U16)
        ident = sb("ident", [P, P], F32)
        ones = sb("ones", [P, P], F32)
        ones16 = sb("ones16", [P, P], F16)
        iota128 = sb("iota128", [P, P], F16)
        iota480 = sb("iota480", [P, R2 * KW], F16)
        iota16 = sb("iota16", [P, WIN], F32)
        pcol = sb("pcol", [P, GR], F32)
        w16col = sb("w16col", [P, 1], F32)
        cnt = sb("cnt", [P, 2], F32)
        GI = sb("gather_idx", [P, 2, GB], I32)
        TCOL = sb("step_tile", [P, SC], F32)
        BC = sb("bias_cols", [P, 32], F32)
        ST = sb("ln_stats", [P, NT, 6], F32)
        MV = sb("ln_mean_var", [P, NT, 2], F32)
        RS = sb("ln_rstd", [P, NT], F32)
        RC = sb("recip_count", [P, NT], F32)
        E3 = sb("edge_ends", [P, 2, NT], I32)
        S3 = sb("scores3", [P, 3, NT * H], F32)
        SC16 = sb("edge_cols", [P, 2, H * GR], F32)
        SCOL = sb("step_times_128", [P, SC], F32)
        NXT = sb("next_tile", [P, GR, 4], I32)
        FLG = sb("unsorted_flag", [P, 1], I32)
        FLF = sb("unsorted_count", [P, 3], F32)
        RD = sb("lane_ends", [P, 2, GR * H], F32)
        PS = [ctx.enter_context(nc.psum_tensor(f"bank{i}", [P, 512], F32)) for i in range(8)]

        def ar(off, *dims, dt=None):
            n = 1
            for d in dims:
                n *= d
            v = AR[:, off:off + n]
            if len(dims) == 2:
                v = v.rearrange("p (a b) -> p a b", b=dims[1])
            elif len(dims) == 3:
                v = v.rearrange("p (a b c) -> p a b c", b=dims[1], c=dims[2])
            return v

        EARLY = ADJ[:, :, :].rearrange("p r k -> p (r k)").bitcast(F32)
        RL = EARLY[:, 0:4 * Q].bitcast(I32)
        RLv = RL.rearrange("p (n f) -> p n f", f=4)
        LI = EARLY[:, 4 * Q:5 * Q].bitcast(I32)
        LJ = EARLY[:, 5 * Q:6 * Q].bitcast(I32)
        IDd = EARLY[:, 6 * Q:7 * Q]
        IDm = EARLY[:, 7 * Q:8 * Q]
        AT = EARLY[:, 8 * Q:8 * Q + 4 * Q * 2].rearrange("p (a n) -> p a n", a=2)
        TMP = EARLY[:, 16 * Q:20 * Q]
        VL = EARLY[:, 20 * Q:20 * Q + 128].rearrange("p (k n) -> p k n", k=2)
        ELS = EARLY[:, 21 * Q:21 * Q + NT * 64].rearrange("p (t n) -> p t n", n=64)

        SB0 = 24 * Q
        DT = EARLY[:, SB0:SB0 + Q]
        DLO, DHI = EARLY[:, SB0 + Q:SB0 + 2 * Q], EARLY[:, SB0 + 2 * Q:SB0 + 3 * Q]
        RT = EARLY[:, SB0 + 3 * Q:SB0 + 7 * Q].bitcast(I32)
        LD = EARLY[:, SB0 + 7 * Q:SB0 + 8 * Q]
        OL, OLT, DGc, TRI, TRIT, JNK = (EARLY[:, SB0 + 8 * Q + P * j:SB0 + 8 * Q + P * (j + 1)] for j in range(6))
        JNK4 = EARLY[:, SB0 + 11 * Q:SB0 + 12 * Q]
        HI16 = EARLY[:, SB0 + 10 * Q:SB0 + 10 * Q + 16]
        CUR = EARLY[:, SB0 + 10 * Q + 16:SB0 + 10 * Q + 32]
        TOT = EARLY[:, SB0 + 10 * Q + 32:SB0 + 10 * Q + 48]
        RNK = EARLY[:, SB0 + 10 * Q + 48:SB0 + 10 * Q + 52]
        POS = EARLY[:, SB0 + 10 * Q + 52:SB0 + 10 * Q + 53].bitcast(I32)
        RS4 = EARLY[:, SB0 + 10 * Q + 56:SB0 + 10 * Q + 60].bitcast(I32)
        NTL = GR * P

        SLO, KEY, DJ, IDX, WS, IOT = (ar(o, STEPS) for o in (A_SLO, A_KEY, A_DJ, A_IDX, A_WS, A_IOT))
        OFF = ar(A_WI, STEPS).bitcast(I32)
        SEL = ar(A_SEL, GR, STEPS)
        Fl = ar(A_F, 4, Q)
        DST = Fl[:, 2, :].rearrange("p (g e) -> p g e", g=GR)
        SUM = ar(A_SUM, Q, H)
        ALS = ar(A_SUM, STEPS, H)
        DG = EARLY[:, 43 * Q:44 * Q]
        LKEY = EARLY[:, 44 * Q:44 * Q + GR * (P + 1)].rearrange("p (g e) -> p g e", g=GR)
        KEY16 = EARLY[:, 47 * Q:47 * Q + SC * P // 2].bitcast(F16).rearrange("p (c e) -> p c e", e=P)
        ERF = EARLY[:, 48 * Q:48 * Q + WINS * H].rearrange("p (w h) -> p w h", h=H)
        ERG = EARLY[:, 49 * Q:49 * Q + WINS * H].rearrange("p (w h) -> p w h", h=H)
        TI = ar(A_IDX, STEPS).bitcast(I32)
        OHS = [AR[:, A_OH + k * (P // 2 + KW):A_OH + k * (P // 2 + KW) + P // 2].bitcast(F16) for k in range(2)]
        OHK = [AR[:, A_OH + k * (P // 2 + KW) + P // 2:A_OH + (k + 1) * (P // 2 + KW)].bitcast(F16) for k in range(2)]
        EV = [AR[:, A_EV + k * KW:A_EV + (k + 1) * KW].bitcast(U16).rearrange("p (r k) -> p r k", r=R2) for k in range(2)]
        W0 = ar(A_W0, 2, R8 * D)
        XT0 = ar(A_XT0, 2, NP)
        FS = ar(A_FS, 4, 512)
        IE = ar(A_IE, Q)
        RING = ar(A_RING, 2 * GB, FW)
        KRB = [AR[:, A_KRB + k * CK * P // 2:A_KRB + (k + 1) * CK * P // 2].bitcast(F16) for k in range(2)]
        OHT = [AR[:, A_OHT + k * CK * P // 2:A_OHT + (k + 1) * CK * P // 2].bitcast(F16) for k in range(2)]
        ERW = AR[:, A_ERW:A_ERS].bitcast(BF16)
        ERWv = ERW.rearrange("p (w q h) -> p w q h", q=3, h=H)
        ERS, ERSf = ar(A_ERS, STEPS, H), ar(A_ERS, STEPS * H)
        ET, SELT = ar(A_ET, 2, 4 * P), ar(A_SELT, 2, 4 * P)
        S, FA, BA = ar(A_S, H, Q), ar(A_FA, H, Q), ar(A_BA, H, Q)
        FL = ar(A_FL, 4, Q)
        ROW = ar(A_ROW, 5, Q)
        FB = ar(A_FB, FR, D)
        WOH = ar(A_WOH, 4, 64)
        ACC = ar(A_ACC, WINS, 64)
        ACCf = ar(A_ACC, WINS * 64)
        ALSf = ar(A_SUM, STEPS * H)
        X, XT = ar(A_X, NT, D), ar(A_XT, 2, NP)
        B1, B2 = ar(A_B1, NT, D), ar(A_B2, NT, D)
        M1, M2 = B1, B2
        XT3 = ar(A_B1, NT, D + 2 * H)
        G3 = ar(A_B2, NT, D + 2 * H)
        AG3 = ar(A_B2 + NT * (D + 2 * H), NT, H)
        T64 = ar(A_XT, NT, HD)
        B2T = ar(A_B2, 2, NP)
        CH = ar(A_CH, 2, NW)
        HC = [ar(A_CH + k * 2 * CN, 2, CN) for k in range(2)]
        WREL = ar(A_WT, 2 * R2, D).rearrange("p (k r) n -> p k r n", k=2)
        WIH = ar(A_WT + 1024, 2, 3 * D)
        W1s, W2s, W3s = ar(A_WT + 2560, 2, P), ar(A_WT + 2816, P), ar(A_WT + 2944, D)
        W2L = [ar(A_WT + 512 * i, 2, D) for i in range(6)]
        WT3 = ar(A_WT, 2, D + 2 * H)
        A3 = ar(A_WT + 528, 2, D)
        TMP3 = ar(A_WT + 1040, D)
        BROW = ar(A_BI, 4, D)
        GT = ar(A_B1, 6, CN)
        CC, HN, X1, X2 = ar(A_B1 + 6 * CN, 2, CN), ar(A_B1 + 8 * CN, 2, CN), ar(A_B1 + 10 * CN, CN), ar(A_B1 + 11 * CN, CN)

        names = """ld_rec ld_w0 ld_xt ld_at ld_e3 consts fields idx_mm idx_ev vl_done tab_mm tab_ev tab_st
            feat_mm feat_ev diag_done bc_mm cmp_done ws_mm sel_ready fld_mm fld_ev steps_done
            a_oh a_mm a_ev a_add pool_link sum_done lane_in lane_mm lane_ev flags_in flags_mm
            tail_ready tail_mm cin_ready cin_mm exp_ready exp_done alpha_ready als_mm als_ev 
            r_all off_acc l_woh l_mm l_acc ld_x ld_bc ld_wt1 ht_ready ht_mm ht_add var_ready std_ready ln_done xt_mm
            xt_eva xt_evd h_mm h_ev m_mm m_ev chunk_ready chunk_used agg_eva agg_evd gate_mm gate_ev
            c_ready tc_ready hn_ready x1_mm x1_ev x2_mm x2_ev x3_mm x3_add ld_wt2 ld_wt3 p_mm p_ev
            cnt_acc cnt_mm cnt_ev o_mm o_ev o_ready sq_done nrm_done h_ready pool_gate vl3_done t_mm t_ev t_st
            key_mm key_ev key_st er_st er_ld erw_ready kr_used oht er_mm er_red et_mm et_ev selt sc_mm tiles_ready flag_cmp flag_mm flag_ready srt_oh srt_hist srt_add srt_pre srt_pmm srt_a srt_b srt_c srt_d srt_e srt_put srt_link srt_in srt_t srt_tv ld_sorted g3 s3_ready s3_exp out_st dve_link""".split()
        s = {n: sem(n) for n in names}
        fs_st = [sem(f"feat_stored{i}") for i in range(4)]
        g_done = [sem(f"scores_gathered{i}") for i in range(2)]
        f_done = [sem(f"rows_loaded{i}") for i in range(FR)]
        r_st = [sem(f"rows_stored{i}") for i in range(2)]
        k_ld = [sem(f"keys_loaded{i}") for i in range(2)]

        def offsets(engine, step, n, most):
            return nc.values_load_multi_w_load_instructions(
                (TI if engine == SP else OFF)[0:1, bass.ds(step, n)],
                engines=[engine], min_val=0, max_val=most,
                skip_runtime_bounds_check_because="window and tile numbers of the walk stay in range for any sorted edges")[1]

        block = ctx.enter_context(nc.Block())

        @block.sync
        def _(sp):
            sp.dma_start(RL.rearrange("p (g n) -> p g n", g=GR),
                         rec[0:EP, :].rearrange("(g t e) f -> t g (e f)", g=GR, t=P)).then_inc(s["ld_rec"], 16)
            sp.dma_start(NXT[:, :, :], rec[P:P + EP, :].rearrange("(g t e) f -> t g e f", g=GR, t=P)[:, :, 0, :])\
              .then_inc(s["ld_rec"], 16)
            sp.dma_start(W0, w0.rearrange("(k p) n -> p k n", k=2)).then_inc(s["ld_w0"], 16)
            sp.dma_start(AT[:, 0, :], a0l.broadcast_to([P, R8 * D])).then_inc(s["ld_at"], 16)
            sp.dma_start(AT[:, 1, :], a0r.broadcast_to([P, R8 * D])).then_inc(s["ld_at"], 16)
            sp.dma_start(XT0, xT.rearrange("(k p) n -> p k n", k=2)).then_inc(s["ld_xt"], 16)
            sp.dma_start(E3[:, :, :], edge0).then_inc(s["ld_e3"], 16)
            sp.dma_start(BC[:, 0:20], cols).then_inc(s["ld_bc"], 16)
            sp.wait_ge(s["flag_ready"], 1)
            unsorted = sp.value_load(FLG[0:1, 0:1], min_val=0, max_val=EP)
            with sp.If(unsorted >= 1):
                sp.dma_start(RT.rearrange("p (t f) -> p t f", f=4),
                             rec[0:EP, :].rearrange("(t e) f -> e t f", e=P)).then_inc(s["srt_in"], 16)
            ftr = feat_t.rearrange("(t p r) d -> t p r d", p=P, r=R8)

            def store_scores():
                sp.wait_ge(s["tab_ev"], 2)
                sp.dma_start(er_t.rearrange("(t p r) h -> p t (r h)", p=P, r=R8), ELS[:, :, 32:64]).then_inc(s["er_st"], 16)
                for t in range(NT):
                    sp.dma_start(ftr[t, :, :, D:FW], ELS[:, t, 0:32].rearrange("p (r h) -> p r h", h=H)).then_inc(s["tab_st"], 16)

            for i in range(NT * 4):
                if i == TABS_AT - 2:
                    store_scores()
                sp.wait_ge(s["feat_ev"], i + 1)
                c = i % 4
                sp.dma_start(ftr[i // 4, :, 2 * c:2 * c + 2, 0:D], FS[:, c, :].rearrange("p (r d) -> p r d", d=D))\
                  .then_inc(fs_st[c], 16)
            rows_b = rows_t.rearrange("(t p) d -> p t d", p=P)

            def store(k, tiles):
                sp.dma_start(rows_b[:, tiles, :], RING[:, GB * k:GB * (k + 1), 0:D]).then_inc(r_st[k], 16)

            with sp.Fori(0, (NGB - 1) // 2) as i:
                for k in range(2):
                    sp.wait_ge(g_done[k], i * BATCH + BATCH)
                    store(k, bass.ds(i * (2 * GB) + GB * k, GB))
            sp.wait_ge(g_done[0], ((NGB - 1) // 2 + 1) * BATCH)
            store(0, slice(GB * (NGB - 1), TILES))
            for k in range(2):
                sp.wait_ge(r_st[k], 16 * ((NGB + 1 - k) // 2))
            sp.wait_ge(s["l_acc"], 1)

            def load(slot, first_edge):
                sp.dma_start(FB[:, slot, :], rows_t[bass.ds(first_edge, P), :]).then_inc(f_done[slot], 16)

            edges = offsets(SP, 0, HEAD + FR, (TILES - 1) * P)
            for st in range(HEAD + FR):
                if st >= FR:
                    sp.wait_ge(s["l_mm"], st - FR + 1)
                load(st % FR, edges[st])
            with sp.Fori(0, (GRPS - 1) // 2) as i:
                edges = offsets(SP, i * (2 * FR) + (HEAD + FR), 2 * FR, (TILES - 1) * P)
                for u in range(2 * FR):
                    st = HEAD + FR + u
                    sp.wait_ge(s["l_mm"], i * (2 * FR) + (st - FR + 1))
                    load(st % FR, edges[u])
            sp.wait_ge(s["l_acc"], STEPS + 1)
            sp.wait_ge(s["ht_ready"], 1)
            sp.dma_start(X[:, 0:NT - 1, :], x[0:(NT - 1) * P, :].rearrange("(t p) d -> p t d", p=P)).then_inc(s["ld_x"], 16)
            sp.dma_start(X[0:NLAST, NT - 1, :], x[(NT - 1) * P:N, :]).then_inc(s["ld_x"], 16)
            for r in range(R2):
                sp.dma_start(WREL[:, :, r, :], wrel[r, :, :].rearrange("(k p) n -> p k n", k=2)).then_inc(s["ld_wt1"], 16)
            sp.dma_start(WIH, wih.rearrange("(k p) n -> p k n", k=2)).then_inc(s["ld_wt1"], 16)
            sp.dma_start(W1s, w1.rearrange("(k p) n -> p k n", k=2)).then_inc(s["ld_wt1"], 16)
            sp.dma_start(W2s, w2).then_inc(s["ld_wt1"], 16)
            sp.dma_start(W3s, w3).then_inc(s["ld_wt1"], 16)
            for i, b in enumerate((brow[0:1, :], brow[1:2, :], b3)):
                sp.dma_start(BROW[0:1, i, :], b).then_inc(s["ld_wt1"], 16)
            sp.wait_ge(s["x3_mm"], NC)
            for i, w in enumerate((wp1, wl1, wr1, wp2, wl2, wr2)):
                sp.dma_start(W2L[i], w.rearrange("(k p) n -> p k n", k=2)).then_inc(s["ld_wt2"], 16)
            for i, b in enumerate((bp1, bl1, bp2, bl2)):
                sp.dma_start(BROW[0:1, i, :], b).then_inc(s["ld_wt2"], 16)
            sp.wait_ge(s["o_mm"], 2 * NT)
            sp.dma_start(WT3[:, :, 0:D], wt3.rearrange("(k p) n -> p k n", k=2)).then_inc(s["ld_wt3"], 16)
            sp.dma_start(A3[:, 0, :], a3l.broadcast_to([P, D])).then_inc(s["ld_wt3"], 16)
            sp.dma_start(A3[:, 1, :], a3r.broadcast_to([P, D])).then_inc(s["ld_wt3"], 16)
            sp.wait_ge(s["t_ev"], NT)
            sp.dma_start(xt_t.rearrange("(t p) n -> p t n", p=P), XT3).then_inc(s["t_st"], 16)
            sp.dma_start(al_t.rearrange("(t p) n -> p t n", p=P), XT3[:, :, D:D + H]).then_inc(s["t_st"], 16)
            sp.wait_ge(s["ln_done"], 4)
            sp.dma_start(out[0:(NT - 1) * P, :].rearrange("(t p) d -> p t d", p=P), X[:, 0:NT - 1, :]).then_inc(s["out_st"], 16)
            sp.dma_start(out[(NT - 1) * P:N, :], X[0:NLAST, NT - 1, :]).then_inc(s["out_st"], 16)
            sp.wait_ge(s["out_st"], 32)

        @block.gpsimd
        def _(pool):
            g = nc.gpsimd
            g.memset(ident[:, :], 0.0).then_inc(s["pool_link"], 1)
            g.memset(ones[:, :], 1.0)
            g.memset(ones16[:, :], 1.0)
            pool.wait_ge(s["pool_link"], 1)
            g.affine_select(out=ident[:, :], in_=ident[:, :], compare_op=ALU.not_equal, fill=1.0, base=0,
                            pattern=[[-1, P]], channel_multiplier=1)
            g.iota(iota128[:, :], pattern=[[1, P]], base=0, channel_multiplier=0, allow_small_or_imprecise_dtypes=True)
            g.iota(iota480[:, :], pattern=[[1, R2 * KW]], base=0, channel_multiplier=0, allow_small_or_imprecise_dtypes=True)
            g.iota(iota16[:, :], pattern=[[1, WIN]], base=0, channel_multiplier=0, allow_small_or_imprecise_dtypes=True)
            g.iota(IOT, pattern=[[1, STEPS]], base=0, channel_multiplier=0, allow_small_or_imprecise_dtypes=True)
            g.iota(pcol[:, :], pattern=[[P, GR]], base=0, channel_multiplier=1, allow_small_or_imprecise_dtypes=True)
            g.iota(w16col[:, :], pattern=[[0, 1]], base=0, channel_multiplier=WIN, allow_small_or_imprecise_dtypes=True)\
             .then_inc(s["consts"], 1)

            pool.wait_ge(s["flag_ready"], 1)
            unsorted = pool.value_load(FLG[0:1, 0:1], min_val=0, max_val=EP)
            with pool.If(unsorted >= 1):
                g.memset(TRI, 1.0).then_inc(s["srt_t"], 1)
                g.memset(TRIT, 1.0).then_inc(s["srt_t"], 1)
                pool.wait_ge(s["srt_t"], 2)
                g.affine_select(out=TRI, in_=TRI, compare_op=ALU.is_gt, fill=0.0, base=0,
                                pattern=[[-1, P]], channel_multiplier=1)
                g.affine_select(out=TRIT, in_=TRIT, compare_op=ALU.is_gt, fill=0.0, base=0,
                                pattern=[[1, P]], channel_multiplier=-1).then_inc(s["srt_tv"], 1)
                with pool.Fori(0, NTL) as i:
                    pool.wait_ge(s["srt_e"], i + 1)
                    pool.sem_inc(s["pool_gate"], 1)
                    g.indirect_dma_start(out=sorted_t, out_offset=bass.IndirectOffsetOnAxis(ap=POS, axis=0),
                                         in_=RS4, in_offset=None).then_inc(s["srt_put"], 16)
                pool.wait_ge(s["srt_put"], 16 * NTL)
                pool.dma_start(RL.rearrange("p (g n) -> p g n", g=GR),
                               sorted_t.rearrange("(g t e) f -> t g (e f)", g=GR, t=P)).then_inc(s["ld_sorted"], 16)

            pool.wait_ge(s["er_st"], 16)
            pool.dma_start(ERF, er_t[0:NW * R8, :].rearrange("(w c) h -> c w h", c=P)).then_inc(s["er_ld"], 16)
            pool.wait_ge(s["key_ev"], SC)
            pool.dma_start(key_t.rearrange("(c p) e -> p c e", p=P), KEY16).then_inc(s["key_st"], 16)

            def issue(k, cols):
                g.tensor_copy(GI[:, k, :], IE[:, cols]).then_inc(s["pool_link"], 1)

            def gathers(k):
                for j in range(GB):
                    g.indirect_dma_start(out=RING[:, GB * k + j, :], out_offset=None, in_=feat_t,
                                         in_offset=bass.IndirectOffsetOnAxis(ap=GI[:, k, j:j + 1], axis=0))\
                     .then_inc(g_done[k], 16)

            def collect(k, cols):
                g.tensor_copy(SUM[:, cols, :], RING[:, GB * k:GB * (k + 1), D:FW]).then_inc(s["pool_link"], 1)

            g.memset(SUM[:, TILES:Q, :], 0.0).then_inc(s["pool_link"], 1)
            pool.wait_ge(s["idx_ev"], 1)
            pool.wait_ge(s["tab_st"], 16 * NT)
            for i in range(4):
                pool.wait_ge(fs_st[i], NT * 16)
            for b in range(2):
                issue(b, slice(GB * b, GB * (b + 1)))
                pool.wait_ge(s["pool_link"], 3 + b)
                gathers(b)
            with pool.Fori(0, N_IT) as i:
                for k in range(2):
                    pool.wait_ge(g_done[k], i * BATCH + BATCH)
                    pool.sem_inc(s["pool_gate"], 1)
                    collect(k, bass.ds(i * (2 * GB) + GB * k, GB))
                    issue(k, bass.ds(i * (2 * GB) + GB * (k + 2), GB))
                    pool.wait_ge(r_st[k], i * 16 + 16)
                    pool.sem_inc(s["pool_gate"], 1)
                    pool.wait_ge(s["pool_link"], i * 4 + (6 + 2 * k))
                    pool.sem_inc(s["pool_gate"], 1)
                    gathers(k)
            last = NGB - 1
            pool.wait_ge(g_done[0], (N_IT + 1) * BATCH)
            collect(0, slice(GB * (last - 2), GB * (last - 1)))
            issue(0, slice(GB * last, GB * NGB))
            pool.wait_ge(r_st[0], 16 * (N_IT + 1))
            pool.wait_ge(s["pool_link"], LINKS - 2)
            gathers(0)
            pool.wait_ge(g_done[1], (N_IT + 1) * BATCH)
            collect(1, slice(GB * (last - 1), GB * last))
            pool.wait_ge(g_done[0], (N_IT + 2) * BATCH)
            collect(0, slice(GB * last, GB * NGB))

            CNTS = B2T[:, 0, 0:NW]
            for c in range(SH):
                pool.wait_ge(s["chunk_ready"], R2 * SH + c + 1)
                if c:
                    pool.wait_ge(s["cnt_acc"], c)
                if c == 0:
                    g.tensor_copy(CNTS, CH[:, 0, :]).then_inc(s["cnt_acc"], 1)
                else:
                    g.tensor_tensor(CNTS, CNTS, CH[:, c % 2, :], ALU.add).then_inc(s["cnt_acc"], 1)

            pool.wait_ge(s["ld_e3"], 16)
            pool.wait_ge(s["t_st"], 32)
            for t in range(NT):
                g.indirect_dma_start(out=AG3[:, t, :], out_offset=None, in_=al_t,
                                     in_offset=bass.IndirectOffsetOnAxis(ap=E3[:, 0, t:t + 1], axis=0)).then_inc(s["g3"], 16)
                g.indirect_dma_start(out=G3[:, t, :], out_offset=None, in_=xt_t,
                                     in_offset=bass.IndirectOffsetOnAxis(ap=E3[:, 1, t:t + 1], axis=0)).then_inc(s["g3"], 16)

        @block.scalar
        def _(act):
            a = nc.scalar
            for i in range(NT * 4):
                act.wait_ge(s["feat_mm"], i + 1)
                if i >= 4:
                    act.wait_ge(fs_st[i % 4], 16 * (i // 4))
                a.activation(FS[:, i % 4, :], PS[i % 4][:, :], ACT.Copy).then_inc(s["feat_ev"], 1)
            for i in range(4):
                act.wait_ge(fs_st[i], NT * 16)
            act.wait_ge(s["feat_mm"], NT * 4)
            act.wait_ge(s["key_st"], 16)
            key_row = key_t.rearrange("(a s) e -> a (s e)", a=1)

            def load_keys(k, at, n):
                act.dma_start(KRB[k][:, 0:n * P], key_row[:, bass.ds(at * P, n * P)].broadcast_to([P, n * P])).then_inc(k_ld[k], 16)

            for k in range(2):
                load_keys(k, CK * k, CK)
            with act.Fori(0, (NCK - 2) // 2) as i:
                for k in range(2):
                    act.wait_ge(s["oht"], i * 2 + (1 + k))
                    load_keys(k, i * (2 * CK) + CK * (2 + k), CK)
            act.wait_ge(s["oht"], NCK - 1)
            load_keys(0, CK * NCK, CTAIL)
            for c in range(SC):
                act.wait_ge(s["et_mm"], c + 1)
                if c >= 2:
                    act.wait_ge(s["sc_mm"], c - 1)
                n = min(P, STEPS - P * c)
                a.activation(ET[0:n, c % 2, :], PS[4 + c % 2][0:n, :], ACT.Copy).then_inc(s["et_ev"], 1)
            def a_evac(k):
                a.activation(EV[k].rearrange("p r k -> p (r k)"), PS[6 + k][:, 0:R2 * KW], ACT.Copy).then_inc(s["a_ev"], 1)
            for k in range(2):
                act.wait_ge(s["a_mm"], k + 1)
                a_evac(k)
            with act.Fori(0, (STEPS - 2) // AU) as i:
                for u in range(AU):
                    act.wait_ge(s["a_mm"], i * AU + (3 + u))
                    act.wait_ge(s["a_add"], i * AU + (2 + u))
                    a_evac(u % 2)
            act.wait_ge(s["r_all"], 1)
            for g in range(GR):
                act.wait_ge(s["lane_mm"], g + 1)
                a.activation(S[:, :, P * g:P * (g + 1)], PS[g][:, :].rearrange("p (h e) -> p h e", h=H), ACT.Copy)\
                 .then_inc(s["lane_ev"], 1)
            act.wait_ge(s["exp_ready"], 1)
            a.activation(S.rearrange("p h n -> p (h n)"), S.rearrange("p h n -> p (h n)"), ACT.Exp).then_inc(s["exp_done"], 1)
            for h in range(H):
                act.wait_ge(s["als_mm"], h + 1)
                a.activation(ALS[:, 0:512, h], PS[2 * h][:, 0:512], ACT.Copy)
                a.activation(ALS[:, 512:STEPS, h], PS[2 * h + 1][:, 0:STEPS - 512], ACT.Copy).then_inc(s["als_ev"], 1)
            def ln_sqrt(n):
                act.wait_ge(s["var_ready"], n)
                a.activation(RS[:, :], MV[:, :, 1], ACT.Sqrt).then_inc(s["std_ready"], 1)

            def xt_evac(n):
                for q in range(4):
                    act.wait_ge(s["xt_mm"], 8 * n + 2 * q + 1)
                    w = min(512, NP - 512 * q)
                    a.activation(XT[:, 0, 512 * q:512 * q + w], PS[2 * q][:, 0:w], ACT.Copy).then_inc(s["xt_eva"], 1)

            ln_sqrt(1)
            xt_evac(0)
            act.wait_ge(s["ld_bc"], 16)
            for i in range(R2 * NC):
                r = i // NC
                if i >= 2:
                    act.wait_ge(s["m_mm"], 3 * (i - 1))
                for fo in range(2):
                    act.wait_ge(s["h_mm"], 2 * i + fo + 1)
                    a.activation(HC[i % 2][:, fo, :], PS[2 * (i % 2) + fo][:, 0:CN], ACT.Relu,
                                 bias=BC[:, 2 + 2 * r + fo:3 + 2 * r + fo]).then_inc(s["h_ev"], 1)
            act.wait_ge(s["m_mm"], 3 * R2 * NC)
            for c in range(R2 * SH):
                r, sh = c // SH, c % SH
                if c >= 2:
                    act.wait_ge(s["chunk_used"], c - 1)
                a.activation(CH[:, c % 2, :], ADJ[:, r, :].rearrange("p (n s) -> p n s", s=SH)[:, :, sh], ACT.Copy)\
                 .then_inc(s["chunk_ready"], 1)

            def agg_evac(dst, total):
                act.wait_ge(s["chunk_used"], total)
                for j in range(4):
                    a.activation(dst[:, 1, CW * j:CW * (j + 1)], PS[4 + j][:, 0:CW], ACT.Copy).then_inc(s["agg_eva"], 1)

            agg_evac(XT, R2 * SH)
            funcs = (ACT.Sigmoid, ACT.Sigmoid, ACT.Tanh, ACT.Tanh, ACT.Sigmoid, ACT.Sigmoid)
            for c in range(NC):
                for j in range(6):
                    act.wait_ge(s["gate_mm"], 6 * c + j + 1)
                    if j == 0 and c:
                        act.wait_ge(s["hn_ready"], c)
                    a.activation(GT[:, j, :], PS[j][:, 0:CN], funcs[j], bias=BC[:, 20 + j:21 + j]).then_inc(s["gate_ev"], 1)
                act.wait_ge(s["c_ready"], c + 1)
                a.activation(CC, CC, ACT.Tanh).then_inc(s["tc_ready"], 1)
                act.wait_ge(s["x1_mm"], c + 1)
                a.activation(X1, PS[6][:, 0:CN], ACT.Relu, bias=BC[:, 18:19]).then_inc(s["x1_ev"], 1)
                act.wait_ge(s["x2_mm"], c + 1)
                a.activation(X2, PS[7][:, 0:CN], ACT.Relu, bias=BC[:, 19:20]).then_inc(s["x2_ev"], 1)
            ln_sqrt(2)
            xt_evac(1)
            for v in range(2):
                for t in range(NT):
                    act.wait_ge(s["p_mm"], NT * v + t + 1)
                    a.activation(M1[:, t, :], PS[t % 4][:, 0:D], ACT.Relu).then_inc(s["p_ev"], 1)
                agg_evac(B2T, (R2 + 1 + v) * SH)
                act.wait_ge(s["o_ready"], NT * (v + 1))
                a.activation(RS[:, :], RS[:, :], ACT.Sqrt).then_inc(s["nrm_done"], 1)
                if v == 0:
                    xt_evac(2)
            ln_sqrt(3)
            xt_evac(3)
            for t in range(NT):
                act.wait_ge(s["t_mm"], t + 1)
                a.activation(XT3[:, t, :], PS[t % 4][:, 0:D + 2 * H], ACT.Copy).then_inc(s["t_ev"], 1)
            act.wait_ge(s["s3_ready"], 1)
            a.activation(S3[:, 0, :], S3[:, 0, :], ACT.Exp).then_inc(s["s3_exp"], 1)
            ln_sqrt(4)

        @block.vector
        def _(dve):
            v = nc.vector
            chain = [0]

            def link(ins):
                chain[0] += 1
                ins.then_inc(s["dve_link"], 1)
                dve.wait_ge(s["dve_link"], chain[0])

            LDv = LD.rearrange("p (g e) -> p g e", g=GR)
            LIf = EARLY[:, 7 * Q:8 * Q].rearrange("p (g e) -> p g e", g=GR)

            def sort_records():
                n = [0]

                def slink(ins):
                    n[0] += 1
                    ins.then_inc(s["srt_link"], 1)
                    dve.wait_ge(s["srt_link"], n[0])

                v.tensor_copy(DT[:, 0:1], FLF[:, 0:1]).then_inc(s["srt_a"], 1)
                dve.wait_ge(s["srt_pre"], 1)
                slink(v.tensor_copy(DT, PS[1][:, :]))
                DTi = JNK4.bitcast(I32)
                slink(v.tensor_copy(DTi, DT))
                slink(v.tensor_single_scalar(LI, DTi, P - 1, ALU.bitwise_and))
                slink(v.tensor_single_scalar(LJ, DTi, 7, ALU.arith_shift_right))
                v.tensor_copy(DLO, LI)
                slink(v.tensor_copy(DHI, LJ))
                slink(v.memset(CUR, 0.0))
                dve.wait_ge(s["consts"], 1)
                with dve.Fori(0, NTL) as i:
                    v.tensor_scalar(OL, iota128[:, :], DLO[:, bass.ds(i, 1)], None, ALU.is_equal)
                    v.tensor_scalar(HI16, iota16[:, :], DHI[:, bass.ds(i, 1)], None, ALU.is_equal).then_inc(s["srt_oh"], 1)
                    dve.wait_ge(s["srt_hist"], i + 1)
                    v.tensor_tensor(CUR, CUR, PS[3][:, 0:16], ALU.add).then_inc(s["srt_add"], 1)
                    dve.wait_ge(s["srt_add"], i + 1)
                v.tensor_copy(TOT, CUR).then_inc(s["srt_pmm"], 1)
                dve.wait_ge(s["srt_pre"], 2)
                slink(v.tensor_copy(TOT, PS[1][:, 0:16]))
                slink(v.memset(JNK[:, 0:16], 1.0))
                slink(v.tensor_tensor_scan(JNK[:, 16:32], JNK[:, 0:16], TOT, 0.0, ALU.mult, ALU.add))
                slink(v.tensor_tensor(JNK[:, 16:32], JNK[:, 16:32], TOT, ALU.subtract))
                slink(v.tensor_tensor(CUR, JNK[:, 16:32], PS[2][:, 0:16], ALU.add))
                dve.wait_ge(s["srt_in"], 16)
                dve.wait_ge(s["srt_tv"], 1)
                K = 3
                base = n[0]
                with dve.Fori(0, NTL) as i:
                    col = bass.ds(i, 1)
                    v.tensor_scalar(OL, iota128[:, :], DLO[:, col], None, ALU.is_equal)
                    v.tensor_scalar(HI16, iota16[:, :], DHI[:, col], None, ALU.is_equal)
                    v.tensor_scalar(DGc, ident[:, :], DT[:, col], None, ALU.mult).then_inc(s["srt_oh"], 1)
                    dve.wait_ge(s["srt_b"], i + 1)
                    v.tensor_copy(OLT, PS[2][:, 0:P]).then_inc(s["srt_c"], 1)
                    v.tensor_scalar(JNK, PS[1][:, 0:P], DT[:, col], None, ALU.is_equal).then_inc(s["srt_link"], 1)
                    dve.wait_ge(s["srt_link"], i * K + (base + 1))
                    v.tensor_tensor(JNK, JNK, TRI, ALU.mult).then_inc(s["srt_link"], 1)
                    dve.wait_ge(s["srt_link"], i * K + (base + 2))
                    v.tensor_reduce(RNK[:, 0:1], JNK, AX.X, ALU.add)
                    dve.wait_ge(s["srt_d"], i + 1)
                    v.tensor_tensor(JNK4[:, 0:16], PS[0][:, 0:16], HI16, ALU.mult).then_inc(s["srt_link"], 1)
                    dve.wait_ge(s["srt_link"], i * K + (base + 3))
                    v.tensor_reduce(RNK[:, 1:2], JNK4[:, 0:16], AX.X, ALU.add).then_inc(s["srt_add"], 1)
                    dve.wait_ge(s["srt_add"], i * 2 + (NTL + 1))
                    v.tensor_copy(RS4, RT[:, bass.ds(i * 4, 4)])
                    v.tensor_tensor(POS, RNK[:, 0:1], RNK[:, 1:2], ALU.add).then_inc(s["srt_e"], 1)
                    v.tensor_tensor(CUR, CUR, PS[3][:, 0:16], ALU.add).then_inc(s["srt_add"], 1)
                    dve.wait_ge(s["srt_add"], i * 2 + (NTL + 2))
                    dve.wait_ge(s["srt_put"], i * 16 + 16)
                dve.wait_ge(s["ld_sorted"], 16)

            dve.wait_ge(s["ld_rec"], 32)
            dst_i = RLv[:, :, 1].rearrange("p (g e) -> p g e", g=GR)
            v.tensor_copy(LDv, dst_i)
            link(v.tensor_tensor(LIf[:, :, 0:P - 1], dst_i[:, :, 0:P - 1], dst_i[:, :, 1:P], ALU.is_gt))
            link(v.tensor_tensor(LIf[:, :, P - 1], dst_i[:, :, P - 1], NXT[:, :, 1], ALU.is_gt))
            v.tensor_reduce(FLF[:, 0:1], LIf.rearrange("p g e -> p (g e)"), AX.X, ALU.add).then_inc(s["flag_cmp"], 1)
            dve.wait_ge(s["flag_mm"], 1)
            v.tensor_copy(FLG[:, 0:1], PS[0][:, 0:1]).then_inc(s["flag_ready"], 1)
            dve.wait_ge(s["flag_ready"], 1)
            unsorted = dve.value_load(FLG[0:1, 0:1], min_val=0, max_val=EP)
            with dve.If(unsorted >= 1):
                sort_records()
            v.tensor_single_scalar(LI, RLv[:, :, 0], P - 1, ALU.bitwise_and)
            link(v.tensor_single_scalar(LJ, RLv[:, :, 0], 7, ALU.arith_shift_right))
            v.tensor_copy(Fl[:, 0, :], LI)
            v.scalar_tensor_tensor(Fl[:, 1, :], RLv[:, :, 2], float(KW), LJ, ALU.mult, ALU.add)
            v.tensor_copy(Fl[:, 2, :], RLv[:, :, 1])
            link(v.scalar_tensor_tensor(IDm, RLv[:, :, 1], float(R8), RLv[:, :, 3], ALU.mult, ALU.add))
            dve.wait_ge(s["consts"], 1)
            for g in range(GR):
                v.tensor_scalar(LKEY[:, g, P:P + 1], pcol[:, g:g + 1], float(P), None, ALU.mult)
            link(v.memset(cnt[:, 0:1], 0.0))
            for g in range(GR):
                v.tensor_scalar(LKEY[:, g, 0:P], IDm[:, P * g:P * (g + 1)], LKEY[:, g, P:P + 1], None, ALU.add)
            v.scalar_tensor_tensor(Fl[:, 3, :], RLv[:, :, 0], float(R8), RLv[:, :, 3], ALU.mult, ALU.add)\
             .then_inc(s["fields"], 1)
            dve.wait_ge(s["idx_mm"], 1)
            v.tensor_copy(IE, PS[4][:, :]).then_inc(s["idx_ev"], 1)
            dve.wait_ge(s["ld_w0"], 16)
            dve.wait_ge(s["ld_at"], 32)
            for lr in range(2):
                for k in range(2):
                    link(v.tensor_tensor(TMP, W0[:, k, :], AT[:, lr, :], ALU.mult))
                    ins = v.tensor_reduce(VL[:, k, 32 * lr:32 * lr + 32], TMP.rearrange("p (r d) -> p r d", d=HD),
                                          AX.X, ALU.add)
                    ins.then_inc(s["vl_done"], 1)
                    dve.wait_ge(s["vl_done"], 2 * lr + k + 1)
            dve.wait_ge(s["consts"], 1)
            for g in range(GR):
                last = v.tensor_scalar(DG[:, P * g:P * (g + 1)], ident[:, :], DST[:, g, P - 1:P], None, ALU.mult)
            last.then_inc(s["diag_done"], 1)
            dve.wait_ge(s["tab_mm"], 1)
            v.tensor_copy(ELS[:, 0:8, :].rearrange("p t n -> p (t n)"), PS[6][:, :]).then_inc(s["tab_ev"], 1)
            v.tensor_copy(ELS[:, 8:NT, :].rearrange("p t n -> p (t n)"), PS[7][:, 0:(NT - 8) * 64]).then_inc(s["tab_ev"], 1)
            dve.wait_ge(s["bc_mm"], 1)
            link(v.tensor_scalar(TMP[:, 0:Q], PS[4][:, :], w16col[:, 0:1], 0.0, ALU.is_lt, ALU.add, accum_out=cnt[:, 0:1]))
            link(v.tensor_tensor(cnt[:, 1:2], cnt[:, 0:1], pcol[:, 0:1], ALU.add))
            CMP = TMP[:, 0:STEPS // 2 + 1].bitcast(F16)[:, 0:STEPS]
            v.tensor_scalar(CMP, IOT, cnt[:, 1:2], None, ALU.is_ge).then_inc(s["cmp_done"], 1)
            dve.wait_ge(s["ws_mm"], 1)
            v.tensor_scalar(WS[:, 0:512], PS[5][:, :], 1.0, None, ALU.subtract)
            link(v.tensor_scalar(WS[:, 512:STEPS], PS[6][:, 0:STEPS - 512], 1.0, None, ALU.subtract))
            v.tensor_scalar(OFF, WS, float(3 * H), None, ALU.mult)
            link(v.tensor_tensor(TMP[:, 1024:1024 + STEPS], IOT, WS, ALU.subtract))
            for g in range(GR):
                last = v.tensor_scalar(SEL[:, g, :], TMP[:, 1024:1024 + STEPS], pcol[:, g:g + 1], None, ALU.is_equal)
            last.then_inc(s["sel_ready"], 1)
            dve.wait_ge(s["fld_mm"], 1)
            v.tensor_copy(SLO[:, 0:512], PS[4][:, :])
            v.tensor_copy(SLO[:, 512:STEPS], PS[5][:, 0:STEPS - 512]).then_inc(s["fld_ev"], 1)
            dve.wait_ge(s["fld_mm"], 2)
            v.scalar_tensor_tensor(DJ[:, 0:512], WS[:, 0:512], -float(WIN), PS[6][:, :], ALU.mult, ALU.add)
            v.scalar_tensor_tensor(DJ[:, 512:STEPS], WS[:, 512:STEPS], -float(WIN), PS[7][:, 0:STEPS - 512], ALU.mult, ALU.add)\
             .then_inc(s["fld_ev"], 1)
            dve.wait_ge(s["fld_ev"], 2)
            link(v.tensor_scalar(TMP[:, 0:STEPS], DJ, 0.0, 1e6, ALU.is_lt, ALU.mult))
            link(v.tensor_scalar(TMP[:, 1024:1024 + STEPS], DJ, float(WIN - 1), 1e6, ALU.is_gt, ALU.mult))
            link(v.tensor_tensor(KEY, TMP[:, 0:STEPS], TMP[:, 1024:1024 + STEPS], ALU.add))
            link(v.scalar_tensor_tensor(KEY, DJ, float(SH), KEY, ALU.mult, ALU.add))
            dve.wait_ge(s["fld_mm"], 3)
            v.tensor_tensor(KEY[:, 0:512], KEY[:, 0:512], PS[4][:, :], ALU.add)
            v.tensor_tensor(KEY[:, 512:STEPS], KEY[:, 512:STEPS], PS[5][:, 0:STEPS - 512], ALU.add)
            link(v.tensor_tensor(IDX, IOT, WS, ALU.subtract))
            v.tensor_scalar(TI, IDX, float(P), None, ALU.mult).then_inc(s["steps_done"], 1)
            for c in range(SC):
                link(v.tensor_scalar(SCOL[:, c:c + 1], pcol[:, 0:1], float(P * c), float(P), ALU.add, ALU.mult))
            for c in range(SC):
                n = min(P, STEPS - P * c)
                dve.wait_ge(s["key_mm"], c + 1)
                v.tensor_scalar(TCOL[0:n, c:c + 1], PS[6 + c % 2][0:n, P:P + 1], 1.0 / P, None, ALU.mult)
                if n < P:
                    v.memset(KEY16[:, c, :], -1.0)
                    link(v.memset(TMP[:, 0:1], 0.0))
                v.tensor_scalar(KEY16[0:n, c, :], PS[6 + c % 2][0:n, 0:P], SCOL[0:n, c:c + 1], None, ALU.subtract)\
                 .then_inc(s["key_ev"], 1)
            dve.wait_ge(s["er_ld"], 16)
            for i in range(4):
                dve.wait_ge(fs_st[i], NT * 16)
            dve.wait_ge(s["feat_mm"], NT * 4)
            link(v.tensor_copy(ERWv[:, :, 0, :], ERF))
            link(v.tensor_tensor(ERG, ERF, ERWv[:, :, 0, :], ALU.subtract))
            link(v.tensor_copy(ERWv[:, :, 1, :], ERG))
            link(v.tensor_tensor(ERF, ERG, ERWv[:, :, 1, :], ALU.subtract))
            v.tensor_copy(ERWv[:, :, 2, :], ERF).then_inc(s["erw_ready"], 1)

            def compare(k, n):
                v.tensor_scalar(OHT[k][:, 0:n * P], KRB[k][:, 0:n * P], pcol[:, 0:1], None, ALU.is_equal).then_inc(s["oht"], 1)

            def sum_parts(k, at, n):
                v.tensor_reduce(ERSf[:, bass.ds(at * H, n * H)],
                                PS[4 + k][:, 0:n * 3 * H].rearrange("p (s q h) -> p s h q", q=3, h=H), AX.X, ALU.add)\
                 .then_inc(s["er_red"], 1)

            for k in range(2):
                dve.wait_ge(k_ld[k], 16)
                compare(k, CK)
            with dve.Fori(0, (NCK - 2) // 2) as i:
                for k in range(2):
                    dve.wait_ge(s["er_mm"], i * 2 + (1 + k))
                    sum_parts(k, i * (2 * CK) + CK * k, CK)
                    dve.wait_ge(k_ld[k], i * 16 + 32)
                    compare(k, CK)
            dve.wait_ge(s["er_mm"], NCK - 1)
            sum_parts(0, CK * (NCK - 2), CK)
            dve.wait_ge(k_ld[0], 16 * (NCK // 2 + 1))
            compare(0, CTAIL)
            dve.wait_ge(s["er_mm"], NCK)
            sum_parts(1, CK * (NCK - 1), CK)
            dve.wait_ge(s["er_mm"], NCK + 1)
            sum_parts(0, CK * NCK, CTAIL)
            for c in range(SC):
                n = min(P, STEPS - P * c)
                if c >= 2:
                    dve.wait_ge(s["sc_mm"], c - 1)
                v.tensor_scalar(SELT[0:n, c % 2, :], IOT[0:n, 0:Q], TCOL[0:n, c:c + 1], None, ALU.is_equal).then_inc(s["selt"], 1)
            dve.wait_ge(s["tab_st"], 16 * NT)
            dve.wait_ge(s["er_st"], 16)
            dve.wait_ge(s["key_st"], 16)
            v.memset(ADJ[:, :, :].rearrange("p r k -> p (r k)").bitcast(F32), 0.0).then_inc(s["a_add"], 1)

            dve.wait_ge(s["er_mm"], NCK + 1)
            link(v.tensor_scalar(OFF, WS, float(KW), None, ALU.mult))

            def onehots(k, col):
                v.tensor_scalar(OHS[k], iota128[:, :], SLO[:, col], None, ALU.is_equal)
                v.tensor_scalar(OHK[k], iota480[:, :], KEY[:, col], None, ALU.is_equal).then_inc(s["a_oh"], 1)

            def add_step(k, off):
                dst = ADJ[:, :, bass.ds(off, KW)]
                v.tensor_tensor(dst, dst, EV[k], ALU.add).then_inc(s["a_add"], 1)

            for k in range(2):
                onehots(k, slice(k, k + 1))
            with dve.Fori(0, (STEPS - 2) // AU) as i:
                offs = offsets(DVE, i * AU, AU, KW * (WINS - 1))
                for u in range(AU):
                    k = u % 2
                    dve.wait_ge(s["a_mm"], i * AU + (u + 1))
                    onehots(k, bass.ds(i * AU + (2 + u), 1))
                    dve.wait_ge(s["a_ev"], i * AU + (u + 1))
                    dve.wait_ge(s["a_add"], i * AU + (u + 1))
                    add_step(k, offs[u])
            offs = offsets(DVE, STEPS - 2, 2, KW * (WINS - 1))
            for k in range(2):
                dve.wait_ge(s["a_ev"], STEPS - 1 + k)
                dve.wait_ge(s["a_add"], STEPS - 1 + k)
                add_step(k, offs[k])
            dve.wait_ge(s["a_add"], STEPS + 1)
            v.tensor_scalar(OFF, WS, 64.0, None, ALU.mult).then_inc(s["off_acc"], 1)

            dve.wait_ge(s["pool_link"], LINKS)
            for k in range(2):
                dve.wait_ge(r_st[k], 16 * ((NGB + 1 - k) // 2))
            v.memset(cnt[:, 0:1], 0.0).then_inc(s["r_all"], 1)
            same = FL[:, 0, :].rearrange("p (g e) -> p g e", g=GR)
            sameb = FL[:, 1, :].rearrange("p (g e) -> p g e", g=GR)
            for f in (FL[:, 0, :], FL[:, 1, :]):
                link(v.memset(f, 0.0))
            v.tensor_tensor(same[:, :, 1:P], DST[:, :, 1:P], DST[:, :, 0:P - 1], ALU.is_equal)
            link(v.tensor_tensor(sameb[:, :, 0:P - 1], DST[:, :, 0:P - 1], DST[:, :, 1:P], ALU.is_equal))
            for j in range(2):
                link(v.tensor_scalar(FL[:, 2 + j, :], FL[:, j, :], -1.0, BIG, ALU.add, ALU.mult))
            for j, e in enumerate((0, P - 1)):
                for h in range(H):
                    last = v.tensor_copy(RD[:, j, :].rearrange("p (g h) -> p g h", h=H)[:, :, h], DST[:, :, e])
            last.then_inc(s["flags_in"], 1)
            D0R, D1R, LKR, UNR, CR = (ROW[0:H, j, :] for j in range(5))
            dve.wait_ge(s["flags_mm"], 1)
            v.tensor_copy(D0R, PS[4][0:H, :])
            link(v.tensor_copy(D1R, PS[5][0:H, :]))
            link(v.tensor_tensor(UNR, D0R, D1R, ALU.is_equal))
            link(v.memset(LKR, 0.0))
            link(v.tensor_tensor(LKR[:, 1:Q], D0R[:, 1:Q], D1R[:, 0:Q - 1], ALU.is_equal))
            D0R_, D1R_ = D0R, D1R

            def seg_scan(dst, op, mx, back, n):
                ident_ = -BIG if mx else 0.0
                op0 = ALU.add if mx else ALU.mult
                flags = FL[:, (2 if mx else 0) + back, :]
                e0, e1 = (P - 1, 0) if back else (0, P - 1)
                rev = (lambda ap: ap[:, ::-1]) if back else (lambda ap: ap)

                def scans():
                    for h in range(H):
                        ins = v.tensor_tensor_scan(rev(dst[:, h, :]), rev(flags), rev(S[:, h, :]), ident_, op0, op)
                    return ins

                scans().then_inc(s["tail_ready"], 1)
                cont = D0R_
                lk = LKR[:, 1:Q] if back else LKR[:, 0:Q]
                link(v.memset(cont, 0.0))
                m = Q - 1 if back else Q
                link(v.tensor_tensor(cont[:, 0:m], UNR[:, 0:m], lk, ALU.mult))
                if mx:
                    link(v.tensor_scalar(cont, cont, -1.0, BIG, ALU.add, ALU.mult))
                dve.wait_ge(s["tail_mm"], n)
                link(v.tensor_copy(D1R_, PS[4][0:H, :]))
                link(v.tensor_tensor_scan(rev(CR), rev(cont), rev(D1R_), ident_, op0, op))
                link(v.memset(cont, ident_))
                lk1 = LKR[:, 1:Q]
                src = CR[:, 1:Q] if back else CR[:, 0:Q - 1]
                to = cont[:, 0:Q - 1] if back else cont[:, 1:Q]
                if mx:
                    link(v.tensor_scalar(D1R_[:, 1:Q], lk1, -1.0, BIG, ALU.add, ALU.mult))
                    v.tensor_tensor(to, src, D1R_[:, 1:Q], ALU.add).then_inc(s["cin_ready"], 1)
                else:
                    v.tensor_tensor(to, src, lk1, ALU.mult).then_inc(s["cin_ready"], 1)
                edge = S.rearrange("p h (g e) -> p h g e", g=GR)[:, :, :, e0]
                keep = SC16[:, 0, :].rearrange("p (h g) -> p h g", h=H)
                link(v.tensor_copy(keep, edge))
                dve.wait_ge(s["cin_mm"], n)
                carry = PS[5][:, 0:GR * H].rearrange("p (g h) -> p h g", h=H)
                link(v.tensor_tensor(edge, keep, carry, op))
                link(scans())
                link(v.tensor_copy(edge, keep))

            dve.wait_ge(s["lane_ev"], GR)
            Sf = S.rearrange("p h n -> p (h n)")
            link(v.scalar_tensor_tensor(Sf, Sf, 0.2, Sf, ALU.mult, ALU.max))
            seg_scan(FA, ALU.max, True, 0, 1)
            seg_scan(BA, ALU.max, True, 1, 2)
            flat = lambda ap: ap.rearrange("p h n -> p (h n)")
            link(v.tensor_tensor(flat(FA), flat(FA), flat(BA), ALU.max))
            v.tensor_tensor(flat(S), flat(S), flat(FA), ALU.subtract).then_inc(s["exp_ready"], 1)
            dve.wait_ge(s["exp_done"], 1)
            seg_scan(FA, ALU.add, False, 0, 3)
            seg_scan(BA, ALU.add, False, 1, 4)
            link(v.tensor_tensor(flat(FA), flat(FA), flat(BA), ALU.add))
            link(v.tensor_tensor(flat(FA), flat(FA), flat(S), ALU.subtract))
            link(v.reciprocal(flat(FA), flat(FA)))
            v.tensor_tensor(flat(S), flat(S), flat(FA), ALU.mult).then_inc(s["alpha_ready"], 1)
            dve.wait_ge(s["als_mm"], H)
            v.memset(ACCf, 0.0).then_inc(s["l_acc"], 1)
            dve.wait_ge(s["als_ev"], H)

            def weigh(slot, st):
                wv = WOH[:, slot, :].rearrange("p (h j) -> p h j", h=H)
                al = ALSf[:, bass.ds(st * H, H)]
                col = bass.ds(st, 1)
                v.scalar_tensor_tensor(wv, iota16[:, :].rearrange("p (a j) -> p a j", a=1).to_broadcast([P, H, WIN]),
                                       DJ[:, col],
                                       al.rearrange("p (h a) -> p h a", a=1).to_broadcast([P, H, WIN]),
                                       ALU.is_equal, ALU.mult).then_inc(s["l_woh"], 1)

            def accumulate(bank, off):
                dst = ACCf[:, bass.ds(off, 64)]
                v.tensor_tensor(dst, dst, PS[bank][:, 0:64], ALU.add).then_inc(s["l_acc"], 1)

            dve.wait_ge(s["off_acc"], 1)
            offs = offsets(DVE, 0, FR, 64 * (WINS - 1))
            for st in range(HEAD + FR):
                if st >= 4:
                    dve.wait_ge(s["l_mm"], st - 3)
                weigh(st % 4, st)
                if st >= 2:
                    dve.wait_ge(s["l_mm"], st - 1)
                    dve.wait_ge(s["l_acc"], st - 1)
                    accumulate(6 + st % 2, offs[st - 2])
            with dve.Fori(0, (GRPS - 1) // 2) as i:
                offs = offsets(DVE, i * (2 * FR) + FR, 2 * FR, 64 * (WINS - 1))
                for u in range(2 * FR):
                    st = HEAD + FR + u
                    dve.wait_ge(s["l_mm"], i * (2 * FR) + (st - 3))
                    weigh(st % 4, i * (2 * FR) + st)
                    dve.wait_ge(s["l_mm"], i * (2 * FR) + (st - 1))
                    dve.wait_ge(s["l_acc"], i * (2 * FR) + (st - 1))
                    accumulate(6 + st % 2, offs[u])
            offs = offsets(DVE, STEPS - 2, 2, 64 * (WINS - 1))
            for st in range(STEPS, STEPS + 2):
                dve.wait_ge(s["l_mm"], st - 1)
                dve.wait_ge(s["l_acc"], st - 1)
                accumulate(6 + st % 2, offs[st - STEPS])

            dve.wait_ge(s["l_acc"], STEPS + 1)
            dve.wait_ge(s["ld_bc"], 16)
            v.memset(XT[:, :, NW:NP], 0.0)
            for f in range(2):
                for hh in range(2):
                    p0 = 64 * hh
                    c0 = 32 * f + 16 * hh
                    v.tensor_scalar(XT[p0:p0 + 64, f, 0:NW].rearrange("p (w j) -> p w j", j=WIN),
                                    ACC[p0:p0 + 64, :, c0:c0 + WIN], BC[p0:p0 + 64, f:f + 1], None, ALU.add)
            v.memset(X[:, NT - 1, :], 0.0).then_inc(s["ht_ready"], 1)
            v.tensor_tensor(BC[:, 20:26], BC[:, 6:12], BC[:, 12:18], ALU.add)
            dve.wait_ge(s["ld_x"], 32)
            for t in range(NT):
                dve.wait_ge(s["ht_mm"], t + 1)
                v.tensor_tensor(X[:, t, :], X[:, t, :], PS[t % 4][:, 0:D], ALU.add).then_inc(s["ht_add"], 1)

            lns = [0]

            def layer_norm():
                lns[0] += 1
                for t in range(NT):
                    ins = v.bn_stats(ST[:, t, :], X[:, t, :])
                link(ins)
                for t in range(NT):
                    ins = v.bn_aggr(MV[:, t, :], ST[:, t, :])
                link(ins)
                v.tensor_scalar(MV[:, :, 1], MV[:, :, 1], EPS, None, ALU.add).then_inc(s["var_ready"], 1)
                dve.wait_ge(s["std_ready"], lns[0])
                link(v.reciprocal(RS[:, :], RS[:, :]))
                for t in range(NT):
                    ins = v.tensor_scalar(X[:, t, :], X[:, t, :], MV[:, t, 0:1], RS[:, t:t + 1], ALU.subtract, ALU.mult)
                ins.then_inc(s["ln_done"], 1)

            def xt_evac(n):
                for q in range(4):
                    dve.wait_ge(s["xt_mm"], 8 * n + 2 * q + 2)
                    w = min(512, NP - 512 * q)
                    v.tensor_copy(XT[:, 1, 512 * q:512 * q + w], PS[2 * q + 1][:, 0:w]).then_inc(s["xt_evd"], 1)

            dve.wait_ge(s["ht_add"], NT)
            layer_norm()
            xt_evac(0)
            for i in range(R2 * NC):
                r, c = i // NC, i % NC
                for j in range(3):
                    dve.wait_ge(s["m_mm"], 3 * i + j + 1)
                    v.tensor_scalar((M1, M2)[r][:, 3 * c + j, :], PS[4 + j][:, 0:D], 0.0, None, ALU.max).then_inc(s["m_ev"], 1)

            def agg_evac(dst, total):
                dve.wait_ge(s["chunk_used"], total)
                for j in range(4):
                    v.tensor_copy(dst[:, 0, CW * j:CW * (j + 1)], PS[j][:, 0:CW])
                v.memset(dst[:, :, NW:NP], 0.0).then_inc(s["agg_evd"], 1)

            agg_evac(XT, R2 * SH)
            for c in range(NC):
                dve.wait_ge(s["gate_ev"], 6 * c + 4)
                v.tensor_tensor(CC, GT[:, 0:2, :], GT[:, 2:4, :], ALU.mult).then_inc(s["c_ready"], 1)
                dve.wait_ge(s["tc_ready"], c + 1)
                dve.wait_ge(s["gate_ev"], 6 * c + 6)
                if c:
                    dve.wait_ge(s["x1_mm"], c)
                v.tensor_tensor(HN, CC, GT[:, 4:6, :], ALU.mult).then_inc(s["hn_ready"], 1)
                dve.wait_ge(s["x3_mm"], c + 1)
                xv = X[:, 3 * c:3 * c + 2, :].rearrange("p t d -> p (t d)")
                v.tensor_tensor(xv, xv, PS[6][:, :], ALU.add)
                v.tensor_tensor(X[:, 3 * c + 2, :], X[:, 3 * c + 2, :], PS[7][:, 0:D], ALU.add).then_inc(s["x3_add"], 1)
            dve.wait_ge(s["x3_add"], NC)
            layer_norm()
            xt_evac(1)
            link(v.memset(RC[:, :], 1.0))
            base = R2 * SH
            for u in range(2):
                for c in range(SH):
                    if c >= 2:
                        dve.wait_ge(s["chunk_used"], base + u * SH + c - 1)
                        if u == 0:
                            dve.wait_ge(s["cnt_acc"], c - 1)
                    a0, a1 = (ADJ[:, r, :].rearrange("p (n s) -> p n s", s=SH)[:, :, c] for r in range(R2))
                    v.tensor_tensor(CH[:, c % 2, :], a0, a1, ALU.add).then_inc(s["chunk_ready"], 1)
                if u == 0:
                    dve.wait_ge(s["cnt_mm"], 1)
                    lastn = NW - (NT - 1) * P
                    v.tensor_scalar(RC[:, 0:NT - 1], PS[4][:, 0:NT - 1], 1.0, None, ALU.max)
                    link(v.tensor_scalar(RC[0:lastn, NT - 1:NT], PS[4][0:lastn, NT - 1:NT], 1.0, None, ALU.max))
                    link(v.reciprocal(RC[:, :], RC[:, :]))
                agg_evac(B2T, base + (u + 1) * SH)
                for t in range(NT):
                    b = 2 * (t % 4)
                    dve.wait_ge(s["o_mm"], NT * u + t + 1)
                    link(v.tensor_scalar(B1[:, t, :], PS[b][:, 0:D], RC[:, t:t + 1], None, ALU.mult))
                    link(v.tensor_tensor(B1[:, t, :], B1[:, t, :], PS[b + 1][:, 0:D], ALU.add))
                    v.tensor_tensor_reduce(out=CH[:, 0, 0:D], in0=B1[:, t, :], in1=B1[:, t, :], scale=1.0, scalar=0.0,
                                           op0=ALU.mult, op1=ALU.add, accum_out=RS[:, t:t + 1]).then_inc(s["o_ready"], 1)
                dve.wait_ge(s["nrm_done"], u + 1)
                link(v.tensor_scalar(RS[:, :], RS[:, :], 1e-12, None, ALU.max))
                link(v.reciprocal(RS[:, :], RS[:, :]))
                if u == 0:
                    for t in range(NT):
                        ins = v.tensor_scalar(B1[:, t, :], B1[:, t, :], RS[:, t:t + 1], 0.0, ALU.mult, ALU.max)
                    ins.then_inc(s["h_ready"], 1)
                    xt_evac(2)
                else:
                    for t in range(NT):
                        ins = v.scalar_tensor_tensor(X[:, t, :], B1[:, t, :], RS[:, t:t + 1], X[:, t, :], ALU.mult, ALU.add)
                    link(ins)
            layer_norm()
            dve.wait_ge(s["ld_wt3"], 48)
            for lr in range(2):
                for k in range(2):
                    link(v.tensor_tensor(TMP3, WT3[:, k, 0:D], A3[:, lr, :], ALU.mult))
                    ins = v.tensor_reduce(WT3[:, k, D + H * lr:D + H * (lr + 1)], TMP3.rearrange("p (h d) -> p h d", d=HD),
                                          AX.X, ALU.add)
                    if (lr, k) == (1, 1):
                        ins.then_inc(s["vl3_done"], 1)
                    else:
                        link(ins)
            xt_evac(3)
            dve.wait_ge(s["g3"], 16 * 2 * NT)
            a3 = lambda j: S3[:, j, :].rearrange("p (t h) -> p t h", h=H)
            link(v.tensor_tensor(a3(0), AG3, G3[:, :, D + H:D + 2 * H], ALU.add))
            link(v.scalar_tensor_tensor(S3[:, 0, :], S3[:, 0, :], 0.01, S3[:, 0, :], ALU.mult, ALU.max))
            m3 = S3[:, 1, 0:NT]
            link(v.tensor_reduce(m3, a3(0), AX.X, ALU.max))
            v.tensor_tensor(a3(0), a3(0), m3.rearrange("p (t a) -> p t a", a=1).to_broadcast([P, NT, H]),
                            ALU.subtract).then_inc(s["s3_ready"], 1)
            dve.wait_ge(s["s3_exp"], 1)
            link(v.tensor_reduce(m3, a3(0), AX.X, ALU.add))
            link(v.reciprocal(m3, m3))
            link(v.tensor_tensor(a3(0), a3(0), m3.rearrange("p (t a) -> p t a", a=1).to_broadcast([P, NT, H]), ALU.mult))
            for t in range(NT):
                gv = G3[:, t, 0:D].rearrange("p (h d) -> p h d", h=H)
                ins = v.tensor_tensor(gv, gv, S3[:, 0, H * t:H * t + H].rearrange("p (h a) -> p h a", a=1).to_broadcast([P, H, HD]), ALU.mult)
            link(ins)
            for t in range(NT):
                ins = v.tensor_reduce(T64[:, t, :], G3[:, t, 0:D].rearrange("p (h d) -> p d h", h=H), AX.X, ALU.add)
            link(ins)
            for t in range(NT):
                xv = X[:, t, :].rearrange("p (h d) -> p h d", h=H)
                ins = v.tensor_tensor(xv, xv, T64[:, t, :].rearrange("p (a d) -> p a d", a=1).to_broadcast([P, H, HD]), ALU.add)
            link(ins)
            layer_norm()

        @block.tensor
        def _(pe):
            mm = nc.tensor.matmul
            tr = nc.tensor.transpose
            pe.wait_ge(s["consts"], 1)
            pe.wait_ge(s["flag_cmp"], 1)
            mm(PS[0][:, 0:1], ones[:, :], FLF[:, 0:1], start=True, stop=True).then_inc(s["flag_mm"], 1)
            pe.wait_ge(s["flag_ready"], 1)
            unsorted = pe.value_load(FLG[0:1, 0:1], min_val=0, max_val=EP)
            with pe.If(unsorted >= 1):
                pe.wait_ge(s["srt_a"], 1)
                for g in range(GR):
                    ins = tr(PS[1][:, P * g:P * (g + 1)], LD[:, P * g:P * (g + 1)], ident[:, :])
                ins.then_inc(s["srt_pre"], 1)
                with pe.Fori(0, NTL) as i:
                    pe.wait_ge(s["srt_oh"], i + 1)
                    mm(PS[3][:, 0:16], OL, HI16, start=True, stop=True).then_inc(s["srt_hist"], 1)
                pe.wait_ge(s["srt_pmm"], 1)
                pe.wait_ge(s["srt_tv"], 1)
                mm(PS[1][:, 0:16], ones[:, :], CUR, start=True, stop=True)
                mm(PS[2][:, 0:16], TRIT, CUR, start=True, stop=True).then_inc(s["srt_pre"], 1)
                with pe.Fori(0, NTL) as i:
                    pe.wait_ge(s["srt_oh"], i + (NTL + 1))
                    mm(PS[1][:, 0:P], ones[:, :], DGc, start=True, stop=True)
                    tr(PS[2][:, 0:P], OL, ident[:, :])
                    mm(PS[3][:, 0:16], OL, HI16, start=True, stop=True).then_inc(s["srt_b"], 1)
                    pe.wait_ge(s["srt_c"], i + 1)
                    mm(PS[0][:, 0:16], OLT, CUR, start=True, stop=True).then_inc(s["srt_d"], 1)
            pe.wait_ge(s["fields"], 1)
            for g in range(GR):
                ins = tr(PS[4][:, P * g:P * (g + 1)], Fl[:, 3, P * g:P * (g + 1)], ident[:, :])
            ins.then_inc(s["idx_mm"], 1)

            def score_tables():
                pe.wait_ge(s["vl_done"], 4)
                for t in range(NT):
                    for k in range(2):
                        ins = mm(PS[6 + t // 8][:, 64 * (t % 8):64 * (t % 8 + 1)], XT0[:, k, P * t:P * (t + 1)],
                                 VL[:, k, :], start=(k == 0), stop=(k == 1))
                ins.then_inc(s["tab_mm"], 1)

            def last_destinations():
                pe.wait_ge(s["diag_done"], 1)
                pe.wait_ge(s["idx_ev"], 1)
                mm(PS[4][:, :], ones[:, :], DG, start=True, stop=True).then_inc(s["bc_mm"], 1)

            def windows_begun():
                pe.wait_ge(s["tab_ev"], 2)
                pe.wait_ge(s["cmp_done"], 1)
                CMP = TMP[:, 0:STEPS // 2 + 1].bitcast(F16)[:, 0:STEPS]
                mm(PS[5][:, :], ones16[:, :], CMP[:, 0:512], start=True, stop=True)
                mm(PS[6][:, 0:STEPS - 512], ones16[:, :], CMP[:, 512:STEPS], start=True, stop=True).then_inc(s["ws_mm"], 1)

            def select(lhs, b0):
                for (bank, lo, hi) in ((b0, 0, 512), (b0 + 1, 512, STEPS)):
                    for g in range(GR):
                        ins = mm(PS[bank][:, 0:hi - lo], lhs(g), SEL[:, g, lo:hi], start=(g == 0), stop=(g == GR - 1))
                return ins

            def step_field(n, f):
                if n == 0:
                    pe.wait_ge(s["sel_ready"], 1)
                if n >= 2:
                    pe.wait_ge(s["fld_ev"], n - 1)
                select(lambda g: Fl[:, f, P * g:P * (g + 1)], 4 + 2 * (n % 2)).then_inc(s["fld_mm"], 1)

            def step_keys(c):
                pe.wait_ge(s["fld_ev"], 2)
                if c >= 2:
                    pe.wait_ge(s["key_ev"], c - 1)
                n = min(P, STEPS - P * c)
                for g in range(GR):
                    ins = mm(PS[6 + c % 2][0:n, 0:P + 1], SEL[:, g, P * c:P * c + n], LKEY[:, g, :],
                             start=(g == 0), stop=(g == GR - 1))
                ins.then_inc(s["key_mm"], 1)

            between = {TABS_AT: score_tables, 16: last_destinations, 19: windows_begun, 22: lambda: step_field(0, 0),
                       24: lambda: step_field(1, 2), 27: lambda: step_field(2, 1)}
            between.update({30 + 2 * c: (lambda c=c: step_keys(c)) for c in range(SC)})
            pe.wait_ge(s["ld_xt"], 16)
            pe.wait_ge(s["ld_w0"], 16)
            for i in range(4 * NT):
                if i in between:
                    between[i]()
                t, c = i // 4, i % 4
                if i >= 4:
                    pe.wait_ge(s["feat_ev"], i - 3)
                for k in range(2):
                    ins = mm(PS[c][:, :], XT0[:, k, P * t:P * (t + 1)], W0[:, k, 512 * c:512 * (c + 1)],
                             start=(k == 0), stop=(k == 1))
                ins.then_inc(s["feat_mm"], 1)

            def er_chunk(k, step, n):
                offs = offsets(PE, step, n, 3 * H * (WINS - 1))
                for j in range(n):
                    ins = mm(PS[4 + k][:, 3 * H * j:3 * H * (j + 1)], OHT[k][:, P * j:P * (j + 1)],
                             ERW[:, bass.ds(offs[j], 3 * H)], start=True, stop=True)
                ins.then_inc(s["er_mm"], 1)

            pe.wait_ge(s["steps_done"], 1)
            pe.wait_ge(s["erw_ready"], 1)
            for k in range(2):
                pe.wait_ge(s["oht"], k + 1)
                er_chunk(k, CK * k, CK)
            with pe.Fori(0, (NCK - 2) // 2) as i:
                for k in range(2):
                    pe.wait_ge(s["oht"], i * 2 + (3 + k))
                    pe.wait_ge(s["er_red"], i * 2 + (1 + k))
                    er_chunk(k, i * (2 * CK) + CK * (2 + k), CK)
            pe.wait_ge(s["oht"], NCK + 1)
            pe.wait_ge(s["er_red"], NCK - 1)
            er_chunk(0, CK * NCK, CTAIL)
            pe.wait_ge(s["er_red"], NCK + 1)

            def step_transposes(c):
                n = min(P, STEPS - P * c)
                if c >= 2:
                    pe.wait_ge(s["et_ev"], c - 1)
                for h in range(H):
                    ins = tr(PS[4 + c % 2][0:n, P * h:P * (h + 1)], ERS[:, P * c:P * c + n, h], ident[:, :])
                ins.then_inc(s["et_mm"], 1)

            step_transposes(0)
            for c in range(SC):
                if c + 1 < SC:
                    step_transposes(c + 1)
                n = min(P, STEPS - P * c)
                pe.wait_ge(s["et_ev"], c + 1)
                pe.wait_ge(s["selt"], c + 1)
                for g in range(GR):
                    ins = mm(PS[g][:, :], SELT[0:n, c % 2, P * g:P * (g + 1)], ET[0:n, c % 2, :], start=(c == 0), stop=False)
                ins.then_inc(s["sc_mm"], 1)
            pe.wait_ge(s["steps_done"], 1)
            for k in range(2):
                pe.wait_ge(s["a_oh"], k + 1)
                mm(PS[6 + k][:, 0:R2 * KW], OHS[k], OHK[k], start=True, stop=True).then_inc(s["a_mm"], 1)
            with pe.Fori(0, (STEPS - 2) // AU) as i:
                for u in range(AU):
                    k = u % 2
                    pe.wait_ge(s["a_oh"], i * AU + (3 + u))
                    pe.wait_ge(s["a_ev"], i * AU + (1 + u))
                    mm(PS[6 + k][:, 0:R2 * KW], OHS[k], OHK[k], start=True, stop=True).then_inc(s["a_mm"], 1)
            pe.wait_ge(s["pool_link"], LINKS)
            for g in range(GR):
                for h in range(H):
                    ins = mm(PS[g][:, P * h:P * (h + 1)], SUM[:, P * g:P * (g + 1), h], ident[:, :],
                             start=False, stop=(h == H - 1))
                ins.then_inc(s["lane_mm"], 1)
            pe.wait_ge(s["flags_in"], 1)
            for j in range(2):
                for g in range(GR):
                    ins = tr(PS[4 + j][0:H, P * g:P * (g + 1)], RD[:, j, H * g:H * (g + 1)], ident[:, :])
            ins.then_inc(s["flags_mm"], 1)
            for n in range(4):
                dst = (FA, BA)[n % 2].rearrange("p h (g e) -> p h g e", g=GR)
                e1 = (P - 1, 0)[n % 2]
                pe.wait_ge(s["tail_ready"], n + 1)
                for g in range(GR):
                    ins = tr(PS[4][0:H, P * g:P * (g + 1)], dst[:, :, g, e1], ident[:, :])
                ins.then_inc(s["tail_mm"], 1)
                pe.wait_ge(s["cin_ready"], n + 1)
                for g in range(GR):
                    ins = tr(PS[5][:, H * g:H * (g + 1)], ROW[0:H, 0, P * g:P * (g + 1)], ident[0:H, 0:H])
                ins.then_inc(s["cin_mm"], 1)
            pe.wait_ge(s["alpha_ready"], 1)
            pe.wait_ge(s["a_ev"], STEPS)
            for h in range(H):
                select(lambda g: S[:, h, P * g:P * (g + 1)], 2 * h).then_inc(s["als_mm"], 1)
            pe.wait_ge(s["als_ev"], H)

            def scatter(slot, woh, bank):
                for f in range(2):
                    ins = mm(PS[bank][:, 32 * f:32 * (f + 1)], FB[:, slot, P * f:P * (f + 1)],
                             WOH[:, woh, 32 * f:32 * (f + 1)], start=True, stop=True)
                ins.then_inc(s["l_mm"], 1)

            for st in range(HEAD + FR):
                pe.wait_ge(s["l_woh"], st + 1)
                pe.wait_ge(f_done[st % FR], 16 * (st // FR + 1))
                if st >= 2:
                    pe.wait_ge(s["l_acc"], st)
                scatter(st % FR, st % 4, 6 + st % 2)
            with pe.Fori(0, (GRPS - 1) // 2) as i:
                for u in range(2 * FR):
                    st = HEAD + FR + u
                    pe.wait_ge(s["l_woh"], i * (2 * FR) + (st + 1))
                    pe.wait_ge(f_done[st % FR], i * 32 + 16 * (st // FR + 1))
                    pe.wait_ge(s["l_acc"], i * (2 * FR) + st)
                    scatter(st % FR, st % 4, 6 + st % 2)
            pe.wait_ge(s["ht_ready"], 1)
            for t in range(NT):
                if t >= 4:
                    pe.wait_ge(s["ht_add"], t - 3)
                for f in range(2):
                    ins = tr(PS[t % 4][:, P * f:P * (f + 1)], XT[:, f, P * t:P * (t + 1)], ident[:, :])
                ins.then_inc(s["ht_mm"], 1)

            def transpose_x(n, src, ready):
                pe.wait_ge(ready[0], ready[1])
                for q in range(4):
                    for k in range(2):
                        for j in range(min(4, NT - 4 * q)):
                            ins = tr(PS[2 * q + k][:, P * j:P * (j + 1)], src[:, 4 * q + j, P * k:P * (k + 1)], ident[:, :])
                        ins.then_inc(s["xt_mm"], 1)
                pe.wait_ge(s["xt_eva"], 4 * (n + 1))
                pe.wait_ge(s["xt_evd"], 4 * (n + 1))

            transpose_x(0, X, (s["ln_done"], 1))
            pe.wait_ge(s["ld_wt1"], 16 * 9)

            def hidden(i):
                r, c = i // NC, i % NC
                if i >= 2:
                    pe.wait_ge(s["h_ev"], 2 * (i - 1))
                for fo in range(2):
                    for k in range(2):
                        ins = mm(PS[2 * (i % 2) + fo][:, 0:CN], WREL[:, k, r, P * fo:P * (fo + 1)],
                                 XT[:, k, CN * c:CN * (c + 1)], start=(k == 0), stop=(k == 1))
                    ins.then_inc(s["h_mm"], 1)

            hidden(0)
            for i in range(R2 * NC):
                if i + 1 < R2 * NC:
                    hidden(i + 1)
                r = i // NC
                pe.wait_ge(s["h_ev"], 2 * (i + 1))
                if i:
                    pe.wait_ge(s["m_ev"], 3 * i)
                for j in range(3):
                    mm(PS[4 + j][:, 0:D], ones[0:1, :], BROW[0:1, r, :], start=True, stop=False)
                    for k in range(2):
                        ins = mm(PS[4 + j][:, 0:D], HC[i % 2][:, k, P * j:P * (j + 1)], WREL[:, k, r, :],
                                 start=False, stop=(k == 1))
                    ins.then_inc(s["m_mm"], 1)
            pe.wait_ge(s["m_ev"], 3 * R2 * NC)

            def aggregate(mats, first):
                n = len(mats) * SH
                for c in range(n):
                    m, sh = mats[c // SH], c % SH
                    pe.wait_ge(s["chunk_ready"], first + c + 1)
                    for fo in range(2):
                        for j in range(4):
                            ins = mm(PS[4 * fo + j][:, 0:CW], m[:, sh, P * fo:P * (fo + 1)],
                                     CH[:, c % 2, CW * j:CW * (j + 1)], start=(c == 0), stop=(c == n - 1))
                    ins.then_inc(s["chunk_used"], 1)

            aggregate((M1, M2), 0)
            pe.wait_ge(s["agg_evd"], 1)
            pe.wait_ge(s["agg_eva"], 4)
            for c in range(NC):
                cs = slice(CN * c, CN * (c + 1))
                if c:
                    pe.wait_ge(s["gate_ev"], 6 * c)
                for j in range(6):
                    for k in range(2):
                        ins = mm(PS[j][:, 0:CN], WIH[:, k, P * j:P * (j + 1)], XT[:, k, cs], start=(k == 0), stop=(k == 1))
                    ins.then_inc(s["gate_mm"], 1)
                pe.wait_ge(s["hn_ready"], c + 1)
                if c:
                    pe.wait_ge(s["x3_add"], c)
                for k in range(2):
                    ins = mm(PS[6][:, 0:CN], W1s[:, k, :], HN[:, k, :], start=(k == 0), stop=(k == 1))
                ins.then_inc(s["x1_mm"], 1)
                pe.wait_ge(s["x1_ev"], c + 1)
                mm(PS[7][:, 0:CN], W2s, X1, start=True, stop=True).then_inc(s["x2_mm"], 1)
                pe.wait_ge(s["x2_ev"], c + 1)
                for j in range(3):
                    o = PS[6 + j // 2][:, D * (j % 2):D * (j % 2 + 1)]
                    mm(o, ones[0:1, :], BROW[0:1, 2, :], start=True, stop=False)
                    ins = mm(o, X2[:, P * j:P * (j + 1)], W3s, start=False, stop=True)
                ins.then_inc(s["x3_mm"], 1)
            transpose_x(1, X, (s["ln_done"], 2))
            pe.wait_ge(s["ld_wt2"], 160)
            for u in range(2):
                Wp, Wl, Wr = W2L[3 * u:3 * u + 3]
                for t in range(NT):
                    if t >= 4:
                        pe.wait_ge(s["p_ev"], NT * u + t - 3)
                    mm(PS[t % 4][:, 0:D], ones[0:1, :], BROW[0:1, 2 * u, :], start=True, stop=False)
                    for k in range(2):
                        ins = mm(PS[t % 4][:, 0:D], XT[:, k, P * t:P * (t + 1)], Wp[:, k, :], start=False, stop=(k == 1))
                    ins.then_inc(s["p_mm"], 1)
                pe.wait_ge(s["p_ev"], NT * (u + 1))
                aggregate((M1,), (R2 + u) * SH)
                if u == 0:
                    pe.wait_ge(s["cnt_acc"], SH)
                    pe.wait_ge(s["agg_eva"], 5)
                    for t in range(NT):
                        w = min(P, NW - P * t)
                        ins = mm(PS[4][0:w, t:t + 1], B2T[:, 0, P * t:P * t + w], ones[:, 0:1], start=True, stop=True)
                    ins.then_inc(s["cnt_mm"], 1)
                pe.wait_ge(s["agg_evd"], 2 + u)
                pe.wait_ge(s["agg_eva"], 4 * (2 + u))
                for t in range(NT):
                    if t >= 4:
                        pe.wait_ge(s["o_ready"], NT * u + t - 3)
                    b = 2 * (t % 4)
                    for k in range(2):
                        mm(PS[b][:, 0:D], B2T[:, k, P * t:P * (t + 1)], Wl[:, k, :], start=(k == 0), stop=(k == 1))
                    mm(PS[b + 1][:, 0:D], ones[0:1, :], BROW[0:1, 1 + 2 * u, :], start=True, stop=False)
                    for k in range(2):
                        ins = mm(PS[b + 1][:, 0:D], XT[:, k, P * t:P * (t + 1)], Wr[:, k, :], start=False, stop=(k == 1))
                    ins.then_inc(s["o_mm"], 1)
                if u == 0:
                    transpose_x(2, B1, (s["h_ready"], 1))
            transpose_x(3, X, (s["ln_done"], 3))
            pe.wait_ge(s["vl3_done"], 1)
            for t in range(NT):
                if t >= 4:
                    pe.wait_ge(s["t_ev"], t - 3)
                for k in range(2):
                    ins = mm(PS[t % 4][:, 0:D + 2 * H], XT[:, k, P * t:P * (t + 1)], WT3[:, k, :], start=(k == 0), stop=(k == 1))
                ins.then_inc(s["t_mm"], 1)


def layout(i):
    import numpy as np
    c = np.ascontiguousarray
    g = {k: np.asarray(v) for k, v in i.items()}
    rec = np.zeros((EP + P, 4), np.int32)
    rec[:, 1] = PAD_DST
    rec[:E, 0] = g["src"]
    rec[:E, 1] = g["dst"]
    rec[:E, 2] = g["edge_type_2"]
    rec[:E, 3] = g["edge_type_8"]
    xT = np.zeros((D, NP), np.float32)
    xT[:, :N] = g["x"].T
    w_ih = g["L1_gnn_W_ih"].T
    pick = lambda a: np.concatenate([a[..., 0:D], a[..., 2 * D:4 * D]], -1)
    row = lambda a: c(a.reshape(1, -1))
    cols = c(np.concatenate([g["L0_gnn_h_bias"], g["L1_gnn_b_rel"].reshape(-1), pick(g["L1_gnn_b_ih"]),
                             pick(g["L1_gnn_b_hh"]), g["L1_gnn_b1"], g["L1_gnn_b2"]]).reshape(20, P).T)
    return [
        ("rec", rec), ("x", c(g["x"])), ("xT", xT), ("edge0", c(np.stack([g["src"][:NP], g["dst"][:NP]]).reshape(2, NT, P).transpose(2, 0, 1))),
        ("w0", c(g["L0_gnn_conv_weights"].transpose(2, 0, 1, 3).reshape(D, R8 * D))),
        ("a0l", row(g["L0_gnn_attn_l"])), ("a0r", row(g["L0_gnn_attn_r"])), ("cols", cols),
        ("wrel", c(g["L1_gnn_W_rel"].transpose(0, 2, 1))), ("brow", c(g["L1_gnn_b_rel"])),
        ("wih", c(pick(w_ih))),
        ("w1", c(g["L1_gnn_W1"].T)), ("w2", c(g["L1_gnn_W2"].T)),
        ("w3", c(g["L1_gnn_W3"].T)), ("b3", row(g["L1_gnn_b3"])),
        ("wp1", c(g["L2_gnn_W_proj1"])), ("bp1", row(g["L2_gnn_b_proj1"])), ("wl1", c(g["L2_gnn_W_l1"])),
        ("bl1", row(g["L2_gnn_b_l1"])), ("wr1", c(g["L2_gnn_W_r1"])),
        ("wp2", c(g["L2_gnn_W_proj2"])), ("bp2", row(g["L2_gnn_b_proj2"])), ("wl2", c(g["L2_gnn_W_l2"])),
        ("bl2", row(g["L2_gnn_b_l2"])), ("wr2", c(g["L2_gnn_W_r2"])),
        ("wt3", c(g["L3_gnn_weight"])), ("a3l", row(g["L3_gnn_attn_l"])), ("a3r", row(g["L3_gnn_attn_r"])),
    ]


def kernel(**inputs):
    import concourse.bacc as bacc
    from concourse.bass_utils import run_bass_kernel_spmd as run

    nc = bacc.Bacc("TRN2", target_bir_lowering=False, num_devices=1)
    arrays, args = {}, []
    for name, a in layout(inputs):
        arrays["in_" + name] = a
        args.append(nc.dram_tensor("in_" + name, a.shape, mybir.dt.from_np(a.dtype), kind="ExternalInput").ap())
    args.append(nc.dram_tensor("out_0", (N, D), F32, kind="ExternalOutput").ap())
    build(nc, *args)
    r = run(nc, [arrays], core_ids=[0])
    return r.results[0]["out_0"]
```

```python
import concourse.bass as bass
from concourse import mybir
from contextlib import ExitStack

F32 = mybir.dt.float32
F16 = mybir.dt.float16
BF16 = mybir.dt.bfloat16
I32 = mybir.dt.int32
SP, DVE, PE = mybir.EngineType.SP, mybir.EngineType.DVE, mybir.EngineType.PE
U16 = mybir.dt.uint16
ALU = mybir.AluOpType
ACT = mybir.ActivationFunctionType
AX = mybir.AxisListType

N = 1875
E = 60000
D = 256
P = 128
NT = -(-N // P)
NP = NT * P
NLAST = N - (NT - 1) * P
H = 4
HD = D // H
R8 = 8
R2 = 2
GR = 4
EP = GR * P * P
TILES = -(-E // P)
WIN = 16
WINS = -(-N // WIN)
NW = WINS * WIN
STEPS = E // P + WINS
SH = NT
KW = WIN * SH
PAD_DST = 2047
BIG = 1e30
EPS = 1e-5
Q = 4 * P

FW = D + H
CK = 16
NCK = STEPS // CK
CTAIL = STEPS - NCK * CK
AU = 32
AS = 8
A_N = (STEPS - AS) // AU
ER_N = (NCK - 2) // 2
assert NCK % 2 == 0 and CTAIL > 0
TABS_AT = 14
SC = -(-STEPS // P)
GB = 7
NGB = TILES // GB
assert NGB * GB == TILES and NGB % 2 == 1
BATCH = 16 * GB
N_IT = (NGB - 3) // 2
LINKS = 4 + 4 * N_IT + 4
FR = 16
HEAD = STEPS % FR
GRPS = STEPS // FR
LAG = 8
NWOH = LAG
GROUPS = [(t, min(t + 4, NT)) for t in range(0, NT, 4)]
assert HEAD >= NWOH and FR % NWOH == 0
CW = NW // 4
CN = 3 * P
NC = NP // CN

A_SLO, A_KEY, A_DJ, A_IDX, A_WS, A_WI, A_IOT = (STEPS * i for i in range(7))
A_SEL = 7 * STEPS
A_F = A_SEL + GR * STEPS
A_SUM = A_F + 4 * Q
A_DG = A_SUM + H * STEPS
A_BIG = A_DG + Q
A_W0 = A_BIG
A_XT0 = A_W0 + 2 * R8 * D
A_FS = A_XT0 + 2 * NP
A_IE = A_DG
A_RING = A_BIG
A_KRB = A_RING + 2 * GB * FW
A_OHT = A_KRB + 2 * CK * P // 2
A_ERW = A_OHT + 2 * CK * P // 2
A_ERS = A_ERW + WINS * 3 * H // 2
A_OH = A_OHT
A_SK = A_OH + AS * (P // 2 + KW)
A_EV = A_ERS
A_ET = A_KRB
A_SELT = A_ET + 2 * 4 * P
A_S = A_BIG
A_FA = A_S + H * Q
A_BA = A_FA + H * Q
A_FL = A_BA + H * Q
A_ROW = A_FL + 4 * Q
A_FB = A_SEL
A_WOH = A_BIG
A_DA = A_WOH + NWOH * 64
A_ACC = A_DA + FR * (1 + H)
assert A_FB + FR * D <= A_SUM and A_SK + 2 * AU <= A_ERS
assert AS * KW <= STEPS * H
A_X = 0
A_XT = A_X + 2 * NP
A_B1 = A_XT + 2 * NP
A_B2 = A_B1 + NT * (D + 2 * H)
A_CH = A_B2 + 2 * NP
A_WT = A_CH + 2 * NW
A_REM = A_WT + 12 * D
A_BI = A_REM + D
A_END = A_BI + 4 * D
MW = 3 * D // 2
A_CNT = A_ACC + WINS * 64
assert A_CNT + 2 * NW <= A_END and A_B1 + R2 * NT * MW <= A_WT and A_B1 + NT * MW <= A_CH
MAX16 = 256
assert A_ACC + WINS * 64 <= A_BI and A_ROW + 5 * Q <= A_END and A_ERS + STEPS * H <= A_END


def build(nc, rec, x, xT, edge0, w0, a0l, a0r, cols, wrel, brow, wih, w1, w2, w3, b3, wp1, bp1, wl1, bl1, wr1, wp2, bp2, wl2, bl2, wr2,
          wt3, a3l, a3r, out):
    ctx = ExitStack()
    with ctx:
        sb = lambda n, s, d: ctx.enter_context(nc.sbuf_tensor(n, s, d))
        sem = lambda n: ctx.enter_context(nc.semaphore(n))

        feat_t = nc.dram_tensor("feat_table", (NP * R8, FW), F32).ap()
        rows_t = nc.dram_tensor("edge_rows", (TILES * P, D), F32).ap()
        key_t = nc.dram_tensor("step_keys", (SC * P, P), F16).ap()
        er_t = nc.dram_tensor("er_table", (NP * R8, H), F32).ap()
        xt_t = nc.dram_tensor("xt_table", (NP, D + 2 * H), F32).ap()
        sorted_t = nc.dram_tensor("sorted_records", (EP, 4), I32).ap()
        al_t = nc.dram_tensor("al_table", (NP, H), F32).ap()

        AR = sb("arena", [P, A_END], F32)
        ADJ = sb("adjacency", [P, R2, NW * SH], U16)
        ident = sb("ident", [P, P], F32)
        ones = sb("ones", [P, P], F32)
        ones16 = sb("ones16", [P, P], F16)
        iota128 = sb("iota128", [P, P], F16)
        iota480 = sb("iota480", [P, R2 * KW], F16)
        iota16 = sb("iota16", [P, WIN], F32)
        pcol = sb("pcol", [P, GR], F32)
        w16col = sb("w16col", [P, 1], F32)
        cnt = sb("cnt", [P, 2], F32)
        GI = sb("gather_idx", [P, 2, GB], I32)
        TCOL = sb("step_tile", [P, SC], F32)
        BC = sb("bias_cols", [P, 32], F32)
        ST = sb("ln_stats", [P, NT, 6], F32)
        MV = sb("ln_mean_var", [P, NT, 2], F32)
        RS = sb("ln_rstd", [P, NT], F32)
        RC = sb("recip_count", [P, NT], F32)
        E3 = sb("edge_ends", [P, 2, NT], I32)
        S3 = sb("scores3", [P, 3, NT * H], F32)
        SC16 = sb("edge_cols", [P, 2, H * GR], F32)
        SCOL = sb("step_times_128", [P, SC], F32)
        NXT = sb("next_tile", [P, GR, 4], I32)
        FLG = sb("unsorted_flag", [P, 1], I32)
        FLF = sb("unsorted_count", [P, 3], F32)
        RD = sb("lane_ends", [P, 2, GR * H], F32)
        PS = [ctx.enter_context(nc.psum_tensor(f"bank{i}", [P, 512], F32)) for i in range(8)]

        def ar(off, *dims, dt=None):
            n = 1
            for d in dims:
                n *= d
            v = AR[:, off:off + n]
            if len(dims) == 2:
                v = v.rearrange("p (a b) -> p a b", b=dims[1])
            elif len(dims) == 3:
                v = v.rearrange("p (a b c) -> p a b c", b=dims[1], c=dims[2])
            return v

        EARLY = ADJ[:, :, :].rearrange("p r k -> p (r k)").bitcast(F32)
        RL = EARLY[:, 0:4 * Q].bitcast(I32)
        RLv = RL.rearrange("p (n f) -> p n f", f=4)
        LI = EARLY[:, 4 * Q:5 * Q].bitcast(I32)
        LJ = EARLY[:, 5 * Q:6 * Q].bitcast(I32)
        IDm = EARLY[:, 7 * Q:8 * Q]
        AT = EARLY[:, 8 * Q:8 * Q + 4 * Q * 2].rearrange("p (a n) -> p a n", a=2)
        TMP = EARLY[:, 16 * Q:20 * Q]
        VL = EARLY[:, 20 * Q:20 * Q + 128].rearrange("p (k n) -> p k n", k=2)
        ELS = EARLY[:, 21 * Q:21 * Q + NT * 64].rearrange("p (t n) -> p t n", n=64)

        SB0 = 24 * Q
        DT = EARLY[:, SB0:SB0 + Q]
        DLO, DHI = EARLY[:, SB0 + Q:SB0 + 2 * Q], EARLY[:, SB0 + 2 * Q:SB0 + 3 * Q]
        RT = EARLY[:, SB0 + 3 * Q:SB0 + 7 * Q].bitcast(I32)
        LD = EARLY[:, SB0 + 7 * Q:SB0 + 8 * Q]
        OL, OLT, DGc, TRI, TRIT, JNK = (EARLY[:, SB0 + 8 * Q + P * j:SB0 + 8 * Q + P * (j + 1)] for j in range(6))
        JNK4 = EARLY[:, SB0 + 11 * Q:SB0 + 12 * Q]
        HI16 = EARLY[:, SB0 + 10 * Q:SB0 + 10 * Q + 16]
        CUR = EARLY[:, SB0 + 10 * Q + 16:SB0 + 10 * Q + 32]
        TOT = EARLY[:, SB0 + 10 * Q + 32:SB0 + 10 * Q + 48]
        RNK = EARLY[:, SB0 + 10 * Q + 48:SB0 + 10 * Q + 52]
        POS = EARLY[:, SB0 + 10 * Q + 52:SB0 + 10 * Q + 53].bitcast(I32)
        RS4 = EARLY[:, SB0 + 10 * Q + 56:SB0 + 10 * Q + 60].bitcast(I32)
        NTL = GR * P

        SLO, KEY, DJ, IDX, WS, IOT = (ar(o, STEPS) for o in (A_SLO, A_KEY, A_DJ, A_IDX, A_WS, A_IOT))
        OFF = ar(A_WI, STEPS).bitcast(I32)
        SEL = ar(A_SEL, GR, STEPS)
        Fl = ar(A_F, 4, Q)
        DST = Fl[:, 2, :].rearrange("p (g e) -> p g e", g=GR)
        SUM = ar(A_SUM, Q, H)
        ALS = ar(A_SUM, STEPS, H)
        DG = EARLY[:, 43 * Q:44 * Q]
        LKEY = EARLY[:, 44 * Q:44 * Q + GR * (P + 1)].rearrange("p (g e) -> p g e", g=GR)
        KEY16 = EARLY[:, 47 * Q:47 * Q + SC * P // 2].bitcast(F16).rearrange("p (c e) -> p c e", e=P)
        ERF = EARLY[:, 48 * Q:48 * Q + WINS * H].rearrange("p (w h) -> p w h", h=H)
        ERG = EARLY[:, 49 * Q:49 * Q + WINS * H].rearrange("p (w h) -> p w h", h=H)
        TI = ar(A_IDX, STEPS).bitcast(I32)
        OHS = [AR[:, A_OH + k * (P // 2 + KW):A_OH + k * (P // 2 + KW) + P // 2].bitcast(F16) for k in range(AS)]
        OHK = [AR[:, A_OH + k * (P // 2 + KW) + P // 2:A_OH + (k + 1) * (P // 2 + KW)].bitcast(F16) for k in range(AS)]
        EV = [AR[:, A_EV + k * KW:A_EV + (k + 1) * KW].bitcast(U16).rearrange("p (r k) -> p r k", r=R2) for k in range(AS)]
        W0 = ar(A_W0, 2, R8 * D)
        XT0 = ar(A_XT0, 2, NP)
        FS = ar(A_FS, 4, 512)
        IE = ar(A_IE, Q)
        RING = ar(A_RING, 2 * GB, FW)
        KRB = [AR[:, A_KRB + k * CK * P // 2:A_KRB + (k + 1) * CK * P // 2].bitcast(F16) for k in range(2)]
        OHT = [AR[:, A_OHT + k * CK * P // 2:A_OHT + (k + 1) * CK * P // 2].bitcast(F16) for k in range(2)]
        ERW = AR[:, A_ERW:A_ERS].bitcast(BF16)
        ERWv = ERW.rearrange("p (w q h) -> p w q h", q=3, h=H)
        ERS, ERSf = ar(A_ERS, STEPS, H), ar(A_ERS, STEPS * H)
        ET, SELT = ar(A_ET, 2, 4 * P), ar(A_SELT, 2, 4 * P)
        S, FA, BA = ar(A_S, H, Q), ar(A_FA, H, Q), ar(A_BA, H, Q)
        FL = ar(A_FL, 4, Q)
        ROW = ar(A_ROW, 5, Q)
        FB = ar(A_FB, FR, D)
        WOH = ar(A_WOH, NWOH, 64)
        SK = ar(A_SK, 2, AU)
        SLO_KEY = ar(A_SLO, 2, STEPS)
        DJT, ALT = ar(A_DA, FR), ar(A_DA + FR, FR * H)
        ACC = ar(A_ACC, WINS, 64)
        ACCf = ar(A_ACC, WINS * 64)
        ALSf = ar(A_SUM, STEPS * H)
        X, XT = ar(A_X, NT, D), ar(A_XT, 2, NP)
        B1, B2 = ar(A_B1, NT, D), ar(A_B2, NT, D)
        MT = [AR[:, A_B1 + MW * i:A_B1 + MW * (i + 1)] for i in range(R2 * NT)]
        CNTS, CNT2 = ar(A_CNT, NW), ar(A_CNT + NW, NW)

        def parts(i):
            return [MT[i].bitcast(BF16)[:, D * q:D * (q + 1)] for q in range(3)]

        def chunk(at, k, wide):
            if wide:
                return AR[:, at + k * NW:at + (k + 1) * NW]
            return AR[:, at + k * NW // 2:at + (k + 1) * NW // 2].bitcast(BF16)

        REM = ar(A_REM, D)
        CH1, CH2 = A_XT, A_CH
        XT3 = ar(A_B1, NT, D + 2 * H)
        G3 = ar(A_B2, NT, D + 2 * H)
        AG3 = ar(A_B2 + NT * (D + 2 * H), NT, H)
        T64 = ar(A_XT, NT, HD)
        B2T = ar(A_B2, 2, NP)
        CH = ar(A_CH, 2, NW)
        HC = [ar(A_WT + 1024 + k * 2 * CN, 2, CN) for k in range(2)]
        WREL = ar(A_WT, 2 * R2, D).rearrange("p (k r) n -> p k r n", k=2)
        WIH = ar(A_WT + 1024, 2, 3 * D)
        W1s, W2s, W3s = ar(A_WT + 2560, 2, P), ar(A_WT + 2816, P), ar(A_WT + 2944, D)
        W2L = [ar(A_WT + 512 * i, 2, D) for i in range(6)]
        WT3 = ar(A_WT, 2, D + 2 * H)
        A3 = ar(A_WT + 528, 2, D)
        TMP3 = ar(A_WT + 1040, D)
        BROW = ar(A_BI, 4 * D)
        BPF = AR[:, A_BI:A_BI + 2 * D].bitcast(BF16)
        BP = BPF.rearrange("p (b n) -> p b n", n=D)
        BHI, BMID, BLO = (AR[:, A_CH + 2 * D * j:A_CH + 2 * D * (j + 1)].bitcast(BF16) for j in range(3))
        BREM = ar(A_CH + 6 * D, 4 * D)
        GT = ar(A_B1, 6, CN)
        CC, HN, X1, X2 = ar(A_B1 + 6 * CN, 2, CN), ar(A_B1 + 8 * CN, 2, CN), ar(A_B1 + 10 * CN, CN), ar(A_B1 + 11 * CN, CN)

        names = """bias_ready turn_cols kb_mm ld_rec ld_w0 ld_xt ld_at ld_e3 consts fields idx_mm idx_ev vl_done tab_mm tab_ev tab_st feat_mm
            feat_ev diag_done bc_mm cmp_done ws_mm sel_ready fld_mm fld_ev steps_done a_oh a_mm a_ev a_add
            pool_link lane_mm lane_ev flags_in flags_mm tail_ready tail_mm cin_ready cin_mm exp_ready exp_done
            alpha_ready als_mm als_ev r_all off_acc l_woh l_mm l_acc ld_x ld_bc ld_wt1 ht_ready ht_mm ht_add
            var_ready std_ready ln_done xt_mm xt_eva xt_evd h_mm h_ev m_mm m_ev chunk_ready chunk_used agg_eva
            agg_evd gate_mm gate_ev c_ready tc_ready hn_ready x1_mm x1_ev x2_mm x2_ev x3_mm x3_add ld_wt2 ld_wt3
            p_mm p_ev hi_ready cnt_mm o_mm o_ready nrm_done h_ready pool_gate vl3_done t_mm t_ev t_st key_mm
            key_ev key_st er_st er_ld erw_ready oht er_mm er_red et_mm et_ev selt sc_mm flag_cmp flag_mm
            flag_ready srt_oh srt_hist srt_add srt_pre srt_a srt_b srt_c srt_d srt_e srt_put srt_link
            srt_in srt_t srt_tv ld_sorted g3 s3_ready s3_exp out_st dve_link""".split()
        s = {n: sem(n) for n in names}
        fs_st = [sem(f"feat_stored{i}") for i in range(4)]
        g_done = [sem(f"scores_gathered{i}") for i in range(2)]
        f_done = [sem(f"rows_loaded{i}") for i in range(FR)]
        r_st = [sem(f"rows_stored{i}") for i in range(2)]
        k_ld = [sem(f"keys_loaded{i}") for i in range(2)]

        def offsets(engine, step, n, most):
            return nc.values_load_multi_w_load_instructions(
                (TI if engine == SP else OFF)[0:1, bass.ds(step, n)],
                engines=[engine], min_val=0, max_val=most,
                skip_runtime_bounds_check_because="window and tile numbers of the walk stay in range for any sorted edges")[1]

        block = ctx.enter_context(nc.Block())

        @block.sync
        def _(sp):
            sp.dma_start(RL.rearrange("p (g n) -> p g n", g=GR),
                         rec[0:EP, :].rearrange("(g t e) f -> t g (e f)", g=GR, t=P)).then_inc(s["ld_rec"], 16)
            sp.dma_start(NXT[:, :, :], rec[P:P + EP, :].rearrange("(g t e) f -> t g e f", g=GR, t=P)[:, :, 0, :])\
              .then_inc(s["ld_rec"], 16)
            sp.dma_start(W0, w0.rearrange("(k p) n -> p k n", k=2)).then_inc(s["ld_w0"], 16)
            sp.dma_start(AT[:, 0, :], a0l.broadcast_to([P, R8 * D])).then_inc(s["ld_at"], 16)
            sp.dma_start(AT[:, 1, :], a0r.broadcast_to([P, R8 * D])).then_inc(s["ld_at"], 16)
            sp.dma_start(XT0, xT.rearrange("(k p) n -> p k n", k=2)).then_inc(s["ld_xt"], 16)
            sp.dma_start(E3[:, :, :], edge0).then_inc(s["ld_e3"], 16)
            sp.dma_start(BC[:, 0:20], cols).then_inc(s["ld_bc"], 16)
            sp.wait_ge(s["flag_ready"], 1)
            unsorted = sp.value_load(FLG[0:1, 0:1], min_val=0, max_val=EP)
            with sp.If(unsorted >= 1):
                sp.dma_start(RT.rearrange("p (t f) -> p t f", f=4),
                             rec[0:EP, :].rearrange("(t e) f -> e t f", e=P)).then_inc(s["srt_in"], 16)
            ftr = feat_t.rearrange("(t p r) d -> t p r d", p=P, r=R8)

            def store_scores():
                sp.wait_ge(s["tab_ev"], 2)
                sp.dma_start(er_t.rearrange("(t p r) h -> p t (r h)", p=P, r=R8), ELS[:, :, 32:64]).then_inc(s["er_st"], 16)
                for t in range(NT):
                    sp.dma_start(ftr[t, :, :, D:FW], ELS[:, t, 0:32].rearrange("p (r h) -> p r h", h=H)).then_inc(s["tab_st"], 16)

            for i in range(NT * 4):
                if i == TABS_AT - 2:
                    store_scores()
                sp.wait_ge(s["feat_ev"], i + 1)
                c = i % 4
                sp.dma_start(ftr[i // 4, :, 2 * c:2 * c + 2, 0:D], FS[:, c, :].rearrange("p (r d) -> p r d", d=D))\
                  .then_inc(fs_st[c], 16)
            rows_b = rows_t.rearrange("(t p) d -> p t d", p=P)

            def store(k, tiles):
                sp.dma_start(rows_b[:, tiles, :], RING[:, GB * k:GB * (k + 1), 0:D]).then_inc(r_st[k], 16)

            with sp.Fori(0, (NGB - 1) // 2) as i:
                for k in range(2):
                    sp.wait_ge(g_done[k], i * BATCH + BATCH)
                    store(k, bass.ds(i * (2 * GB) + GB * k, GB))
            sp.wait_ge(g_done[0], ((NGB - 1) // 2 + 1) * BATCH)
            store(0, slice(GB * (NGB - 1), TILES))
            for k in range(2):
                sp.wait_ge(r_st[k], 16 * ((NGB + 1 - k) // 2))
            sp.wait_ge(s["als_mm"], H)

            def load(slot, first_edge):
                sp.dma_start(FB[:, slot, :], rows_t[bass.ds(first_edge, P), :]).then_inc(f_done[slot], 16)

            edges = offsets(SP, 0, HEAD + FR, (TILES - 1) * P)
            for st in range(HEAD + FR):
                if st >= FR:
                    sp.wait_ge(s["l_mm"], st - FR + 1)
                load(st % FR, edges[st])
            with sp.Fori(0, GRPS - 1) as i:
                edges = offsets(SP, i * FR + (HEAD + FR), FR, (TILES - 1) * P)
                for u in range(FR):
                    st = HEAD + FR + u
                    sp.wait_ge(s["l_mm"], i * FR + (st - FR + 1))
                    load(st % FR, edges[u])
            sp.wait_ge(s["l_acc"], STEPS + 1)
            sp.wait_ge(s["ht_ready"], 1)
            sp.wait_ge(s["cnt_mm"], 1)
            sp.dma_start(X[:, 0:NT - 1, :], x[0:(NT - 1) * P, :].rearrange("(t p) d -> p t d", p=P)).then_inc(s["ld_x"], 16)
            sp.dma_start(X[0:NLAST, NT - 1, :], x[(NT - 1) * P:N, :]).then_inc(s["ld_x"], 16)
            for r in range(R2):
                sp.dma_start(WREL[:, :, r, :], wrel[r, :, :].rearrange("(k p) n -> p k n", k=2)).then_inc(s["ld_wt1"], 16)
            for i, b in enumerate((brow[0:1, :], brow[1:2, :], b3)):
                sp.dma_start(BROW[0:3, D * i:D * (i + 1)], b.broadcast_to([3, D])).then_inc(s["ld_wt1"], 16)
            sp.wait_ge(s["m_ev"], 3 * R2 * NC)
            sp.wait_ge(s["ld_wt1"], 16 * 5)
            sp.dma_start(WIH, wih.rearrange("(k p) n -> p k n", k=2)).then_inc(s["ld_wt1"], 16)
            sp.dma_start(W1s, w1.rearrange("(k p) n -> p k n", k=2)).then_inc(s["ld_wt1"], 16)
            sp.dma_start(W2s, w2).then_inc(s["ld_wt1"], 16)
            sp.dma_start(W3s, w3).then_inc(s["ld_wt1"], 16)
            sp.wait_ge(s["x3_mm"], NC)
            for i, w in enumerate((wp1, wl1, wr1, wp2, wl2, wr2)):
                sp.dma_start(W2L[i], w.rearrange("(k p) n -> p k n", k=2)).then_inc(s["ld_wt2"], 16)
            for i, b in enumerate((bp1, bl1, bp2, bl2)):
                sp.dma_start(BROW[0:3, D * i:D * (i + 1)], b.broadcast_to([3, D])).then_inc(s["ld_wt2"], 16)
            sp.wait_ge(s["o_mm"], 2 * NT)
            sp.dma_start(WT3[:, :, 0:D], wt3.rearrange("(k p) n -> p k n", k=2)).then_inc(s["ld_wt3"], 16)
            sp.dma_start(A3[:, 0, :], a3l.broadcast_to([P, D])).then_inc(s["ld_wt3"], 16)
            sp.dma_start(A3[:, 1, :], a3r.broadcast_to([P, D])).then_inc(s["ld_wt3"], 16)
            for t0, t1 in GROUPS:
                sp.wait_ge(s["t_ev"], t1)
                sp.dma_start(xt_t.rearrange("(t p) n -> p t n", p=P)[:, t0:t1, :], XT3[:, t0:t1, :]).then_inc(s["t_st"], 16)
                sp.dma_start(al_t.rearrange("(t p) n -> p t n", p=P)[:, t0:t1, :], XT3[:, t0:t1, D:D + H])\
                  .then_inc(s["t_st"], 16)
            for q, (t0, t1) in enumerate(GROUPS):
                sp.wait_ge(s["ln_done"], 3 * len(GROUPS) + q + 1)
                t1 = min(t1, NT - 1)
                sp.dma_start(out[t0 * P:t1 * P, :].rearrange("(t p) d -> p t d", p=P), X[:, t0:t1, :]).then_inc(s["out_st"], 16)
            sp.dma_start(out[(NT - 1) * P:N, :], X[0:NLAST, NT - 1, :]).then_inc(s["out_st"], 16)
            sp.wait_ge(s["out_st"], 16 * (len(GROUPS) + 1))

        @block.gpsimd
        def _(pool):
            g = nc.gpsimd
            g.memset(ident[:, :], 0.0).then_inc(s["pool_link"], 1)
            g.memset(ones[:, :], 1.0)
            g.memset(ones16[:, :], 1.0)
            pool.wait_ge(s["pool_link"], 1)
            g.affine_select(out=ident[:, :], in_=ident[:, :], compare_op=ALU.not_equal, fill=1.0, base=0,
                            pattern=[[-1, P]], channel_multiplier=1)
            g.iota(iota128[:, :], pattern=[[1, P]], base=0, channel_multiplier=0, allow_small_or_imprecise_dtypes=True)
            g.iota(iota480[:, :], pattern=[[1, R2 * KW]], base=0, channel_multiplier=0, allow_small_or_imprecise_dtypes=True)
            g.iota(iota16[:, :], pattern=[[1, WIN]], base=0, channel_multiplier=0, allow_small_or_imprecise_dtypes=True)
            g.iota(IOT, pattern=[[1, STEPS]], base=0, channel_multiplier=0, allow_small_or_imprecise_dtypes=True)
            g.iota(pcol[:, :], pattern=[[P, GR]], base=0, channel_multiplier=1, allow_small_or_imprecise_dtypes=True)
            g.iota(w16col[:, :], pattern=[[0, 1]], base=0, channel_multiplier=WIN, allow_small_or_imprecise_dtypes=True)\
             .then_inc(s["consts"], 1)

            pool.wait_ge(s["flag_ready"], 1)
            unsorted = pool.value_load(FLG[0:1, 0:1], min_val=0, max_val=EP)
            with pool.If(unsorted >= 1):
                g.memset(TRI, 1.0).then_inc(s["srt_t"], 1)
                g.memset(TRIT, 1.0).then_inc(s["srt_t"], 1)
                pool.wait_ge(s["srt_t"], 2)
                g.affine_select(out=TRI, in_=TRI, compare_op=ALU.is_gt, fill=0.0, base=0,
                                pattern=[[-1, P]], channel_multiplier=1)
                g.affine_select(out=TRIT, in_=TRIT, compare_op=ALU.is_gt, fill=0.0, base=0,
                                pattern=[[1, P]], channel_multiplier=-1).then_inc(s["srt_tv"], 1)
                with pool.Fori(0, NTL) as i:
                    pool.wait_ge(s["srt_e"], i + 1)
                    pool.sem_inc(s["pool_gate"], 1)
                    g.indirect_dma_start(out=sorted_t, out_offset=bass.IndirectOffsetOnAxis(ap=POS, axis=0),
                                         in_=RS4, in_offset=None).then_inc(s["srt_put"], 16)
                pool.wait_ge(s["srt_put"], 16 * NTL)
                pool.dma_start(RL.rearrange("p (g n) -> p g n", g=GR),
                               sorted_t.rearrange("(g t e) f -> t g (e f)", g=GR, t=P)).then_inc(s["ld_sorted"], 16)

            pool.wait_ge(s["er_st"], 16)
            pool.dma_start(ERF, er_t[0:NW * R8, :].rearrange("(w c) h -> c w h", c=P)).then_inc(s["er_ld"], 16)
            pool.wait_ge(s["key_ev"], SC)
            pool.dma_start(key_t.rearrange("(c p) e -> p c e", p=P), KEY16).then_inc(s["key_st"], 16)

            def issue(k, cols):
                g.tensor_copy(GI[:, k, :], IE[:, cols]).then_inc(s["pool_link"], 1)

            def gathers(k):
                for j in range(GB):
                    g.indirect_dma_start(out=RING[:, GB * k + j, :], out_offset=None, in_=feat_t,
                                         in_offset=bass.IndirectOffsetOnAxis(ap=GI[:, k, j:j + 1], axis=0))\
                     .then_inc(g_done[k], 16)

            def collect(k, cols):
                g.tensor_copy(SUM[:, cols, :], RING[:, GB * k:GB * (k + 1), D:FW]).then_inc(s["pool_link"], 1)

            g.memset(SUM[:, TILES:Q, :], 0.0).then_inc(s["pool_link"], 1)
            pool.wait_ge(s["idx_ev"], 1)
            pool.wait_ge(s["tab_st"], 16 * NT)
            for i in range(4):
                pool.wait_ge(fs_st[i], NT * 16)
            for b in range(2):
                issue(b, slice(GB * b, GB * (b + 1)))
                pool.wait_ge(s["pool_link"], 3 + b)
                gathers(b)
            with pool.Fori(0, N_IT) as i:
                for k in range(2):
                    pool.wait_ge(g_done[k], i * BATCH + BATCH)
                    pool.sem_inc(s["pool_gate"], 1)
                    collect(k, bass.ds(i * (2 * GB) + GB * k, GB))
                    issue(k, bass.ds(i * (2 * GB) + GB * (k + 2), GB))
                    pool.wait_ge(r_st[k], i * 16 + 16)
                    pool.sem_inc(s["pool_gate"], 1)
                    pool.wait_ge(s["pool_link"], i * 4 + (6 + 2 * k))
                    pool.sem_inc(s["pool_gate"], 1)
                    gathers(k)
            last = NGB - 1
            pool.wait_ge(g_done[0], (N_IT + 1) * BATCH)
            collect(0, slice(GB * (last - 2), GB * (last - 1)))
            issue(0, slice(GB * last, GB * NGB))
            pool.wait_ge(r_st[0], 16 * (N_IT + 1))
            pool.wait_ge(s["pool_link"], LINKS - 2)
            gathers(0)
            pool.wait_ge(g_done[1], (N_IT + 1) * BATCH)
            collect(1, slice(GB * (last - 1), GB * last))
            pool.wait_ge(g_done[0], (N_IT + 2) * BATCH)
            collect(0, slice(GB * last, GB * NGB))

            pool.wait_ge(s["a_add"], STEPS + 1)
            pool.wait_ge(s["l_acc"], 1)
            cols = [ADJ[:, r, :].rearrange("p (n s) -> p n s", s=SH)[:, :, c] for r in range(R2) for c in range(SH)]
            for c in range(R2 * SH):
                g.tensor_copy(CNT2 if c else CNTS, cols[c]).then_inc(s["pool_link"], 1)
                pool.wait_ge(s["pool_link"], LINKS + max(1, 2 * c))
                if c:
                    g.tensor_tensor(CNTS, CNTS, CNT2, ALU.add).then_inc(s["pool_link"], 1)
                    pool.wait_ge(s["pool_link"], LINKS + 2 * c + 1)

            pool.wait_ge(s["ld_e3"], 16)
            pool.wait_ge(s["t_st"], 32 * len(GROUPS))
            for t in range(NT):
                g.indirect_dma_start(out=AG3[:, t, :], out_offset=None, in_=al_t,
                                     in_offset=bass.IndirectOffsetOnAxis(ap=E3[:, 0, t:t + 1], axis=0)).then_inc(s["g3"], 16)
                g.indirect_dma_start(out=G3[:, t, :], out_offset=None, in_=xt_t,
                                     in_offset=bass.IndirectOffsetOnAxis(ap=E3[:, 1, t:t + 1], axis=0)).then_inc(s["g3"], 16)

        @block.scalar
        def _(act):
            a = nc.scalar
            for i in range(NT * 4):
                act.wait_ge(s["feat_mm"], i + 1)
                if i >= 4:
                    act.wait_ge(fs_st[i % 4], 16 * (i // 4))
                a.activation(FS[:, i % 4, :], PS[i % 4][:, :], ACT.Copy).then_inc(s["feat_ev"], 1)
            for i in range(4):
                act.wait_ge(fs_st[i], NT * 16)
            act.wait_ge(s["feat_mm"], NT * 4)
            act.wait_ge(s["key_st"], 16)
            key_row = key_t.rearrange("(a s) e -> a (s e)", a=1)

            def load_keys(k, at):
                act.dma_start(KRB[k][0:1, :], key_row[:, bass.ds(at * P, CK * P)]).then_inc(k_ld[k], 16)

            for k in range(2):
                load_keys(k, CK * k)
            act.wait_ge(s["tab_st"], 16 * NT)
            act.wait_ge(s["er_st"], 16)
            act.wait_ge(s["erw_ready"], 1)
            ZN = NW * SH * R2 // 2
            ZW = ZN // ER_N

            def zero(at, n):
                return a.activation(EARLY[:, at if n is None else bass.ds(at, n)], ones[:, 0:1].to_broadcast([P, n or ZN - ER_N * ZW]),
                                    ACT.Copy, scale=0.0)

            with act.Fori(0, ER_N) as i:
                zero(i * ZW, ZW)
                for k in range(2):
                    act.wait_ge(s["kb_mm"], i * 4 + (2 + 2 * k))
                    load_keys(k, i * (2 * CK) + CK * (2 + k))
            act.wait_ge(s["kb_mm"], 2 * NCK - 2)
            load_keys(0, CK * NCK)
            zero(slice(ER_N * ZW, ZN), None).then_inc(s["a_add"], 1)
            for c in range(SC):
                act.wait_ge(s["et_mm"], c + 1)
                if c >= 2:
                    act.wait_ge(s["sc_mm"], c - 1)
                n = min(P, STEPS - P * c)
                a.activation(ET[0:n, c % 2, :], PS[4 + c % 2][0:n, :], ACT.Copy).then_inc(s["et_ev"], 1)
            def a_evac(i, st):
                act.wait_ge(s["a_mm"], i * AU + (st + 1))
                a.activation(EV[st % AS].rearrange("p r k -> p (r k)"), PS[4 + st % 4][:, 0:R2 * KW], ACT.Copy)\
                 .then_inc(s["a_ev"], 1)

            for st in range(AS):
                a_evac(0, st)
            with act.Fori(0, A_N) as i:
                for u in range(AU):
                    a_evac(i, AS + u)
            for st in range(AS + A_N * AU, STEPS):
                a_evac(0, st)
            act.wait_ge(s["r_all"], 1)
            for g in range(GR):
                act.wait_ge(s["lane_mm"], g + 1)
                a.activation(S[:, :, P * g:P * (g + 1)], PS[g][:, :].rearrange("p (h e) -> p h e", h=H), ACT.Copy)\
                 .then_inc(s["lane_ev"], 1)
            act.wait_ge(s["exp_ready"], 1)
            a.activation(S.rearrange("p h n -> p (h n)"), S.rearrange("p h n -> p (h n)"), ACT.Exp).then_inc(s["exp_done"], 1)
            for h in range(H):
                act.wait_ge(s["als_mm"], h + 1)
                a.activation(ALS[:, 0:512, h], PS[2 * h][:, 0:512], ACT.Copy)
                a.activation(ALS[:, 512:STEPS, h], PS[2 * h + 1][:, 0:STEPS - 512], ACT.Copy).then_inc(s["als_ev"], 1)
            def ln_sqrt(n):
                act.wait_ge(s["var_ready"], n)
                a.activation(RS[:, :], MV[:, :, 1], ACT.Sqrt).then_inc(s["std_ready"], 1)

            def xt_evac(n):
                for q in range(4):
                    act.wait_ge(s["xt_mm"], 8 * n + 2 * q + 1)
                    w = min(512, NP - 512 * q)
                    a.activation(XT[:, 0, 512 * q:512 * q + w], PS[2 * q][:, 0:w], ACT.Copy).then_inc(s["xt_eva"], 1)

            ln_sqrt(1)
            xt_evac(0)
            act.wait_ge(s["ld_bc"], 16)

            def message(n, bank, wide):
                dst = MT[n % (R2 * NT)][:, 0:D] if wide else parts(n % (R2 * NT))[0]
                a.activation(dst, PS[bank][:, 0:D], ACT.Relu).then_inc(s["hi_ready"], 1)

            def messages1(wide):
                for i in range(R2 * NC + 1):
                    if i < R2 * NC:
                        if i >= 2:
                            act.wait_ge(s["m_mm"], 3 * (i - 1))
                        for fo in range(2):
                            act.wait_ge(s["h_mm"], 2 * i + fo + 1)
                            b = 2 + 2 * (i // NC) + fo
                            a.activation(HC[i % 2][:, fo, :], PS[2 * (i % 2) + fo][:, 0:CN], ACT.Relu,
                                         bias=BC[:, b:b + 1]).then_inc(s["h_ev"], 1)
                    if i:
                        for j in range(3):
                            act.wait_ge(s["m_mm"], 3 * (i - 1) + j + 1)
                            message(3 * (i - 1) + j, 4 + j, wide)
                act.wait_ge(s["m_mm"], 3 * R2 * NC)
                for c in range(R2 * SH):
                    r, sh = c // SH, c % SH
                    if c >= 2:
                        act.wait_ge(s["chunk_used"], c - 1)
                    a.activation(chunk(CH1, c % 2, wide), ADJ[:, r, :].rearrange("p (n s) -> p n s", s=SH)[:, :, sh],
                                 ACT.Copy).then_inc(s["chunk_ready"], 1)

            act.wait_ge(s["flag_ready"], 2)
            large = act.value_load(FLG[0:1, 0:1], min_val=0, max_val=P)
            with act.If(large < 1):
                messages1(False)
            with act.If(large >= 1):
                messages1(True)

            def agg_evac(dst, total):
                act.wait_ge(s["chunk_used"], total)
                for j in range(4):
                    a.activation(dst[:, 1, CW * j:CW * (j + 1)], PS[4 + j][:, 0:CW], ACT.Copy).then_inc(s["agg_eva"], 1)

            agg_evac(XT, R2 * SH)
            funcs = (ACT.Sigmoid, ACT.Sigmoid, ACT.Tanh, ACT.Tanh, ACT.Sigmoid, ACT.Sigmoid)
            for c in range(NC):
                for j in range(6):
                    act.wait_ge(s["gate_mm"], 6 * c + j + 1)
                    if j == 0 and c:
                        act.wait_ge(s["hn_ready"], c)
                    a.activation(GT[:, j, :], PS[j][:, 0:CN], funcs[j], bias=BC[:, 20 + j:21 + j]).then_inc(s["gate_ev"], 1)
                act.wait_ge(s["c_ready"], c + 1)
                a.activation(CC, CC, ACT.Tanh).then_inc(s["tc_ready"], 1)
                act.wait_ge(s["x1_mm"], c + 1)
                a.activation(X1, PS[6][:, 0:CN], ACT.Relu, bias=BC[:, 18:19]).then_inc(s["x1_ev"], 1)
                act.wait_ge(s["x2_mm"], c + 1)
                a.activation(X2, PS[7][:, 0:CN], ACT.Relu, bias=BC[:, 19:20]).then_inc(s["x2_ev"], 1)
            ln_sqrt(2)
            xt_evac(1)
            for v in range(2):
                def messages2(wide):
                    for t in range(NT):
                        act.wait_ge(s["p_mm"], NT * v + t + 1)
                        message(t, t % 4, wide)

                with act.If(large < 1):
                    messages2(False)
                with act.If(large >= 1):
                    messages2(True)
                agg_evac(B2T, (R2 + 1 + v) * SH)
                act.wait_ge(s["o_ready"], NT * (v + 1))
                a.activation(RS[:, :], RS[:, :], ACT.Sqrt).then_inc(s["nrm_done"], 1)
                if v == 0:
                    xt_evac(2)
            ln_sqrt(3)
            xt_evac(3)
            for t in range(NT):
                act.wait_ge(s["t_mm"], t + 1)
                a.activation(XT3[:, t, :], PS[t % 4][:, 0:D + 2 * H], ACT.Copy).then_inc(s["t_ev"], 1)
            act.wait_ge(s["s3_ready"], 1)
            a.activation(S3[:, 0, :], S3[:, 0, :], ACT.Exp).then_inc(s["s3_exp"], 1)
            ln_sqrt(4)

        @block.vector
        def _(dve):
            v = nc.vector
            chain = [0]

            def link(ins):
                chain[0] += 1
                ins.then_inc(s["dve_link"], 1)
                dve.wait_ge(s["dve_link"], chain[0])

            LDv = LD.rearrange("p (g e) -> p g e", g=GR)
            LIf = EARLY[:, 7 * Q:8 * Q].rearrange("p (g e) -> p g e", g=GR)

            def sort_records():
                n = [0]

                def slink(ins):
                    n[0] += 1
                    ins.then_inc(s["srt_link"], 1)
                    dve.wait_ge(s["srt_link"], n[0])

                v.tensor_copy(DT[:, 0:1], FLF[:, 0:1]).then_inc(s["srt_a"], 1)
                dve.wait_ge(s["srt_pre"], 1)
                slink(v.tensor_copy(DT, PS[1][:, :]))
                DTi = JNK4.bitcast(I32)
                slink(v.tensor_copy(DTi, DT))
                slink(v.tensor_single_scalar(LI, DTi, P - 1, ALU.bitwise_and))
                slink(v.tensor_single_scalar(LJ, DTi, 7, ALU.arith_shift_right))
                v.tensor_copy(DLO, LI)
                slink(v.tensor_copy(DHI, LJ))
                slink(v.memset(CUR, 0.0))
                dve.wait_ge(s["consts"], 1)
                with dve.Fori(0, NTL) as i:
                    v.tensor_scalar(OL, iota128[:, :], DLO[:, bass.ds(i, 1)], None, ALU.is_equal)
                    v.tensor_scalar(HI16, iota16[:, :], DHI[:, bass.ds(i, 1)], None, ALU.is_equal).then_inc(s["srt_oh"], 1)
                    dve.wait_ge(s["srt_hist"], i + 1)
                    v.tensor_tensor(CUR, CUR, PS[3][:, 0:16], ALU.add).then_inc(s["srt_add"], 1)
                    dve.wait_ge(s["srt_add"], i + 1)
                v.tensor_copy(TOT, CUR).then_inc(s["srt_a"], 1)
                dve.wait_ge(s["srt_pre"], 2)
                slink(v.tensor_copy(TOT, PS[1][:, 0:16]))
                slink(v.memset(JNK[:, 0:16], 1.0))
                slink(v.tensor_tensor_scan(JNK[:, 16:32], JNK[:, 0:16], TOT, 0.0, ALU.mult, ALU.add))
                slink(v.tensor_tensor(JNK[:, 16:32], JNK[:, 16:32], TOT, ALU.subtract))
                slink(v.tensor_tensor(CUR, JNK[:, 16:32], PS[2][:, 0:16], ALU.add))
                dve.wait_ge(s["srt_in"], 16)
                dve.wait_ge(s["srt_tv"], 1)
                K = 3
                base = n[0]
                with dve.Fori(0, NTL) as i:
                    col = bass.ds(i, 1)
                    v.tensor_scalar(OL, iota128[:, :], DLO[:, col], None, ALU.is_equal)
                    v.tensor_scalar(HI16, iota16[:, :], DHI[:, col], None, ALU.is_equal)
                    v.tensor_scalar(DGc, ident[:, :], DT[:, col], None, ALU.mult).then_inc(s["srt_oh"], 1)
                    dve.wait_ge(s["srt_b"], i + 1)
                    v.tensor_copy(OLT, PS[2][:, 0:P]).then_inc(s["srt_c"], 1)
                    v.tensor_scalar(JNK, PS[1][:, 0:P], DT[:, col], None, ALU.is_equal).then_inc(s["srt_link"], 1)
                    dve.wait_ge(s["srt_link"], i * K + (base + 1))
                    v.tensor_tensor(JNK, JNK, TRI, ALU.mult).then_inc(s["srt_link"], 1)
                    dve.wait_ge(s["srt_link"], i * K + (base + 2))
                    v.tensor_reduce(RNK[:, 0:1], JNK, AX.X, ALU.add)
                    dve.wait_ge(s["srt_d"], i + 1)
                    v.tensor_tensor(JNK4[:, 0:16], PS[0][:, 0:16], HI16, ALU.mult).then_inc(s["srt_link"], 1)
                    dve.wait_ge(s["srt_link"], i * K + (base + 3))
                    v.tensor_reduce(RNK[:, 1:2], JNK4[:, 0:16], AX.X, ALU.add).then_inc(s["srt_add"], 1)
                    dve.wait_ge(s["srt_add"], i * 2 + (NTL + 1))
                    v.tensor_copy(RS4, RT[:, bass.ds(i * 4, 4)])
                    v.tensor_tensor(POS, RNK[:, 0:1], RNK[:, 1:2], ALU.add).then_inc(s["srt_e"], 1)
                    v.tensor_tensor(CUR, CUR, PS[3][:, 0:16], ALU.add).then_inc(s["srt_add"], 1)
                    dve.wait_ge(s["srt_add"], i * 2 + (NTL + 2))
                    dve.wait_ge(s["srt_put"], i * 16 + 16)
                dve.wait_ge(s["ld_sorted"], 16)

            dve.wait_ge(s["ld_rec"], 32)
            dst_i = RLv[:, :, 1].rearrange("p (g e) -> p g e", g=GR)
            v.tensor_copy(LDv, dst_i)
            link(v.tensor_tensor(LIf[:, :, 0:P - 1], dst_i[:, :, 0:P - 1], dst_i[:, :, 1:P], ALU.is_gt))
            link(v.tensor_tensor(LIf[:, :, P - 1], dst_i[:, :, P - 1], NXT[:, :, 1], ALU.is_gt))
            v.tensor_reduce(FLF[:, 0:1], LIf.rearrange("p g e -> p (g e)"), AX.X, ALU.add).then_inc(s["flag_cmp"], 1)
            dve.wait_ge(s["flag_mm"], 1)
            v.tensor_copy(FLG[:, 0:1], PS[0][:, 0:1]).then_inc(s["flag_ready"], 1)
            dve.wait_ge(s["flag_ready"], 1)
            unsorted = dve.value_load(FLG[0:1, 0:1], min_val=0, max_val=EP)
            with dve.If(unsorted >= 1):
                sort_records()
            v.tensor_single_scalar(LI, RLv[:, :, 0], P - 1, ALU.bitwise_and)
            link(v.tensor_single_scalar(LJ, RLv[:, :, 0], 7, ALU.arith_shift_right))
            v.tensor_copy(Fl[:, 0, :], LI)
            v.scalar_tensor_tensor(Fl[:, 1, :], RLv[:, :, 2], float(KW), LJ, ALU.mult, ALU.add)
            v.tensor_copy(Fl[:, 2, :], RLv[:, :, 1])
            link(v.scalar_tensor_tensor(IDm, RLv[:, :, 1], float(R8), RLv[:, :, 3], ALU.mult, ALU.add))
            dve.wait_ge(s["consts"], 1)
            for g in range(GR):
                v.tensor_scalar(LKEY[:, g, P:P + 1], pcol[:, g:g + 1], float(P), None, ALU.mult)
            link(v.memset(cnt[:, 0:1], 0.0))
            for g in range(GR):
                v.tensor_scalar(LKEY[:, g, 0:P], IDm[:, P * g:P * (g + 1)], LKEY[:, g, P:P + 1], None, ALU.add)
            v.scalar_tensor_tensor(Fl[:, 3, :], RLv[:, :, 0], float(R8), RLv[:, :, 3], ALU.mult, ALU.add)\
             .then_inc(s["fields"], 1)
            dve.wait_ge(s["idx_mm"], 1)
            v.tensor_copy(IE, PS[4][:, :]).then_inc(s["idx_ev"], 1)
            dve.wait_ge(s["ld_w0"], 16)
            dve.wait_ge(s["ld_at"], 32)
            for lr in range(2):
                for k in range(2):
                    link(v.tensor_tensor(TMP, W0[:, k, :], AT[:, lr, :], ALU.mult))
                    ins = v.tensor_reduce(VL[:, k, 32 * lr:32 * lr + 32], TMP.rearrange("p (r d) -> p r d", d=HD),
                                          AX.X, ALU.add)
                    ins.then_inc(s["vl_done"], 1)
                    dve.wait_ge(s["vl_done"], 2 * lr + k + 1)
            dve.wait_ge(s["consts"], 1)
            for g in range(GR):
                last = v.tensor_scalar(DG[:, P * g:P * (g + 1)], ident[:, :], DST[:, g, P - 1:P], None, ALU.mult)
            last.then_inc(s["diag_done"], 1)
            dve.wait_ge(s["tab_mm"], 1)
            v.tensor_copy(ELS[:, 0:8, :].rearrange("p t n -> p (t n)"), PS[6][:, :]).then_inc(s["tab_ev"], 1)
            v.tensor_copy(ELS[:, 8:NT, :].rearrange("p t n -> p (t n)"), PS[7][:, 0:(NT - 8) * 64]).then_inc(s["tab_ev"], 1)
            dve.wait_ge(s["bc_mm"], 1)
            link(v.tensor_scalar(TMP[:, 0:Q], PS[4][:, :], w16col[:, 0:1], 0.0, ALU.is_lt, ALU.add, accum_out=cnt[:, 0:1]))
            link(v.tensor_tensor(cnt[:, 1:2], cnt[:, 0:1], pcol[:, 0:1], ALU.add))
            CMP = TMP[:, 0:STEPS // 2 + 1].bitcast(F16)[:, 0:STEPS]
            v.tensor_scalar(CMP, IOT, cnt[:, 1:2], None, ALU.is_ge).then_inc(s["cmp_done"], 1)
            dve.wait_ge(s["ws_mm"], 1)
            v.tensor_scalar(WS[:, 0:512], PS[5][:, :], 1.0, None, ALU.subtract)
            link(v.tensor_scalar(WS[:, 512:STEPS], PS[6][:, 0:STEPS - 512], 1.0, None, ALU.subtract))
            v.tensor_scalar(OFF, WS, float(3 * H), None, ALU.mult)
            link(v.tensor_tensor(TMP[:, 1024:1024 + STEPS], IOT, WS, ALU.subtract))
            for g in range(GR):
                last = v.tensor_scalar(SEL[:, g, :], TMP[:, 1024:1024 + STEPS], pcol[:, g:g + 1], None, ALU.is_equal)
            last.then_inc(s["sel_ready"], 1)
            dve.wait_ge(s["fld_mm"], 1)
            v.tensor_copy(SLO[:, 0:512], PS[4][:, :])
            v.tensor_copy(SLO[:, 512:STEPS], PS[5][:, 0:STEPS - 512]).then_inc(s["fld_ev"], 1)
            dve.wait_ge(s["fld_mm"], 2)
            v.scalar_tensor_tensor(DJ[:, 0:512], WS[:, 0:512], -float(WIN), PS[6][:, :], ALU.mult, ALU.add)
            v.scalar_tensor_tensor(DJ[:, 512:STEPS], WS[:, 512:STEPS], -float(WIN), PS[7][:, 0:STEPS - 512], ALU.mult, ALU.add)\
             .then_inc(s["fld_ev"], 1)
            dve.wait_ge(s["fld_ev"], 2)
            link(v.tensor_scalar(TMP[:, 0:STEPS], DJ, 0.0, 1e6, ALU.is_lt, ALU.mult))
            link(v.tensor_scalar(TMP[:, 1024:1024 + STEPS], DJ, float(WIN - 1), 1e6, ALU.is_gt, ALU.mult))
            link(v.tensor_tensor(KEY, TMP[:, 0:STEPS], TMP[:, 1024:1024 + STEPS], ALU.add))
            link(v.scalar_tensor_tensor(KEY, DJ, float(SH), KEY, ALU.mult, ALU.add))
            dve.wait_ge(s["fld_mm"], 3)
            v.tensor_tensor(KEY[:, 0:512], KEY[:, 0:512], PS[4][:, :], ALU.add)
            v.tensor_tensor(KEY[:, 512:STEPS], KEY[:, 512:STEPS], PS[5][:, 0:STEPS - 512], ALU.add)
            link(v.tensor_tensor(IDX, IOT, WS, ALU.subtract))
            v.tensor_scalar(TI, IDX, float(P), None, ALU.mult).then_inc(s["steps_done"], 1)
            for c in range(SC):
                link(v.tensor_scalar(SCOL[:, c:c + 1], pcol[:, 0:1], float(P * c), float(P), ALU.add, ALU.mult))
            for c in range(SC):
                n = min(P, STEPS - P * c)
                dve.wait_ge(s["key_mm"], c + 1)
                v.tensor_scalar(TCOL[0:n, c:c + 1], PS[6 + c % 2][0:n, P:P + 1], 1.0 / P, None, ALU.mult)
                if n < P:
                    v.memset(KEY16[:, c, :], -1.0)
                    link(v.memset(TMP[:, 0:1], 0.0))
                v.tensor_scalar(KEY16[0:n, c, :], PS[6 + c % 2][0:n, 0:P], SCOL[0:n, c:c + 1], None, ALU.subtract)\
                 .then_inc(s["key_ev"], 1)
            dve.wait_ge(s["er_ld"], 16)
            for i in range(4):
                dve.wait_ge(fs_st[i], NT * 16)
            dve.wait_ge(s["feat_mm"], NT * 4)
            link(v.tensor_copy(ERWv[:, :, 0, :], ERF))
            link(v.tensor_tensor(ERG, ERF, ERWv[:, :, 0, :], ALU.subtract))
            link(v.tensor_copy(ERWv[:, :, 1, :], ERG))
            link(v.tensor_tensor(ERF, ERG, ERWv[:, :, 1, :], ALU.subtract))
            v.tensor_copy(ERWv[:, :, 2, :], ERF).then_inc(s["erw_ready"], 1)

            def compare(k, i, c):
                for hf in range(2):
                    dve.wait_ge(s["kb_mm"], i * 4 + (2 * c + hf + 1))
                    for b in range(2):
                        ins = v.tensor_scalar(OHT[k][:, 512 * (2 * hf + b):512 * (2 * hf + b + 1)], PS[2 * hf + b][:, :],
                                              pcol[:, 0:1], None, ALU.is_equal)
                    ins.then_inc(s["oht"], 1)

            def sum_parts(k, at, n):
                v.tensor_reduce(ERSf[:, bass.ds(at * H, n * H)],
                                PS[4 + k][:, 0:n * 3 * H].rearrange("p (s q h) -> p s h q", q=3, h=H), AX.X, ALU.add)\
                 .then_inc(s["er_red"], 1)

            compare(0, 0, 0)
            compare(1, 0, 1)
            dve.wait_ge(s["er_mm"], 1)
            sum_parts(0, 0, CK)
            compare(0, 0, 2)
            dve.wait_ge(s["er_mm"], 2)
            sum_parts(1, CK, CK)
            with dve.Fori(0, ER_N) as i:
                for k in range(2):
                    dve.wait_ge(s["er_mm"], i * 2 + (2 + k))
                    compare(1 - k, i, 3 + k)
                    dve.wait_ge(s["er_mm"], i * 2 + (3 + k))
                    sum_parts(k, i * (2 * CK) + CK * (2 + k), CK)
            dve.wait_ge(s["er_mm"], NCK + 1)
            sum_parts(0, CK * NCK, CTAIL)
            for c in range(SC):
                n = min(P, STEPS - P * c)
                if c >= 2:
                    dve.wait_ge(s["sc_mm"], c - 1)
                v.tensor_scalar(SELT[0:n, c % 2, :], IOT[0:n, 0:Q], TCOL[0:n, c:c + 1], None, ALU.is_equal).then_inc(s["selt"], 1)
            dve.wait_ge(s["er_mm"], NCK + 1)
            dve.wait_ge(s["er_mm"], NCK + 1)
            link(v.tensor_scalar(OFF, WS, float(KW), None, ALU.mult))

            def onehots(st, lo, key):
                v.tensor_scalar(OHS[st % AS], iota128[:, :], lo, None, ALU.is_equal)
                v.tensor_scalar(OHK[st % AS], iota480[:, :], key, None, ALU.is_equal).then_inc(s["a_oh"], 1)

            def add_step(i, st, off):
                dve.wait_ge(s["a_ev"], i * AU + (st + 1))
                dve.wait_ge(s["a_add"], i * AU + (st + 1))
                dst = ADJ[:, :, bass.ds(off, KW)]
                v.tensor_tensor(dst, dst, EV[st % AS], ALU.add).then_inc(s["a_add"], 1)

            dve.wait_ge(s["a_add"], 1)

            def step_cols(st):
                return SLO[:, st:st + 1], KEY[:, st:st + 1]

            for st in range(AS):
                onehots(st, *step_cols(st))
            with dve.Fori(0, A_N) as i:
                offs = offsets(DVE, i * AU, AU, KW * (WINS - 1))
                dve.wait_ge(s["a_oh"], i * AU + AS)
                v.tensor_copy(SK, SLO_KEY[:, :, bass.ds(i * AU + AS, AU)]).then_inc(s["turn_cols"], 1)
                dve.wait_ge(s["turn_cols"], i + 1)
                for u in range(AU):
                    add_step(i, u, offs[u])
                    onehots(AS + u, SK[:, 0, u:u + 1], SK[:, 1, u:u + 1])
            offs = offsets(DVE, A_N * AU, STEPS - A_N * AU, KW * (WINS - 1))
            for st in range(A_N * AU, STEPS):
                add_step(0, st, offs[st - A_N * AU])
                if st + AS < STEPS:
                    onehots(AS + st, *step_cols(AS + st))
            dve.wait_ge(s["a_add"], STEPS + 1)
            v.tensor_scalar(OFF, WS, 64.0, None, ALU.mult).then_inc(s["off_acc"], 1)

            dve.wait_ge(s["pool_link"], LINKS)
            for k in range(2):
                dve.wait_ge(r_st[k], 16 * ((NGB + 1 - k) // 2))
            v.memset(cnt[:, 0:1], 0.0).then_inc(s["r_all"], 1)
            same = FL[:, 0, :].rearrange("p (g e) -> p g e", g=GR)
            sameb = FL[:, 1, :].rearrange("p (g e) -> p g e", g=GR)
            for f in (FL[:, 0, :], FL[:, 1, :]):
                link(v.memset(f, 0.0))
            v.tensor_tensor(same[:, :, 1:P], DST[:, :, 1:P], DST[:, :, 0:P - 1], ALU.is_equal)
            link(v.tensor_tensor(sameb[:, :, 0:P - 1], DST[:, :, 0:P - 1], DST[:, :, 1:P], ALU.is_equal))
            for j in range(2):
                link(v.tensor_scalar(FL[:, 2 + j, :], FL[:, j, :], -1.0, BIG, ALU.add, ALU.mult))
            for j, e in enumerate((0, P - 1)):
                for h in range(H):
                    last = v.tensor_copy(RD[:, j, :].rearrange("p (g h) -> p g h", h=H)[:, :, h], DST[:, :, e])
            last.then_inc(s["flags_in"], 1)
            D0R, D1R, LKR, UNR, CR = (ROW[0:H, j, :] for j in range(5))
            dve.wait_ge(s["flags_mm"], 1)
            v.tensor_copy(D0R, PS[4][0:H, :])
            link(v.tensor_copy(D1R, PS[5][0:H, :]))
            link(v.tensor_tensor(UNR, D0R, D1R, ALU.is_equal))
            link(v.memset(LKR, 0.0))
            link(v.tensor_tensor(LKR[:, 1:Q], D0R[:, 1:Q], D1R[:, 0:Q - 1], ALU.is_equal))

            def seg_scan(dst, op, mx, back, n):
                ident_ = -BIG if mx else 0.0
                op0 = ALU.add if mx else ALU.mult
                flags = FL[:, (2 if mx else 0) + back, :]
                e0, e1 = (P - 1, 0) if back else (0, P - 1)
                rev = (lambda ap: ap[:, ::-1]) if back else (lambda ap: ap)

                def scans():
                    for h in range(H):
                        ins = v.tensor_tensor_scan(rev(dst[:, h, :]), rev(flags), rev(S[:, h, :]), ident_, op0, op)
                    return ins

                scans().then_inc(s["tail_ready"], 1)
                cont = D0R
                lk = LKR[:, 1:Q] if back else LKR[:, 0:Q]
                link(v.memset(cont, 0.0))
                m = Q - 1 if back else Q
                link(v.tensor_tensor(cont[:, 0:m], UNR[:, 0:m], lk, ALU.mult))
                if mx:
                    link(v.tensor_scalar(cont, cont, -1.0, BIG, ALU.add, ALU.mult))
                dve.wait_ge(s["tail_mm"], n)
                link(v.tensor_copy(D1R, PS[4][0:H, :]))
                link(v.tensor_tensor_scan(rev(CR), rev(cont), rev(D1R), ident_, op0, op))
                link(v.memset(cont, ident_))
                lk1 = LKR[:, 1:Q]
                src = CR[:, 1:Q] if back else CR[:, 0:Q - 1]
                to = cont[:, 0:Q - 1] if back else cont[:, 1:Q]
                if mx:
                    link(v.tensor_scalar(D1R[:, 1:Q], lk1, -1.0, BIG, ALU.add, ALU.mult))
                    v.tensor_tensor(to, src, D1R[:, 1:Q], ALU.add).then_inc(s["cin_ready"], 1)
                else:
                    v.tensor_tensor(to, src, lk1, ALU.mult).then_inc(s["cin_ready"], 1)
                edge = S.rearrange("p h (g e) -> p h g e", g=GR)[:, :, :, e0]
                keep = SC16[:, 0, :].rearrange("p (h g) -> p h g", h=H)
                link(v.tensor_copy(keep, edge))
                dve.wait_ge(s["cin_mm"], n)
                carry = PS[5][:, 0:GR * H].rearrange("p (g h) -> p h g", h=H)
                link(v.tensor_tensor(edge, keep, carry, op))
                link(scans())
                link(v.tensor_copy(edge, keep))

            dve.wait_ge(s["lane_ev"], GR)
            Sf = S.rearrange("p h n -> p (h n)")
            link(v.scalar_tensor_tensor(Sf, Sf, 0.2, Sf, ALU.mult, ALU.max))
            seg_scan(FA, ALU.max, True, 0, 1)
            seg_scan(BA, ALU.max, True, 1, 2)
            flat = lambda ap: ap.rearrange("p h n -> p (h n)")
            link(v.tensor_tensor(flat(FA), flat(FA), flat(BA), ALU.max))
            v.tensor_tensor(flat(S), flat(S), flat(FA), ALU.subtract).then_inc(s["exp_ready"], 1)
            dve.wait_ge(s["exp_done"], 1)
            seg_scan(FA, ALU.add, False, 0, 3)
            seg_scan(BA, ALU.add, False, 1, 4)
            link(v.tensor_tensor(flat(FA), flat(FA), flat(BA), ALU.add))
            link(v.tensor_tensor(flat(FA), flat(FA), flat(S), ALU.subtract))
            link(v.reciprocal(flat(FA), flat(FA)))
            v.tensor_tensor(flat(S), flat(S), flat(FA), ALU.mult).then_inc(s["alpha_ready"], 1)
            over = A_S + H * Q - A_ACC
            dve.wait_ge(s["alpha_ready"], 1)
            v.memset(ACCf[:, over:], 0.0)
            dve.wait_ge(s["als_mm"], H)
            v.memset(ACCf[:, 0:over], 0.0).then_inc(s["l_acc"], 1)
            dve.wait_ge(s["als_ev"], H)

            def weigh(i, st, place, al):
                dve.wait_ge(f_done[st % FR], i * 16 + 16 * (st // FR + 1))
                wv = WOH[:, st % NWOH, :].rearrange("p (h j) -> p h j", h=H)
                v.scalar_tensor_tensor(wv, iota16[:, :].rearrange("p (a j) -> p a j", a=1).to_broadcast([P, H, WIN]),
                                       place,
                                       al.rearrange("p (h a) -> p h a", a=1).to_broadcast([P, H, WIN]),
                                       ALU.is_equal, ALU.mult).then_inc(s["l_woh"], 1)

            def accumulate(bank, off):
                dst = ACCf[:, bass.ds(off, 64)]
                v.tensor_tensor(dst, dst, PS[bank][:, 0:64], ALU.add).then_inc(s["l_acc"], 1)

            dve.wait_ge(s["off_acc"], 1)
            def sum_step(i, st, off):
                if st % 2 == 0:
                    dve.wait_ge(s["l_mm"], i * FR + (st + 2))
                dve.wait_ge(s["l_acc"], i * FR + (st + 1))
                accumulate(st % LAG, off)

            offs = offsets(DVE, 0, HEAD - LAG, 64 * (WINS - 1))
            for st in range(HEAD):
                if st >= LAG:
                    sum_step(0, st - LAG, offs[st - LAG])
                weigh(0, st, DJ[:, st:st + 1], ALSf[:, H * st:H * (st + 1)])
            with dve.Fori(0, GRPS) as i:
                offs = offsets(DVE, i * FR + (HEAD - LAG), FR, 64 * (WINS - 1))
                dve.wait_ge(s["l_woh"], i * FR + HEAD)
                v.tensor_copy(DJT, DJ[:, bass.ds(i * FR + HEAD, FR)])
                v.tensor_copy(ALT, ALSf[:, bass.ds(i * (FR * H) + HEAD * H, FR * H)]).then_inc(s["turn_cols"], 1)
                dve.wait_ge(s["turn_cols"], i + (A_N + 1))
                for u in range(FR):
                    sum_step(i, HEAD + u - LAG, offs[u])
                    weigh(i, HEAD + u, DJT[:, u:u + 1], ALT[:, H * u:H * (u + 1)])
            offs = offsets(DVE, STEPS - LAG, LAG, 64 * (WINS - 1))
            for u in range(LAG):
                sum_step(0, STEPS - LAG + u, offs[u])

            dve.wait_ge(s["pool_link"], LINKS + 2 * R2 * SH - 1)
            link(v.tensor_reduce(FLF[:, 1:2], CNTS, AX.X, ALU.max))
            v.tensor_scalar(FLF[:, 2:3], FLF[:, 1:2], float(MAX16), None, ALU.is_gt).then_inc(s["flag_cmp"], 1)
            dve.wait_ge(s["l_acc"], STEPS + 1)
            dve.wait_ge(s["ld_bc"], 16)
            v.memset(XT[:, :, NW:NP], 0.0)
            for f in range(2):
                for hh in range(2):
                    p0 = 64 * hh
                    c0 = 32 * f + 16 * hh
                    v.tensor_scalar(XT[p0:p0 + 64, f, 0:NW].rearrange("p (w j) -> p w j", j=WIN),
                                    ACC[p0:p0 + 64, :, c0:c0 + WIN], BC[p0:p0 + 64, f:f + 1], None, ALU.add)
            v.memset(X[:, NT - 1, :], 0.0).then_inc(s["ht_ready"], 1)
            link(v.memset(RC[:, :], 1.0))
            dve.wait_ge(s["cnt_mm"], 1)
            v.tensor_copy(FLG[:, 0:1], PS[4][:, NT:NT + 1]).then_inc(s["flag_ready"], 1)
            lastn = NW - (NT - 1) * P
            v.tensor_scalar(RC[:, 0:NT - 1], PS[4][:, 0:NT - 1], 1.0, None, ALU.max)
            link(v.tensor_scalar(RC[0:lastn, NT - 1:NT], PS[4][0:lastn, NT - 1:NT], 1.0, None, ALU.max))
            link(v.reciprocal(RC[:, :], RC[:, :]))
            dve.wait_ge(s["flag_ready"], 2)
            large = dve.value_load(FLG[0:1, 0:1], min_val=0, max_val=P)
            v.tensor_tensor(BC[:, 20:26], BC[:, 6:12], BC[:, 12:18], ALU.add)
            dve.wait_ge(s["ld_x"], 32)
            for t in range(NT):
                dve.wait_ge(s["ht_mm"], t + 1)
                v.tensor_tensor(X[:, t, :], X[:, t, :], PS[t % 4][:, 0:D], ALU.add).then_inc(s["ht_add"], 1)
                if t:
                    dve.wait_ge(s["ht_add"], t)
                    v.bn_stats(ST[:, t - 1, :], X[:, t - 1, :])

            lns = [0]

            def layer_norm(first=0):
                lns[0] += 1
                for t in range(first, NT):
                    ins = v.bn_stats(ST[:, t, :], X[:, t, :])
                link(ins)
                for t in range(NT):
                    ins = v.bn_aggr(MV[:, t, :], ST[:, t, :])
                link(ins)
                v.tensor_scalar(MV[:, :, 1], MV[:, :, 1], EPS, None, ALU.add).then_inc(s["var_ready"], 1)
                dve.wait_ge(s["std_ready"], lns[0])
                link(v.reciprocal(RS[:, :], RS[:, :]))
                for t in range(NT):
                    ins = v.tensor_scalar(X[:, t, :], X[:, t, :], MV[:, t, 0:1], RS[:, t:t + 1], ALU.subtract, ALU.mult)
                    if t % 4 == 3 or t == NT - 1:
                        ins.then_inc(s["ln_done"], 1)

            def xt_evac(n):
                for q in range(4):
                    dve.wait_ge(s["xt_mm"], 8 * n + 2 * q + 2)
                    w = min(512, NP - 512 * q)
                    v.tensor_copy(XT[:, 1, 512 * q:512 * q + w], PS[2 * q + 1][:, 0:w]).then_inc(s["xt_evd"], 1)

            def bias_parts(n):
                row = lambda ap: ap[0:3, 0:n * D]
                part = lambda q: ident[0:3, q:q + 1]
                link(v.tensor_copy(row(BHI), row(BROW)))
                link(v.tensor_tensor(row(BREM), row(BROW), row(BHI), ALU.subtract))
                link(v.tensor_copy(row(BMID), row(BREM)))
                link(v.tensor_tensor(row(BLO), row(BREM), row(BMID), ALU.subtract))
                link(v.tensor_scalar(row(BPF), row(BHI), part(0), None, ALU.mult))
                link(v.scalar_tensor_tensor(row(BPF), row(BMID), part(1), row(BPF), ALU.mult, ALU.add))
                v.scalar_tensor_tensor(row(BPF), row(BLO), part(2), row(BPF), ALU.mult, ALU.add).then_inc(s["bias_ready"], 1)
                dve.wait_ge(s["bias_ready"], n - 2)

            dve.wait_ge(s["ht_add"], NT)
            layer_norm(NT - 1)
            xt_evac(0)
            dve.wait_ge(s["ld_wt1"], 16 * 5)
            bias_parts(3)
            def rest(n, slot, bank, done, before):
                hi, mid, lo = parts(slot)
                dve.wait_ge(s["hi_ready"], n + 1)
                if before:
                    dve.wait_ge(done, before)
                link(v.scalar_tensor_tensor(REM, PS[bank][:, 0:D], 0.0, hi, ALU.max, ALU.subtract))
                link(v.tensor_copy(mid, REM))
                v.tensor_tensor(lo, REM, mid, ALU.subtract).then_inc(done, 1)

            def no_rest(n, done):
                dve.wait_ge(s["hi_ready"], n + 1)
                dve.sem_inc(s["dve_link"], 2)
                dve.sem_inc(done, 1)

            with dve.If(large < 1):
                for n in range(R2 * NT):
                    rest(n, n, 4 + n % 3, s["m_ev"], n)
            chain[0] -= 2 * R2 * NT
            with dve.If(large >= 1):
                for n in range(R2 * NT):
                    no_rest(n, s["m_ev"])
            chain[0] += 2 * R2 * NT

            def agg_evac(dst, total):
                dve.wait_ge(s["chunk_used"], total)
                for j in range(4):
                    v.tensor_copy(dst[:, 0, CW * j:CW * (j + 1)], PS[j][:, 0:CW])
                v.memset(dst[:, :, NW:NP], 0.0).then_inc(s["agg_evd"], 1)

            agg_evac(XT, R2 * SH)
            for c in range(NC):
                dve.wait_ge(s["gate_ev"], 6 * c + 4)
                v.tensor_tensor(CC, GT[:, 0:2, :], GT[:, 2:4, :], ALU.mult).then_inc(s["c_ready"], 1)
                dve.wait_ge(s["tc_ready"], c + 1)
                dve.wait_ge(s["gate_ev"], 6 * c + 6)
                if c:
                    dve.wait_ge(s["x1_mm"], c)
                v.tensor_tensor(HN, CC, GT[:, 4:6, :], ALU.mult).then_inc(s["hn_ready"], 1)
                if c:
                    dve.wait_ge(s["x3_add"], c)
                    for t in range(3 * c - 3, 3 * c):
                        v.bn_stats(ST[:, t, :], X[:, t, :])
                dve.wait_ge(s["x3_mm"], c + 1)
                xv = X[:, 3 * c:3 * c + 2, :].rearrange("p t d -> p (t d)")
                v.tensor_tensor(xv, xv, PS[6][:, :], ALU.add)
                v.tensor_tensor(X[:, 3 * c + 2, :], X[:, 3 * c + 2, :], PS[7][:, 0:D], ALU.add).then_inc(s["x3_add"], 1)
            dve.wait_ge(s["x3_add"], NC)
            layer_norm(NT - 3)
            xt_evac(1)
            dve.wait_ge(s["ld_wt2"], 160)
            bias_parts(4)
            base = R2 * SH

            def both(u, c, wide):
                if c >= 2:
                    dve.wait_ge(s["chunk_used"], base + u * SH + c - 1)
                a0, a1 = (ADJ[:, r, :].rearrange("p (n s) -> p n s", s=SH)[:, :, c] for r in range(R2))
                v.tensor_tensor(chunk(CH2, c % 2, wide), a0, a1, ALU.add).then_inc(s["chunk_ready"], 1)

            for u in range(2):
                with dve.If(large < 1):
                    for c in range(2):
                        both(u, c, False)
                    for t in range(NT):
                        rest(R2 * NT + u * NT + t, t, t % 4, s["p_ev"], u * NT + t)
                    for c in range(2, SH):
                        both(u, c, False)
                chain[0] -= 2 * NT
                with dve.If(large >= 1):
                    for c in range(2):
                        both(u, c, True)
                    for t in range(NT):
                        no_rest(R2 * NT + u * NT + t, s["p_ev"])
                    for c in range(2, SH):
                        both(u, c, True)
                chain[0] += 2 * NT
                agg_evac(B2T, base + (u + 1) * SH)
                for t in range(NT):
                    b = 2 * (t % 4)
                    dve.wait_ge(s["o_mm"], NT * u + t + 1)
                    link(v.tensor_scalar(B1[:, t, :], PS[b][:, 0:D], RC[:, t:t + 1], None, ALU.mult))
                    link(v.tensor_tensor(B1[:, t, :], B1[:, t, :], PS[b + 1][:, 0:D], ALU.add))
                    v.tensor_tensor_reduce(out=CH[:, 0, 0:D], in0=B1[:, t, :], in1=B1[:, t, :], scale=1.0, scalar=0.0,
                                           op0=ALU.mult, op1=ALU.add, accum_out=RS[:, t:t + 1]).then_inc(s["o_ready"], 1)
                dve.wait_ge(s["nrm_done"], u + 1)
                link(v.tensor_scalar(RS[:, :], RS[:, :], 1e-12, None, ALU.max))
                link(v.reciprocal(RS[:, :], RS[:, :]))
                if u == 0:
                    for t in range(NT):
                        ins = v.tensor_scalar(B1[:, t, :], B1[:, t, :], RS[:, t:t + 1], 0.0, ALU.mult, ALU.max)
                        if t % 4 == 3 or t == NT - 1:
                            ins.then_inc(s["h_ready"], 1)
                    xt_evac(2)
                else:
                    for t in range(NT):
                        ins = v.scalar_tensor_tensor(X[:, t, :], B1[:, t, :], RS[:, t:t + 1], X[:, t, :], ALU.mult, ALU.add)
                    link(ins)
            layer_norm()
            dve.wait_ge(s["ld_wt3"], 48)
            for lr in range(2):
                for k in range(2):
                    link(v.tensor_tensor(TMP3, WT3[:, k, 0:D], A3[:, lr, :], ALU.mult))
                    ins = v.tensor_reduce(WT3[:, k, D + H * lr:D + H * (lr + 1)], TMP3.rearrange("p (h d) -> p h d", d=HD),
                                          AX.X, ALU.add)
                    if (lr, k) == (1, 1):
                        ins.then_inc(s["vl3_done"], 1)
                    else:
                        link(ins)
            xt_evac(3)
            dve.wait_ge(s["g3"], 16 * 2 * NT)
            a3 = lambda j: S3[:, j, :].rearrange("p (t h) -> p t h", h=H)
            link(v.tensor_tensor(a3(0), AG3, G3[:, :, D + H:D + 2 * H], ALU.add))
            link(v.scalar_tensor_tensor(S3[:, 0, :], S3[:, 0, :], 0.01, S3[:, 0, :], ALU.mult, ALU.max))
            m3 = S3[:, 1, 0:NT]
            link(v.tensor_reduce(m3, a3(0), AX.X, ALU.max))
            v.tensor_tensor(a3(0), a3(0), m3.rearrange("p (t a) -> p t a", a=1).to_broadcast([P, NT, H]),
                            ALU.subtract).then_inc(s["s3_ready"], 1)
            dve.wait_ge(s["s3_exp"], 1)
            link(v.tensor_reduce(m3, a3(0), AX.X, ALU.add))
            link(v.reciprocal(m3, m3))
            link(v.tensor_tensor(a3(0), a3(0), m3.rearrange("p (t a) -> p t a", a=1).to_broadcast([P, NT, H]), ALU.mult))
            for t in range(NT):
                gv = G3[:, t, 0:D].rearrange("p (h d) -> p h d", h=H)
                ins = v.tensor_tensor(gv, gv, S3[:, 0, H * t:H * t + H].rearrange("p (h a) -> p h a", a=1).to_broadcast([P, H, HD]), ALU.mult)
            link(ins)
            for t in range(NT):
                ins = v.tensor_reduce(T64[:, t, :], G3[:, t, 0:D].rearrange("p (h d) -> p d h", h=H), AX.X, ALU.add)
            link(ins)
            for t in range(NT):
                xv = X[:, t, :].rearrange("p (h d) -> p h d", h=H)
                ins = v.tensor_tensor(xv, xv, T64[:, t, :].rearrange("p (a d) -> p a d", a=1).to_broadcast([P, H, HD]), ALU.add)
            link(ins)
            layer_norm()

        @block.tensor
        def _(pe):
            mm = nc.tensor.matmul
            tr = nc.tensor.transpose
            pe.wait_ge(s["consts"], 1)
            pe.wait_ge(s["flag_cmp"], 1)
            mm(PS[0][:, 0:1], ones[:, :], FLF[:, 0:1], start=True, stop=True).then_inc(s["flag_mm"], 1)
            pe.wait_ge(s["flag_ready"], 1)
            unsorted = pe.value_load(FLG[0:1, 0:1], min_val=0, max_val=EP)
            with pe.If(unsorted >= 1):
                pe.wait_ge(s["srt_a"], 1)
                for g in range(GR):
                    ins = tr(PS[1][:, P * g:P * (g + 1)], LD[:, P * g:P * (g + 1)], ident[:, :])
                ins.then_inc(s["srt_pre"], 1)
                with pe.Fori(0, NTL) as i:
                    pe.wait_ge(s["srt_oh"], i + 1)
                    mm(PS[3][:, 0:16], OL, HI16, start=True, stop=True).then_inc(s["srt_hist"], 1)
                pe.wait_ge(s["srt_a"], 2)
                pe.wait_ge(s["srt_tv"], 1)
                mm(PS[1][:, 0:16], ones[:, :], CUR, start=True, stop=True)
                mm(PS[2][:, 0:16], TRIT, CUR, start=True, stop=True).then_inc(s["srt_pre"], 1)
                with pe.Fori(0, NTL) as i:
                    pe.wait_ge(s["srt_oh"], i + (NTL + 1))
                    mm(PS[1][:, 0:P], ones[:, :], DGc, start=True, stop=True)
                    tr(PS[2][:, 0:P], OL, ident[:, :])
                    mm(PS[3][:, 0:16], OL, HI16, start=True, stop=True).then_inc(s["srt_b"], 1)
                    pe.wait_ge(s["srt_c"], i + 1)
                    mm(PS[0][:, 0:16], OLT, CUR, start=True, stop=True).then_inc(s["srt_d"], 1)
            pe.wait_ge(s["fields"], 1)
            for g in range(GR):
                ins = tr(PS[4][:, P * g:P * (g + 1)], Fl[:, 3, P * g:P * (g + 1)], ident[:, :])
            ins.then_inc(s["idx_mm"], 1)

            def score_tables():
                pe.wait_ge(s["vl_done"], 4)
                for t in range(NT):
                    for k in range(2):
                        ins = mm(PS[6 + t // 8][:, 64 * (t % 8):64 * (t % 8 + 1)], XT0[:, k, P * t:P * (t + 1)],
                                 VL[:, k, :], start=(k == 0), stop=(k == 1))
                ins.then_inc(s["tab_mm"], 1)

            def last_destinations():
                pe.wait_ge(s["diag_done"], 1)
                pe.wait_ge(s["idx_ev"], 1)
                mm(PS[4][:, :], ones[:, :], DG, start=True, stop=True).then_inc(s["bc_mm"], 1)

            def windows_begun():
                pe.wait_ge(s["tab_ev"], 2)
                pe.wait_ge(s["cmp_done"], 1)
                CMP = TMP[:, 0:STEPS // 2 + 1].bitcast(F16)[:, 0:STEPS]
                mm(PS[5][:, :], ones16[:, :], CMP[:, 0:512], start=True, stop=True)
                mm(PS[6][:, 0:STEPS - 512], ones16[:, :], CMP[:, 512:STEPS], start=True, stop=True).then_inc(s["ws_mm"], 1)

            def select(lhs, b0):
                for (bank, lo, hi) in ((b0, 0, 512), (b0 + 1, 512, STEPS)):
                    for g in range(GR):
                        ins = mm(PS[bank][:, 0:hi - lo], lhs(g), SEL[:, g, lo:hi], start=(g == 0), stop=(g == GR - 1))
                return ins

            def step_field(n, f):
                if n == 0:
                    pe.wait_ge(s["sel_ready"], 1)
                if n >= 2:
                    pe.wait_ge(s["fld_ev"], n - 1)
                select(lambda g: Fl[:, f, P * g:P * (g + 1)], 4 + 2 * (n % 2)).then_inc(s["fld_mm"], 1)

            def step_keys(c):
                pe.wait_ge(s["fld_ev"], 2)
                if c >= 2:
                    pe.wait_ge(s["key_ev"], c - 1)
                n = min(P, STEPS - P * c)
                for g in range(GR):
                    ins = mm(PS[6 + c % 2][0:n, 0:P + 1], SEL[:, g, P * c:P * c + n], LKEY[:, g, :],
                             start=(g == 0), stop=(g == GR - 1))
                ins.then_inc(s["key_mm"], 1)

            between = {TABS_AT: score_tables, 16: last_destinations, 19: windows_begun, 22: lambda: step_field(0, 0),
                       24: lambda: step_field(1, 2), 27: lambda: step_field(2, 1)}
            between.update({30 + 2 * c: (lambda c=c: step_keys(c)) for c in range(SC)})
            pe.wait_ge(s["ld_xt"], 16)
            pe.wait_ge(s["ld_w0"], 16)
            for i in range(4 * NT):
                if i in between:
                    between[i]()
                t, c = i // 4, i % 4
                if i >= 4:
                    pe.wait_ge(s["feat_ev"], i - 3)
                for k in range(2):
                    ins = mm(PS[c][:, :], XT0[:, k, P * t:P * (t + 1)], W0[:, k, 512 * c:512 * (c + 1)],
                             start=(k == 0), stop=(k == 1))
                ins.then_inc(s["feat_mm"], 1)

            def window_offsets(step, n):
                return offsets(PE, step, n, 3 * H * (WINS - 1))

            def er_chunk(k, offs):
                for j in range(len(offs)):
                    ins = mm(PS[4 + k][:, 3 * H * j:3 * H * (j + 1)], OHT[k][:, P * j:P * (j + 1)],
                             ERW[:, bass.ds(offs[j], 3 * H)], start=True, stop=True)
                ins.then_inc(s["er_mm"], 1)

            pe.wait_ge(s["steps_done"], 1)
            pe.wait_ge(s["erw_ready"], 1)
            def broadcast_keys(k, i, c):
                pe.wait_ge(k_ld[k], i * 16 + 16 * (c // 2 + 1))
                for hf in range(2):
                    if c:
                        pe.wait_ge(s["oht"], i * 4 + (2 * c + hf - 1))
                    for b in range(2):
                        lo = 512 * (2 * hf + b)
                        ins = mm(PS[2 * hf + b][:, :], ones16[0:1, :], KRB[k][0:1, lo:lo + 512], start=True, stop=True)
                    ins.then_inc(s["kb_mm"], 1)

            pe.wait_ge(s["feat_ev"], NT * 4)
            broadcast_keys(0, 0, 0)
            broadcast_keys(1, 0, 1)
            pe.wait_ge(s["oht"], 2)
            offs = window_offsets(0, 2 * CK)
            er_chunk(0, offs[0:CK])
            broadcast_keys(0, 0, 2)
            pe.wait_ge(s["oht"], 4)
            er_chunk(1, offs[CK:2 * CK])
            with pe.Fori(0, ER_N) as i:
                offs = window_offsets(i * (2 * CK) + 2 * CK, 2 * CK)
                for k in range(2):
                    broadcast_keys(1 - k, i, 3 + k)
                    pe.wait_ge(s["oht"], i * 4 + (6 + 2 * k))
                    pe.wait_ge(s["er_red"], i * 2 + (1 + k))
                    er_chunk(k, offs[CK * k:CK * (k + 1)])
            pe.wait_ge(s["oht"], 2 * NCK + 2)
            pe.wait_ge(s["er_red"], NCK - 1)
            er_chunk(0, window_offsets(CK * NCK, CTAIL))
            pe.wait_ge(s["er_red"], NCK + 1)

            def step_transposes(c):
                n = min(P, STEPS - P * c)
                if c >= 2:
                    pe.wait_ge(s["et_ev"], c - 1)
                for h in range(H):
                    ins = tr(PS[4 + c % 2][0:n, P * h:P * (h + 1)], ERS[:, P * c:P * c + n, h], ident[:, :])
                ins.then_inc(s["et_mm"], 1)

            step_transposes(0)
            for c in range(SC):
                if c + 1 < SC:
                    step_transposes(c + 1)
                n = min(P, STEPS - P * c)
                pe.wait_ge(s["et_ev"], c + 1)
                pe.wait_ge(s["selt"], c + 1)
                for g in range(GR):
                    ins = mm(PS[g][:, :], SELT[0:n, c % 2, P * g:P * (g + 1)], ET[0:n, c % 2, :], start=(c == 0), stop=False)
                ins.then_inc(s["sc_mm"], 1)
            pe.wait_ge(s["steps_done"], 1)

            def count(i, st):
                pe.wait_ge(s["a_oh"], i * AU + (st + 1))
                if st >= 4:
                    pe.wait_ge(s["a_ev"], i * AU + (st - 3))
                mm(PS[4 + st % 4][:, 0:R2 * KW], OHS[st % AS], OHK[st % AS], start=True, stop=True).then_inc(s["a_mm"], 1)

            for st in range(AS):
                count(0, st)
            with pe.Fori(0, A_N) as i:
                for u in range(AU):
                    count(i, AS + u)
            for st in range(AS + A_N * AU, STEPS):
                count(0, st)
            pe.wait_ge(s["pool_link"], LINKS)
            for g in range(GR):
                for h in range(H):
                    ins = mm(PS[g][:, P * h:P * (h + 1)], SUM[:, P * g:P * (g + 1), h], ident[:, :],
                             start=False, stop=(h == H - 1))
                ins.then_inc(s["lane_mm"], 1)
            pe.wait_ge(s["flags_in"], 1)
            for j in range(2):
                for g in range(GR):
                    ins = tr(PS[4 + j][0:H, P * g:P * (g + 1)], RD[:, j, H * g:H * (g + 1)], ident[:, :])
            ins.then_inc(s["flags_mm"], 1)
            for n in range(4):
                dst = (FA, BA)[n % 2].rearrange("p h (g e) -> p h g e", g=GR)
                e1 = (P - 1, 0)[n % 2]
                pe.wait_ge(s["tail_ready"], n + 1)
                for g in range(GR):
                    ins = tr(PS[4][0:H, P * g:P * (g + 1)], dst[:, :, g, e1], ident[:, :])
                ins.then_inc(s["tail_mm"], 1)
                pe.wait_ge(s["cin_ready"], n + 1)
                for g in range(GR):
                    ins = tr(PS[5][:, H * g:H * (g + 1)], ROW[0:H, 0, P * g:P * (g + 1)], ident[0:H, 0:H])
                ins.then_inc(s["cin_mm"], 1)
            pe.wait_ge(s["alpha_ready"], 1)
            pe.wait_ge(s["a_ev"], STEPS)
            for h in range(H):
                select(lambda g: S[:, h, P * g:P * (g + 1)], 2 * h).then_inc(s["als_mm"], 1)
            pe.wait_ge(s["als_ev"], H)

            def scatter(i, st):
                pe.wait_ge(s["l_woh"], i * FR + (st + 1))
                for f in range(2):
                    ins = mm(PS[st % LAG][:, 32 * f:32 * (f + 1)], FB[:, st % FR, P * f:P * (f + 1)],
                             WOH[:, st % NWOH, 32 * f:32 * (f + 1)], start=True, stop=True)
                ins.then_inc(s["l_mm"], 1)

            for st in range(HEAD):
                scatter(0, st)
            with pe.Fori(0, GRPS) as i:
                for u in range(FR):
                    scatter(i, HEAD + u)
            pe.wait_ge(s["l_acc"], STEPS + 1)
            pe.wait_ge(s["flag_cmp"], 2)
            for t in range(NT):
                w = min(P, NW - P * t)
                mm(PS[4][0:w, t:t + 1], CNTS[:, P * t:P * t + w], ones[:, 0:1], start=True, stop=True)
            mm(PS[4][:, NT:NT + 1], ones[:, :], FLF[:, 2:3], start=True, stop=True).then_inc(s["cnt_mm"], 1)
            pe.wait_ge(s["ht_ready"], 1)
            for t in range(NT):
                if t >= 4:
                    pe.wait_ge(s["ht_add"], t - 3)
                for f in range(2):
                    ins = tr(PS[t % 4][:, P * f:P * (f + 1)], XT[:, f, P * t:P * (t + 1)], ident[:, :])
                ins.then_inc(s["ht_mm"], 1)

            def transpose_x(n, src, ready, before):
                for q in range(4):
                    pe.wait_ge(ready, before + q + 1)
                    for k in range(2):
                        for j in range(min(4, NT - 4 * q)):
                            ins = tr(PS[2 * q + k][:, P * j:P * (j + 1)], src[:, 4 * q + j, P * k:P * (k + 1)], ident[:, :])
                        ins.then_inc(s["xt_mm"], 1)
                pe.wait_ge(s["xt_eva"], 4 * (n + 1))
                pe.wait_ge(s["xt_evd"], 4 * (n + 1))

            transpose_x(0, X, s["ln_done"], 0)
            pe.wait_ge(s["ld_wt1"], 16 * 5)
            pe.wait_ge(s["flag_ready"], 2)
            large = pe.value_load(FLG[0:1, 0:1], min_val=0, max_val=P)

            def hidden(i):
                r, c = i // NC, i % NC
                if i >= 2:
                    pe.wait_ge(s["h_ev"], 2 * (i - 1))
                for fo in range(2):
                    for k in range(2):
                        ins = mm(PS[2 * (i % 2) + fo][:, 0:CN], WREL[:, k, r, P * fo:P * (fo + 1)],
                                 XT[:, k, CN * c:CN * (c + 1)], start=(k == 0), stop=(k == 1))
                    ins.then_inc(s["h_mm"], 1)

            hidden(0)
            pe.wait_ge(s["bias_ready"], 1)
            for i in range(R2 * NC):
                if i + 1 < R2 * NC:
                    hidden(i + 1)
                r = i // NC
                pe.wait_ge(s["h_ev"], 2 * (i + 1))
                if i:
                    pe.wait_ge(s["m_ev"], 3 * i)
                for j in range(3):
                    mm(PS[4 + j][:, 0:D], ones16[0:3, :], BP[0:3, r, :], start=True, stop=False)
                    for k in range(2):
                        ins = mm(PS[4 + j][:, 0:D], HC[i % 2][:, k, P * j:P * (j + 1)], WREL[:, k, r, :],
                                 start=False, stop=(k == 1))
                    ins.then_inc(s["m_mm"], 1)
            pe.wait_ge(s["m_ev"], 3 * R2 * NC)

            def aggregate(at, n, first):
                def products(wide):
                    for c in range(n):
                        pe.wait_ge(s["chunk_ready"], first + c + 1)
                        ch = chunk(at, c % 2, wide)
                        ms = [MT[c][:, 0:D]] if wide else parts(c)
                        for q, m in enumerate(ms):
                            for fo in range(2):
                                for j in range(4):
                                    ins = mm(PS[4 * fo + j][:, 0:CW], m[:, P * fo:P * (fo + 1)], ch[:, CW * j:CW * (j + 1)],
                                             start=(c == 0 and q == 0), stop=(c == n - 1 and q == len(ms) - 1))
                        ins.then_inc(s["chunk_used"], 1)

                with pe.If(large < 1):
                    products(False)
                with pe.If(large >= 1):
                    products(True)

            aggregate(CH1, R2 * SH, 0)
            pe.wait_ge(s["ld_wt1"], 16 * 9)
            pe.wait_ge(s["agg_evd"], 1)
            pe.wait_ge(s["agg_eva"], 4)
            for c in range(NC):
                cs = slice(CN * c, CN * (c + 1))
                if c:
                    pe.wait_ge(s["gate_ev"], 6 * c)
                for j in range(6):
                    for k in range(2):
                        ins = mm(PS[j][:, 0:CN], WIH[:, k, P * j:P * (j + 1)], XT[:, k, cs], start=(k == 0), stop=(k == 1))
                    ins.then_inc(s["gate_mm"], 1)
                pe.wait_ge(s["hn_ready"], c + 1)
                if c:
                    pe.wait_ge(s["x3_add"], c)
                for k in range(2):
                    ins = mm(PS[6][:, 0:CN], W1s[:, k, :], HN[:, k, :], start=(k == 0), stop=(k == 1))
                ins.then_inc(s["x1_mm"], 1)
                pe.wait_ge(s["x1_ev"], c + 1)
                mm(PS[7][:, 0:CN], W2s, X1, start=True, stop=True).then_inc(s["x2_mm"], 1)
                pe.wait_ge(s["x2_ev"], c + 1)
                for j in range(3):
                    o = PS[6 + j // 2][:, D * (j % 2):D * (j % 2 + 1)]
                    mm(o, ones16[0:3, :], BP[0:3, 2, :], start=True, stop=False)
                    ins = mm(o, X2[:, P * j:P * (j + 1)], W3s, start=False, stop=True)
                ins.then_inc(s["x3_mm"], 1)
            transpose_x(1, X, s["ln_done"], 4)
            pe.wait_ge(s["ld_wt2"], 160)
            pe.wait_ge(s["bias_ready"], 2)
            for u in range(2):
                Wp, Wl, Wr = W2L[3 * u:3 * u + 3]
                for t in range(NT):
                    if t >= 4:
                        pe.wait_ge(s["p_ev"], NT * u + t - 3)
                    mm(PS[t % 4][:, 0:D], ones16[0:3, :], BP[0:3, 2 * u, :], start=True, stop=False)
                    for k in range(2):
                        ins = mm(PS[t % 4][:, 0:D], XT[:, k, P * t:P * (t + 1)], Wp[:, k, :], start=False, stop=(k == 1))
                    ins.then_inc(s["p_mm"], 1)
                pe.wait_ge(s["p_ev"], NT * (u + 1))
                aggregate(CH2, SH, (R2 + u) * SH)
                pe.wait_ge(s["agg_evd"], 2 + u)
                pe.wait_ge(s["agg_eva"], 4 * (2 + u))
                for t in range(NT):
                    if t >= 4:
                        pe.wait_ge(s["o_ready"], NT * u + t - 3)
                    b = 2 * (t % 4)
                    for k in range(2):
                        mm(PS[b][:, 0:D], B2T[:, k, P * t:P * (t + 1)], Wl[:, k, :], start=(k == 0), stop=(k == 1))
                    mm(PS[b + 1][:, 0:D], ones16[0:3, :], BP[0:3, 1 + 2 * u, :], start=True, stop=False)
                    for k in range(2):
                        ins = mm(PS[b + 1][:, 0:D], XT[:, k, P * t:P * (t + 1)], Wr[:, k, :], start=False, stop=(k == 1))
                    ins.then_inc(s["o_mm"], 1)
                if u == 0:
                    transpose_x(2, B1, s["h_ready"], 0)
            transpose_x(3, X, s["ln_done"], 8)
            pe.wait_ge(s["vl3_done"], 1)
            for t in range(NT):
                if t >= 4:
                    pe.wait_ge(s["t_ev"], t - 3)
                for k in range(2):
                    ins = mm(PS[t % 4][:, 0:D + 2 * H], XT[:, k, P * t:P * (t + 1)], WT3[:, k, :], start=(k == 0), stop=(k == 1))
                ins.then_inc(s["t_mm"], 1)


def layout(i):
    import numpy as np
    c = np.ascontiguousarray
    g = {k: np.asarray(v) for k, v in i.items()}
    rec = np.zeros((EP + P, 4), np.int32)
    rec[:, 1] = PAD_DST
    rec[:E, 0] = g["src"]
    rec[:E, 1] = g["dst"]
    rec[:E, 2] = g["edge_type_2"]
    rec[:E, 3] = g["edge_type_8"]
    xT = np.zeros((D, NP), np.float32)
    xT[:, :N] = g["x"].T
    w_ih = g["L1_gnn_W_ih"].T
    pick = lambda a: np.concatenate([a[..., 0:D], a[..., 2 * D:4 * D]], -1)
    row = lambda a: c(a.reshape(1, -1))
    cols = c(np.concatenate([g["L0_gnn_h_bias"], g["L1_gnn_b_rel"].reshape(-1), pick(g["L1_gnn_b_ih"]),
                             pick(g["L1_gnn_b_hh"]), g["L1_gnn_b1"], g["L1_gnn_b2"]]).reshape(20, P).T)
    return [
        ("rec", rec), ("x", c(g["x"])), ("xT", xT), ("edge0", c(np.stack([g["src"][:NP], g["dst"][:NP]]).reshape(2, NT, P).transpose(2, 0, 1))),
        ("w0", c(g["L0_gnn_conv_weights"].transpose(2, 0, 1, 3).reshape(D, R8 * D))),
        ("a0l", row(g["L0_gnn_attn_l"])), ("a0r", row(g["L0_gnn_attn_r"])), ("cols", cols),
        ("wrel", c(g["L1_gnn_W_rel"].transpose(0, 2, 1))), ("brow", c(g["L1_gnn_b_rel"])),
        ("wih", c(pick(w_ih))),
        ("w1", c(g["L1_gnn_W1"].T)), ("w2", c(g["L1_gnn_W2"].T)),
        ("w3", c(g["L1_gnn_W3"].T)), ("b3", row(g["L1_gnn_b3"])),
        ("wp1", c(g["L2_gnn_W_proj1"])), ("bp1", row(g["L2_gnn_b_proj1"])), ("wl1", c(g["L2_gnn_W_l1"])),
        ("bl1", row(g["L2_gnn_b_l1"])), ("wr1", c(g["L2_gnn_W_r1"])),
        ("wp2", c(g["L2_gnn_W_proj2"])), ("bp2", row(g["L2_gnn_b_proj2"])), ("wl2", c(g["L2_gnn_W_l2"])),
        ("bl2", row(g["L2_gnn_b_l2"])), ("wr2", c(g["L2_gnn_W_r2"])),
        ("wt3", c(g["L3_gnn_weight"])), ("a3l", row(g["L3_gnn_attn_l"])), ("a3r", row(g["L3_gnn_attn_r"])),
    ]


def kernel(**inputs):
    import concourse.bacc as bacc
    from concourse.bass_utils import run_bass_kernel_spmd as run

    nc = bacc.Bacc("TRN2", target_bir_lowering=False, num_devices=1)
    arrays, args = {}, []
    for name, a in layout(inputs):
        arrays["in_" + name] = a
        args.append(nc.dram_tensor("in_" + name, a.shape, mybir.dt.from_np(a.dtype), kind="ExternalInput").ap())
    args.append(nc.dram_tensor("out_0", (N, D), F32, kind="ExternalOutput").ap())
    build(nc, *args)
    r = run(nc, [arrays], core_ids=[0])
    return r.results[0]["out_0"]
```
